# Optimizing a Trainium2 kernel written in Bass

```python
import numpy as np
import jax
import jax.numpy as jnp

def _softmax(x, axis=-1):
    return jax.nn.softmax(x, axis=axis)

def _gelu(x):
    return jax.nn.gelu(x, approximate=True)

def _silu(x):
    return jax.nn.silu(x)

def _sigmoid(x):
    return jax.nn.sigmoid(x)

def _layernorm(x, axis=-1, eps=1e-05):
    m = jnp.mean(x, axis=axis, keepdims=True)
    v = jnp.var(x, axis=axis, keepdims=True)
    return (x - m) / jnp.sqrt(v + eps)

def _scatter_add(tgt, idx, src, axis=0):
    return tgt.at[idx].add(src)

def _segment_sum(src, seg, n):
    return jax.ops.segment_sum(src, seg, n)
kernel_name = 'mk_early_fusion_d2_tok_img512_r4_8cd5a3'

def setup_inputs(seed: int=0):
    np.random.seed(seed)
    _w = jnp.asarray

    def _rec_inputs():
        import jax
        import jax.numpy as jnp
        _rk = jax.random.key(seed)
        x = 7.57192e-06 + 1.00007 * jax.random.normal(jax.random.fold_in(_rk, 1), (16, 112, 112, 3), jnp.float32)
        txt = -0.000319884 + 0.450765 * jax.random.normal(jax.random.fold_in(_rk, 2), (16, 77, 128), jnp.float32)
        return (x, txt)
    x, txt = _rec_inputs()

    def _L0_tok_setup():
        import jax, jax.numpy as jnp
        import numpy as np
        B, H, W, C = (64, 224, 224, 3)
        P, D = (16, 128)
        LN_EPS = 0.001

        def _shift4(x):
            pad = lambda a, spec: jnp.pad(a, spec)
            right = pad(x[:, :, :-1, :], ((0, 0), (0, 0), (1, 0), (0, 0)))
            left = pad(x[:, :, 1:, :], ((0, 0), (0, 0), (0, 1), (0, 0)))
            down = pad(x[:, :-1, :, :], ((0, 0), (1, 0), (0, 0), (0, 0)))
            up = pad(x[:, 1:, :, :], ((0, 0), (0, 1), (0, 0), (0, 0)))
            return [right, left, down, up]
        key = jax.random.key(seed)
        k0, k1, k2 = jax.random.split(key, 3)
        x = jax.random.normal(k0, (B, H, W, C), jnp.float32)
        conv_w = jax.random.normal(k1, (P, P, 5 * C, D), jnp.float32) * 0.02
        conv_b = jnp.zeros((D,), jnp.float32)
        gamma = jnp.ones((D,), jnp.float32)
        beta = jnp.zeros((D,), jnp.float32)
        dense_w = jax.random.normal(k2, (D, D), jnp.float32) * 0.02
        dense_b = jnp.zeros((D,), jnp.float32)
        return {'x': x, 'conv_w': conv_w, 'conv_b': conv_b, 'gamma': gamma, 'beta': beta, 'dense_w': dense_w, 'dense_b': dense_b}
    _L0_tok_all = _L0_tok_setup()
    _L0_tok_in = {k: v for k, v in _L0_tok_all.items() if k in ('conv_w', 'conv_b', 'gamma', 'beta', 'dense_w', 'dense_b')}
    del _L0_tok_all

    def _L0_attn_setup():
        import jax, jax.numpy as jnp
        import numpy as np
        B, S, E, H = (2, 1024, 128, 8)
        D = E // H
        key = jax.random.key(seed)
        ks = jax.random.split(key, 6)
        x = jax.random.normal(ks[0], (B, S, E), dtype=jnp.float32)
        scale = E ** (-0.5)
        in_proj_w = jax.random.normal(ks[1], (3 * E, E), dtype=jnp.float32) * scale
        in_proj_b = jnp.zeros((3 * E,), dtype=jnp.float32)
        out_proj_w = jax.random.normal(ks[2], (E, E), dtype=jnp.float32) * scale
        out_proj_b = jnp.zeros((E,), dtype=jnp.float32)
        t = jax.random.normal(ks[3], (H,), dtype=jnp.float32)
        return {'x': x, 'in_proj_w': in_proj_w, 'in_proj_b': in_proj_b, 'out_proj_w': out_proj_w, 'out_proj_b': out_proj_b, 't': t}
    _L0_attn_all = _L0_attn_setup()
    _L0_attn_in = {k: v for k, v in _L0_attn_all.items() if k in ('in_proj_w', 'in_proj_b', 'out_proj_w', 'out_proj_b', 't')}
    del _L0_attn_all

    def _L0_ffn_setup():
        import jax, jax.numpy as jnp
        import numpy as np
        G = 4
        EPG = 4
        E = 16
        KG = 2
        K = 2
        GTP = 0.9
        TP = 0.9
        SCALE = 1.0 / float(np.sqrt(G))

        def _routing_weights(xf, Wr, br, Wgate, bgate):
            N = xf.shape[0]
            gp = jax.nn.softmax(xf @ Wr + br, axis=-1)
            order = jnp.argsort(-gp, axis=-1)
            sp_k = jnp.take_along_axis(gp, order, axis=-1)[:, :KG]
            idx_k = order[:, :KG]
            act = jnp.cumsum(sp_k, axis=-1) <= GTP
            act = act.at[:, 0].set(True)
            mp = sp_k * act
            rn = mp / (jnp.sum(mp, axis=-1, keepdims=True) + 1e-09)
            w_group = jnp.zeros((N, G), xf.dtype).at[jnp.arange(N)[:, None], idx_k].set(rn)
            ep = jax.nn.softmax(jnp.einsum('nd,gde->nge', xf, Wgate) + bgate, axis=-1)
            eorder = jnp.argsort(-ep, axis=-1)
            esp = jnp.take_along_axis(ep, eorder, axis=-1)[:, :, :K]
            eidx = eorder[:, :, :K]
            eact = jnp.cumsum(esp, axis=-1) <= TP
            eact = eact.at[:, :, 0].set(True)
            emp = esp * eact
            ern = emp / (jnp.sum(emp, axis=-1, keepdims=True) + 1e-09)
            w_exp = jnp.zeros((N, G, EPG), xf.dtype).at[jnp.arange(N)[:, None, None], jnp.arange(G)[None, :, None], eidx].set(ern)
            return (w_group[:, :, None] * w_exp * SCALE).reshape(N, E)
        key = jax.random.key(seed)
        ks = jax.random.split(key, 6)
        B, T, D, H = (2, 256, 128, 512)
        x = jax.random.normal(ks[0], (B, T, D), jnp.float32)
        Wr = jax.random.normal(ks[1], (D, G), jnp.float32) * 0.02
        br = jnp.zeros((G,), jnp.float32)
        Wgate = jax.random.normal(ks[2], (G, D, EPG), jnp.float32) * 0.02
        bgate = jnp.zeros((G, EPG), jnp.float32)
        W1 = jax.random.normal(ks[3], (E, D, H), jnp.float32) * 0.02
        W3 = jax.random.normal(ks[4], (E, D, H), jnp.float32) * 0.02
        W2 = jax.random.normal(ks[5], (E, H, D), jnp.float32) * 0.02
        return {'x': x, 'Wr': Wr, 'br': br, 'Wgate': Wgate, 'bgate': bgate, 'W1': W1, 'W3': W3, 'W2': W2}
    _L0_ffn_all = _L0_ffn_setup()
    _L0_ffn_in = {k: v for k, v in _L0_ffn_all.items() if k in ('Wr', 'br', 'Wgate', 'bgate', 'W1', 'W3', 'W2')}
    del _L0_ffn_all

    def _L1_attn_setup():
        import jax, jax.numpy as jnp
        import numpy as np
        B, T, IN, H, OUT = (32, 128, 128, 256, 128)

        def _xavier(key, shape):
            fan_in, fan_out = (shape[0], shape[1])
            a = np.sqrt(6.0 / (fan_in + fan_out))
            return jax.random.uniform(key, shape, jnp.float32, -a, a)

        def _run_layer(x_seq, Wx, Wh, b):
            h_dim = Wh.shape[0]
            gx = jnp.einsum('btd,dg->btg', x_seq, Wx) + b
            gx = jnp.swapaxes(gx, 0, 1)

            def step(carry, gx_t):
                h, c, m = carry
                g = gx_t + h @ Wh
                i = jax.nn.sigmoid(g[:, 0 * h_dim:1 * h_dim])
                f = jax.nn.sigmoid(g[:, 1 * h_dim:2 * h_dim])
                c_tilde = jnp.tanh(g[:, 2 * h_dim:3 * h_dim])
                o = jax.nn.sigmoid(g[:, 3 * h_dim:4 * h_dim])
                m_new = jnp.tanh(g[:, 4 * h_dim:5 * h_dim])
                c_new = f * c + i * c_tilde
                h_new = o * jnp.tanh(c_new) + m_new
                return ((h_new, c_new, m_new), h_new)
            bsz = x_seq.shape[0]
            init = (jnp.zeros((bsz, h_dim), x_seq.dtype), jnp.zeros((bsz, h_dim), x_seq.dtype), jnp.zeros((bsz, h_dim), x_seq.dtype))
            _, hs = jax.lax.scan(step, init, gx)
            return jnp.swapaxes(hs, 0, 1)
        key = jax.random.key(seed)
        ks = jax.random.split(key, 12)
        x = jax.random.normal(ks[0], (B, T, IN), jnp.float32)
        Wx0 = jnp.concatenate([_xavier(ks[1 + g], (IN, H)) for g in range(5)], axis=1)
        Wh0 = jnp.concatenate([_xavier(jax.random.fold_in(ks[6], g), (H, H)) for g in range(5)], axis=1)
        b0 = jnp.zeros((5 * H,), jnp.float32)
        Wx1 = jnp.concatenate([_xavier(jax.random.fold_in(ks[7], g), (H, H)) for g in range(5)], axis=1)
        Wh1 = jnp.concatenate([_xavier(jax.random.fold_in(ks[8], g), (H, H)) for g in range(5)], axis=1)
        b1 = jnp.zeros((5 * H,), jnp.float32)
        Wfc = _xavier(ks[9], (H, OUT))
        bfc = jnp.zeros((OUT,), jnp.float32)
        return {'x': x, 'Wx0': Wx0, 'Wh0': Wh0, 'b0': b0, 'Wx1': Wx1, 'Wh1': Wh1, 'b1': b1, 'Wfc': Wfc, 'bfc': bfc}
    _L1_attn_all = _L1_attn_setup()
    _L1_attn_in = {k: v for k, v in _L1_attn_all.items() if k in ('Wx0', 'Wh0', 'b0', 'Wx1', 'Wh1', 'b1', 'Wfc', 'bfc')}
    del _L1_attn_all

    def _L1_ffn_setup():
        import jax, jax.numpy as jnp
        import numpy as np
        B, N, D, E = (8, 2048, 128, 8)
        H = 2 * D
        key = jax.random.key(seed)
        ks = jax.random.split(key, 7)
        s = 0.02
        return {'x': jax.random.normal(ks[0], (B, N, D), dtype=jnp.float32), 'W1': jax.random.normal(ks[1], (E, D, H), dtype=jnp.float32) * s, 'b1': jnp.zeros((E, H), dtype=jnp.float32), 'W2': jax.random.normal(ks[2], (E, H, D), dtype=jnp.float32) * s, 'b2': jnp.zeros((E, D), dtype=jnp.float32), 'Wg': jax.random.normal(ks[3], (D, E), dtype=jnp.float32) * s, 'bg': jnp.zeros((E,), dtype=jnp.float32)}
    _L1_ffn_all = _L1_ffn_setup()
    _L1_ffn_in = {k: v for k, v in _L1_ffn_all.items() if k in ('W1', 'b1', 'W2', 'b2', 'Wg', 'bg')}
    del _L1_ffn_all
    return {'x': x, 'txt': txt, 'L0_tok_conv_w': _L0_tok_in['conv_w'], 'L0_tok_conv_b': _L0_tok_in['conv_b'], 'L0_tok_gamma': _L0_tok_in['gamma'], 'L0_tok_beta': _L0_tok_in['beta'], 'L0_tok_dense_w': _L0_tok_in['dense_w'], 'L0_tok_dense_b': _L0_tok_in['dense_b'], 'L0_attn_in_proj_w': _L0_attn_in['in_proj_w'], 'L0_attn_in_proj_b': _L0_attn_in['in_proj_b'], 'L0_attn_out_proj_w': _L0_attn_in['out_proj_w'], 'L0_attn_out_proj_b': _L0_attn_in['out_proj_b'], 'L0_attn_t': _L0_attn_in['t'], 'L0_ffn_Wr': _L0_ffn_in['Wr'], 'L0_ffn_br': _L0_ffn_in['br'], 'L0_ffn_Wgate': _L0_ffn_in['Wgate'], 'L0_ffn_bgate': _L0_ffn_in['bgate'], 'L0_ffn_W1': _L0_ffn_in['W1'], 'L0_ffn_W3': _L0_ffn_in['W3'], 'L0_ffn_W2': _L0_ffn_in['W2'], 'L1_attn_Wx0': _L1_attn_in['Wx0'], 'L1_attn_Wh0': _L1_attn_in['Wh0'], 'L1_attn_b0': _L1_attn_in['b0'], 'L1_attn_Wx1': _L1_attn_in['Wx1'], 'L1_attn_Wh1': _L1_attn_in['Wh1'], 'L1_attn_b1': _L1_attn_in['b1'], 'L1_attn_Wfc': _L1_attn_in['Wfc'], 'L1_attn_bfc': _L1_attn_in['bfc'], 'L1_ffn_W1': _L1_ffn_in['W1'], 'L1_ffn_b1': _L1_ffn_in['b1'], 'L1_ffn_W2': _L1_ffn_in['W2'], 'L1_ffn_b2': _L1_ffn_in['b2'], 'L1_ffn_Wg': _L1_ffn_in['Wg'], 'L1_ffn_bg': _L1_ffn_in['bg']}

def reference(x, txt, L0_tok_conv_w, L0_tok_conv_b, L0_tok_gamma, L0_tok_beta, L0_tok_dense_w, L0_tok_dense_b, L0_attn_in_proj_w, L0_attn_in_proj_b, L0_attn_out_proj_w, L0_attn_out_proj_b, L0_attn_t, L0_ffn_Wr, L0_ffn_br, L0_ffn_Wgate, L0_ffn_bgate, L0_ffn_W1, L0_ffn_W3, L0_ffn_W2, L1_attn_Wx0, L1_attn_Wh0, L1_attn_b0, L1_attn_Wx1, L1_attn_Wh1, L1_attn_b1, L1_attn_Wfc, L1_attn_bfc, L1_ffn_W1, L1_ffn_b1, L1_ffn_W2, L1_ffn_b2, L1_ffn_Wg, L1_ffn_bg):
    import jax
    import jax.numpy as jnp

    def _L0_tok_ref(x, conv_w, conv_b, gamma, beta, dense_w, dense_b):
        import jax, jax.numpy as jnp
        import numpy as np
        B, H, W, C = (64, 224, 224, 3)
        P, D = (16, 128)
        LN_EPS = 0.001

        def _shift4(x):
            pad = lambda a, spec: jnp.pad(a, spec)
            right = pad(x[:, :, :-1, :], ((0, 0), (0, 0), (1, 0), (0, 0)))
            left = pad(x[:, :, 1:, :], ((0, 0), (0, 0), (0, 1), (0, 0)))
            down = pad(x[:, :-1, :, :], ((0, 0), (1, 0), (0, 0), (0, 0)))
            up = pad(x[:, 1:, :, :], ((0, 0), (0, 1), (0, 0), (0, 0)))
            return [right, left, down, up]
        xs = jnp.concatenate([x, *_shift4(x)], axis=-1)
        y = jax.lax.conv_general_dilated(xs, conv_w, window_strides=(P, P), padding='VALID', dimension_numbers=('NHWC', 'HWIO', 'NHWC')) + conv_b
        y = y.reshape(y.shape[0], -1, D)
        mu = jnp.mean(y, axis=-1, keepdims=True)
        var = jnp.mean(jnp.square(y - mu), axis=-1, keepdims=True)
        y = (y - mu) * jax.lax.rsqrt(var + LN_EPS) * gamma + beta
        return y @ dense_w + dense_b

    def _L0_attn_ref(x, in_proj_w, in_proj_b, out_proj_w, out_proj_b, t):
        import jax, jax.numpy as jnp
        import numpy as np
        B, S, E, H = (2, 1024, 128, 8)
        D = E // H
        b, s, e = x.shape
        h, d = (H, D)
        qkv = x @ in_proj_w.T + in_proj_b
        q, k, v = jnp.split(qkv, 3, axis=-1)
        q = q.reshape(b, s, h, d).transpose(0, 2, 1, 3)
        k = k.reshape(b, s, h, d).transpose(0, 2, 1, 3)
        v = v.reshape(b, s, h, d).transpose(0, 2, 1, 3)
        scores = jnp.einsum('bhqd,bhkd->bhqk', q, k) / jnp.sqrt(jnp.float32(d))
        idx = jnp.arange(s)
        dist2 = (idx[None, :] - idx[:, None]).astype(jnp.float32) ** 2
        sigma = t ** 2
        bias = -dist2[None, :, :] / (2.0 * (sigma ** 2)[:, None, None])
        attn = jax.nn.softmax(scores + bias[None], axis=-1)
        out = jnp.einsum('bhqk,bhkd->bhqd', attn, v)
        out = out.transpose(0, 2, 1, 3).reshape(b, s, e)
        return out @ out_proj_w.T + out_proj_b

    def _L0_ffn_ref(x, Wr, br, Wgate, bgate, W1, W3, W2):
        import jax, jax.numpy as jnp
        import numpy as np
        G = 4
        EPG = 4
        E = 16
        KG = 2
        K = 2
        GTP = 0.9
        TP = 0.9
        SCALE = 1.0 / float(np.sqrt(G))

        def _routing_weights(xf, Wr, br, Wgate, bgate):
            N = xf.shape[0]
            gp = jax.nn.softmax(xf @ Wr + br, axis=-1)
            order = jnp.argsort(-gp, axis=-1)
            sp_k = jnp.take_along_axis(gp, order, axis=-1)[:, :KG]
            idx_k = order[:, :KG]
            act = jnp.cumsum(sp_k, axis=-1) <= GTP
            act = act.at[:, 0].set(True)
            mp = sp_k * act
            rn = mp / (jnp.sum(mp, axis=-1, keepdims=True) + 1e-09)
            w_group = jnp.zeros((N, G), xf.dtype).at[jnp.arange(N)[:, None], idx_k].set(rn)
            ep = jax.nn.softmax(jnp.einsum('nd,gde->nge', xf, Wgate) + bgate, axis=-1)
            eorder = jnp.argsort(-ep, axis=-1)
            esp = jnp.take_along_axis(ep, eorder, axis=-1)[:, :, :K]
            eidx = eorder[:, :, :K]
            eact = jnp.cumsum(esp, axis=-1) <= TP
            eact = eact.at[:, :, 0].set(True)
            emp = esp * eact
            ern = emp / (jnp.sum(emp, axis=-1, keepdims=True) + 1e-09)
            w_exp = jnp.zeros((N, G, EPG), xf.dtype).at[jnp.arange(N)[:, None, None], jnp.arange(G)[None, :, None], eidx].set(ern)
            return (w_group[:, :, None] * w_exp * SCALE).reshape(N, E)
        B, T, D = x.shape
        xf = x.reshape(-1, D)
        tw = _routing_weights(xf, Wr, br, Wgate, bgate)
        out = jnp.zeros_like(xf)
        for e in range(E):
            h = jax.nn.silu(xf @ W1[e]) * (xf @ W3[e])
            out = out + tw[:, e:e + 1] * (h @ W2[e])
        return out.reshape(B, T, D)

    def _L1_attn_ref(x, Wx0, Wh0, b0, Wx1, Wh1, b1, Wfc, bfc):
        import jax, jax.numpy as jnp
        import numpy as np
        B, T, IN, H, OUT = (32, 128, 128, 256, 128)

        def _xavier(key, shape):
            fan_in, fan_out = (shape[0], shape[1])
            a = np.sqrt(6.0 / (fan_in + fan_out))
            return jax.random.uniform(key, shape, jnp.float32, -a, a)

        def _run_layer(x_seq, Wx, Wh, b):
            h_dim = Wh.shape[0]
            gx = jnp.einsum('btd,dg->btg', x_seq, Wx) + b
            gx = jnp.swapaxes(gx, 0, 1)

            def step(carry, gx_t):
                h, c, m = carry
                g = gx_t + h @ Wh
                i = jax.nn.sigmoid(g[:, 0 * h_dim:1 * h_dim])
                f = jax.nn.sigmoid(g[:, 1 * h_dim:2 * h_dim])
                c_tilde = jnp.tanh(g[:, 2 * h_dim:3 * h_dim])
                o = jax.nn.sigmoid(g[:, 3 * h_dim:4 * h_dim])
                m_new = jnp.tanh(g[:, 4 * h_dim:5 * h_dim])
                c_new = f * c + i * c_tilde
                h_new = o * jnp.tanh(c_new) + m_new
                return ((h_new, c_new, m_new), h_new)
            bsz = x_seq.shape[0]
            init = (jnp.zeros((bsz, h_dim), x_seq.dtype), jnp.zeros((bsz, h_dim), x_seq.dtype), jnp.zeros((bsz, h_dim), x_seq.dtype))
            _, hs = jax.lax.scan(step, init, gx)
            return jnp.swapaxes(hs, 0, 1)
        h1 = _run_layer(x, Wx0, Wh0, b0)
        h2 = _run_layer(h1, Wx1, Wh1, b1)
        return jnp.einsum('bth,ho->bto', h2, Wfc) + bfc

    def _L1_ffn_ref(x, W1, b1, W2, b2, Wg, bg):
        import jax, jax.numpy as jnp
        import numpy as np
        B, N, D, E = (8, 2048, 128, 8)
        H = 2 * D
        Bs, Ns, Ds = x.shape
        xf = x.reshape(Bs * Ns, Ds)
        logits = xf @ Wg + bg
        idx = jnp.argmax(logits, axis=-1)
        out = jnp.zeros_like(xf)
        num_experts = W1.shape[0]
        for e in range(num_experts):
            h = jax.nn.relu(xf @ W1[e] + b1[e])
            y = h @ W2[e] + b2[e]
            out = jnp.where((idx == e)[:, None], y, out)
        return out.reshape(Bs, Ns, Ds)
    h = _L0_tok_ref(x, L0_tok_conv_w, L0_tok_conv_b, L0_tok_gamma, L0_tok_beta, L0_tok_dense_w, L0_tok_dense_b)
    h = jnp.concatenate([h, txt], axis=1)
    h = h + _L0_attn_ref(_layernorm(h, axis=-1), L0_attn_in_proj_w, L0_attn_in_proj_b, L0_attn_out_proj_w, L0_attn_out_proj_b, L0_attn_t)
    h = h + _L0_ffn_ref(_layernorm(h, axis=-1), L0_ffn_Wr, L0_ffn_br, L0_ffn_Wgate, L0_ffn_bgate, L0_ffn_W1, L0_ffn_W3, L0_ffn_W2)
    h = h + _L1_attn_ref(_layernorm(h, axis=-1), L1_attn_Wx0, L1_attn_Wh0, L1_attn_b0, L1_attn_Wx1, L1_attn_Wh1, L1_attn_b1, L1_attn_Wfc, L1_attn_bfc)
    h = h + _L1_ffn_ref(_layernorm(h, axis=-1), L1_ffn_W1, L1_ffn_b1, L1_ffn_W2, L1_ffn_b2, L1_ffn_Wg, L1_ffn_bg)
    return h

_drawn_inputs = setup_inputs


def setup_inputs(seed=0):
    import zlib

    import numpy as np

    out = dict(_drawn_inputs(seed))
    spreads = {'L0_tok_conv_b': (0.0, 0.1),
     'L0_tok_gamma': (1.0, 0.2),
     'L0_tok_beta': (0.0, 0.1),
     'L0_tok_dense_b': (0.0, 0.1),
     'L0_attn_in_proj_b': (0.0, 0.1),
     'L0_attn_out_proj_b': (0.0, 0.1),
     'L0_ffn_br': (0.0, 0.8),
     'L0_ffn_bgate': (0.0, 0.8),
     'L1_attn_b0': (0.0, 0.1),
     'L1_attn_b1': (0.0, 0.1),
     'L1_attn_bfc': (0.0, 0.1),
     'L1_ffn_b1': (0.0, 0.401),
     'L1_ffn_b2': (0.0, 0.1),
     'L1_ffn_bg': (0.0, 0.1)}
    factors = {'L0_ffn_Wr': 8.0,
     'L0_ffn_Wgate': 8.0,
     'L0_ffn_W1': 7.09,
     'L0_ffn_W3': 5.628,
     'L0_ffn_W2': 5.886}
    for name, (base, spread) in spreads.items():
        noise = np.random.default_rng([zlib.crc32(name.encode()), seed]).standard_normal(out[name].shape)
        drawn = base * np.exp(spread * noise) if base else spread * noise
        out[name] = jnp.asarray(drawn.astype(out[name].dtype))
    for name, factor in factors.items():
        out[name] = (out[name] * factor).astype(out[name].dtype)
    return out
```

```python
from contextlib import ExitStack

import concourse.bass as bass
from concourse import mybir

F32 = mybir.dt.float32
F32R = mybir.dt.float32r
BF16 = mybir.dt.bfloat16
F16 = mybir.dt.float16
ALU = mybir.AluOpType
ACT = mybir.ActivationFunctionType
AX = mybir.AxisListType.X

P = 128
BATCH, SIDE, COLORS = 16, 112, 3
PATCH = 16
GRID = SIDE // PATCH
WIDE = PATCH + 2
WORDS = 77
PATCHES = GRID * GRID
SEQ = PATCHES + WORDS
TOKENS = SEQ * BATCH
NBLK = 4
BLK = TOKENS // NBLK
TILES = TOKENS // SEQ
D = 128
ROWS2 = 2 * WIDE * COLORS
RCH = WIDE // 2
EMB = PATCHES * BATCH
EBLK = EMB // 2
SHIFTS = 5
HEADS, HD = 8, 16
HALF = HEADS // 2
PAD = P // HALF
E0, GROUPS, H0 = 16, 4, 512
C0 = H0 // P
W0 = 3 * H0
E1, H1 = 8, 256
C1 = H1 // P
F0 = 2 * H1
RH = 256
KH = RH // P
GCH = 5 * RH // P
GP = GCH * P
GW = GCH * BATCH
SW = KH * BATCH
WX0, WH0, WX1, WH1 = 0, 1, 3, 5
H_SCALE = 1024.0
LAG = 2
CONV_B, GAMMA, BETA, DENSE_B, OUT_B, FC_B, QKV_B = 0, 1, 2, 3, 4, 5, 6
FB1 = QKV_B + 6
NCOLS = FB1 + E1 * C1
C_ID, C_DIST, C_SEL = 0, P, P + SEQ
C_PRI = C_SEL + GW
NCONST = C_PRI + E1


def build(nc, taps_in, patches_in, txt_in, cols_in, const_in, dense_in, qkvw_in, outw_in, heads_in, w0_in,
          route_in, routeb_in, rec_in, recb_in, fcw_in, f_in, fb2_in, fg_in, fgb_in, out):
    share_dram = nc.dram_tensor("share_scratch", (E0, TOKENS), F32, kind="Internal").ap()
    mask_dram = nc.dram_tensor("mask_scratch", (E1, TOKENS), F32, kind="Internal").ap()

    with ExitStack() as ctx:
        def sb(name, shape, dt=F32):
            return ctx.enter_context(nc.sbuf_tensor(name, shape, dt))

        sems = {}

        def sg(name):
            if name not in sems:
                sems[name] = ctx.enter_context(nc.semaphore(name))
            return sems[name]

        def reach(eng, name, value):
            if not isinstance(value, int) or value > 0:
                eng.wait_ge(sg(name), value)

        def settle(eng):
            eng.wait_ge(sg("warm"), 1)

        low_banks = [ctx.enter_context(nc.psum_tensor(f"bank{i}", [P, 512], F32)) for i in range(4)]
        quad = ctx.enter_context(nc.psum_tensor("quad", [P, 4, 512], F32))
        bank = [b[:, :] for b in low_banks] + [quad[:, i, :] for i in range(4)]

        stream = sb("stream", [P, TOKENS])
        xn = sb("xn", [P, TOKENS])
        mean_mat = sb("mean_mat", [P, P])
        cols = sb("cols", [P, NCOLS])
        const = sb("const", [P, NCONST])
        eps = sb("eps", [P, 2])
        ones_row = sb("ones_row", [1, SEQ])
        warm = sb("warm", [P, 1])
        one = sb("one", [P, 1])
        ident = const[:, C_ID:C_ID + P]

        wH = sb("wH", [P, 2, W0], F32R)
        wL = sb("wL", [P, 2, W0], F32R)
        xnH = sb("xnH", [P, TOKENS], F32R)
        xnL = sb("xnL", [P, TOKENS], F32R)
        xeH = sb("xeH", [P, 2, BLK], F32R)
        xeL = sb("xeL", [P, 2, BLK], F32R)
        hidH = sb("hidH", [P, 4, BLK], F32R)
        hidL = sb("hidL", [P, 4, BLK], F32R)

        AREA = 30000
        area = sb("area", [P, AREA])

        def region(start, size=AREA):
            at = [start]

            def view(words, parts=P):
                a = area[0:parts, at[0]:at[0] + words]
                at[0] += words
                assert at[0] <= min(AREA, size), (at[0], size)
                return a
            return view, at

        view, at = region(0)
        sq = view(NBLK * BLK).rearrange("p (u n) -> p u n", u=NBLK)
        STAGE = at[0]
        taps = view(SHIFTS * RCH * D, ROWS2).rearrange("p (s k d) -> p s k d", s=SHIFTS, k=RCH)
        patches = view(RCH * EMB, ROWS2).rearrange("p (k n) -> p k n", k=RCH)
        conv = view(EMB)
        emb = view(EMB)
        dense_w = view(D)
        headsT = view(2 * TOKENS).rearrange("p (a t b) -> p a t b", a=2, b=BATCH)
        qkv_w = view(6 * P).rearrange("p (w n) -> p w n", w=6)
        out_w = view(2 * P).rearrange("p (a o) -> p a o", a=2)
        slope = view(4 * HEADS, SEQ).rearrange("p (a h) -> p a h", a=4)
        decay = view(HEADS * SEQ, SEQ).rearrange("p (h k) -> p h k", h=HEADS)
        xb = view(2 * SEQ).rearrange("p (u n) -> p u n", u=2)
        qk = view(2 * 4 * SEQ).rearrange("p (u w n) -> p u w n", u=2, w=4)
        vb = view(2 * 2 * P, SEQ).rearrange("p (u n) -> p u n", u=2)
        att = view(2 * HEADS * SEQ, SEQ).rearrange("p (u h k) -> p u h k", u=2, h=HEADS)
        attT = view(2 * HALF * SEQ, SEQ).rearrange("p (a j k) -> p a j k", a=2, j=HALF)
        smax = view(2 * HEADS, SEQ).rearrange("p (u h) -> p u h", u=2)
        ssum = view(2 * HEADS, SEQ).rearrange("p (u h) -> p u h", u=2)
        srec = view(2 * HEADS, SEQ).rearrange("p (u h) -> p u h", u=2)

        view, at = region(STAGE)
        w_raw = view(2 * W0).rearrange("p (u n) -> p u n", u=2)
        assert at[0] <= STAGE + SHIFTS * RCH * D
        share = view(2 * TOKENS).rearrange("p (u n) -> p u n", u=2)
        xe = view(2 * BLK).rearrange("p (u n) -> p u n", u=2)
        silu = view(2 * BLK).rearrange("p (u n) -> p u n", u=2)
        hid = view(2 * BLK).rearrange("p (u n) -> p u n", u=2)
        n_soft = TILES * (1 + GROUPS)
        route_w = view(20)
        route_b = view(20, SEQ)
        route_at = at[0]
        prob = view(n_soft * 4, SEQ).rearrange("p (n k) -> p n k", k=4)
        rank = view(n_soft * 4, SEQ).rearrange("p (n k) -> p n k", k=4)
        pick = view(n_soft * 4, SEQ).rearrange("p (n k) -> p n k", k=4)
        beat = view(n_soft * 6, SEQ).rearrange("p (a n) -> p a n", a=6)
        top = view(n_soft * 3, SEQ).rearrange("p (a n) -> p a n", a=3)
        weight = view(TILES * E0, SEQ).rearrange("p (t g e) -> p t g e", t=TILES, g=GROUPS)
        shareT = view(TOKENS, E0)
        REC_AT = at[0]
        rec_w = view(7 * 3 * GP // 2).bitcast(BF16).rearrange("p (w s n) -> p w s n", w=7, s=3)
        rec_raw = area[:, route_at:route_at + GP]
        assert route_at + GP <= REC_AT

        view, at = region(STAGE, REC_AT)
        xpair = view(SEQ * 2 * BATCH // 2).bitcast(F16).rearrange("p (t g b) -> p t g b", t=SEQ, g=2)
        hist = view(KH * TOKENS).rearrange("p (t n) -> p t n", t=SEQ)
        xcur = view(2 * 2 * BATCH // 2).bitcast(F16).rearrange("p (u g b) -> p u g b", u=2, g=2)
        hpair = view(4 * KH * 2 * BATCH // 2).bitcast(F16).rearrange(
            "p (l u k g b) -> p l u k g b", l=2, u=2, k=KH, g=2)
        pre = view(2 * GW).rearrange("p (l n) -> p l n", l=2)
        gates = view(2 * 7 * SW).rearrange("p (l n) -> p l n", l=2)
        prod = view(2 * 2 * SW).rearrange("p (l n) -> p l n", l=2)
        tanh_c = view(2 * SW).rearrange("p (l n) -> p l n", l=2)
        out_h = view(2 * SW).rearrange("p (l n) -> p l n", l=2)
        hfull = view(2 * 2 * SW).rearrange("p (l u n) -> p l u n", l=2, u=2)
        bias_raw = view(2 * P).rearrange("p (l n) -> p l n", l=2)
        bias_cast = view(2 * 3 * P // 2).bitcast(BF16).rearrange("p (l s n) -> p l s n", l=2, s=3)
        bias_part = view(2 * P // 2).bitcast(BF16).rearrange("p (l n) -> p l n", l=2)
        bias_sel = view(GW // 2).bitcast(BF16)
        fc_w = view(KH * D).rearrange("p (k n) -> p k n", k=KH)
        f_raw = view(2 * F0).rearrange("p (u n) -> p u n", u=2)
        fb2 = view(D, E1)
        fg_w = view(E1)
        fg_b = view(E1, SEQ)
        view, at = region(REC_AT)
        fc_sb = view(2 * BLK).rearrange("p (u n) -> p u n", u=2)
        logit = view(TILES * E1, SEQ).rearrange("p (t e) -> p t e", t=TILES)
        chosen = view(TILES * E1, SEQ).rearrange("p (t e) -> p t e", t=TILES)
        best = view(2 * TILES, SEQ).rearrange("p (a t) -> p a t", a=2)
        mask_T = view(TOKENS, E1)
        relu = view(2 * BLK).rearrange("p (u n) -> p u n", u=2)
        fhid = view(2 * BLK).rearrange("p (u n) -> p u n", u=2)
        f_bias = view(2 * C1).rearrange("p (u n) -> p u n", u=2)
        mask_b = view(2 * TOKENS).rearrange("p (u n) -> p u n", u=2)

        def col(i):
            return cols[:, i:i + 1]

        def blk(t, j):
            return t[:, j * BLK:(j + 1) * BLK]

        def split3(eng, acc, aH, aL, bH, bL, start, stop):
            eng.matmul(acc, aH, bH, start=start, stop=False, skip_group_check=True)
            eng.matmul(acc, aH, bL, start=False, stop=False, skip_group_check=True)
            return eng.matmul(acc, aL, bH, start=False, stop=stop, skip_group_check=True)

        NORM = {"tok": 0, "ln1": 2, "ln2": 2 + NBLK, "ln3": 2 + 2 * NBLK, "ln4": 2 + 3 * NBLK}

        def normed(eng, tag, blocks=NBLK):
            eng.wait_ge(sg("normed"), NORM[tag] + blocks)

        def norm_pe(pe, tag, src, banks, wait):
            n = len(src)
            for j in range(n):
                wait(pe, j)
                pe.matmul(banks[j][:, 0:src[j].shape[1]], mean_mat[:, :], src[j], start=True, stop=True
                          ).then_inc(sg("mean"), 1)
            for j in range(n):
                pe.wait_ge(sg("squared"), NORM[tag] + j + 1)
                pe.matmul(banks[n + j][:, 0:src[j].shape[1]], mean_mat[:, :], sq[:, j, 0:src[j].shape[1]],
                          start=True, stop=True).then_inc(sg("variance"), 1)

        def norm_act(act, tag, dst, banks, e):
            n = len(dst)
            for j in range(n):
                act.wait_ge(sg("centred"), NORM[tag] + j + 1)
                act.activation(sq[:, j, 0:dst[j].shape[1]], dst[j], ACT.Square).then_inc(sg("squared"), 1)
            for j in range(n):
                act.wait_ge(sg("variance"), NORM[tag] + j + 1)
                act.activation(sq[:, j, 0:dst[j].shape[1]], banks[n + j][:, 0:dst[j].shape[1]], ACT.Sqrt,
                               bias=eps[:, e:e + 1]).then_inc(sg("deviation"), 1)

        def norm_dve(dve, tag, src, dst, banks):
            n = len(dst)
            for j in range(n):
                dve.wait_ge(sg("mean"), NORM[tag] + j + 1)
                dve.tensor_tensor(dst[j], src[j], banks[j][:, 0:src[j].shape[1]], ALU.subtract
                                  ).then_inc(sg("centred"), 1)
            for j in range(n):
                r = sq[:, j, 0:dst[j].shape[1]]
                dve.wait_ge(sg("deviation"), NORM[tag] + j + 1)
                dve.reciprocal(r, r).then_inc(sg("inverted"), 1)
                dve.wait_ge(sg("inverted"), NORM[tag] + j + 1)
                dve.tensor_tensor(dst[j], dst[j], r, ALU.mult).then_inc(sg("normed"), 1)

        xn_blocks = [blk(xn, j) for j in range(NBLK)]
        st_blocks = [blk(stream, j) for j in range(NBLK)]

        conv_blocks = [conv[:, j * EBLK:(j + 1) * EBLK] for j in range(2)]
        emb_blocks = [emb[:, j * EBLK:(j + 1) * EBLK] for j in range(2)]

        def tok_sp(sp):
            sp.dma_start(taps, taps_in).then_inc(sg("taps_in"), 16)
            for j in range(2):
                sp.dma_start(patches[:, :, j * EBLK:(j + 1) * EBLK], patches_in[:, :, j * EBLK:(j + 1) * EBLK]
                             ).then_inc(sg(f"patches_in{j}"), 16)
            sp.dma_start(cols[:, :], cols_in).then_inc(sg("cols_in"), 16)
            sp.dma_start(dense_w, dense_in).then_inc(sg("dense_in"), 16)
            sp.dma_start(stream[:, EMB:TOKENS], txt_in).then_inc(sg("words_in"), 16)
            sp.dma_start(const[:, :], const_in).then_inc(sg("const_in"), 16)
            sp.dma_start(qkv_w, qkvw_in).then_inc(sg("att_w_in"), 16)
            sp.dma_start(out_w, outw_in).then_inc(sg("att_w_in"), 16)
            sp.dma_start(slope[:, 0, :], heads_in.broadcast_to([SEQ, HEADS])).then_inc(sg("slope_in"), 16)

        def tok_pool(pool):
            pool.memset(mean_mat[:, :], 1.0 / D).then_inc(sg("mean_mat"), 1)
            pool.memset(eps[:, 0:1], 1e-3).then_inc(sg("eps"), 1)
            pool.memset(eps[:, 1:2], 1e-5).then_inc(sg("eps"), 1)
            pool.memset(ones_row[:, :], 1.0).then_inc(sg("ones"), 1)
            pool.memset(one[:, :], 1.0).then_inc(sg("ones"), 1)
            pool.memset(warm[:, :], 0.0).then_inc(sg("warm"), 1)

        def tok_pe(pe):
            pe.wait_ge(sg("taps_sum"), SHIFTS - 1)
            for j in range(2):
                pe.wait_ge(sg(f"patches_in{j}"), 16)
                for k in range(RCH):
                    mm = pe.matmul(bank[j][:, 0:EBLK], taps[:, 0, k, :], patches[:, k, j * EBLK:(j + 1) * EBLK],
                                   start=(k == 0), stop=(k == RCH - 1))
                mm.then_inc(sg("conv"), 1)
            pe.wait_ge(sg("mean_mat"), 1)
            norm_pe(pe, "tok", conv_blocks, bank[2:6], lambda e, j: e.wait_ge(sg("conv_sb"), j + 1))
            pe.wait_ge(sg("dense_in"), 16)
            for j in range(2):
                pe.wait_ge(sg("emb"), j + 1)
                pe.matmul(bank[6 + j][:, 0:EBLK], dense_w, emb_blocks[j], start=True, stop=True
                          ).then_inc(sg("dense"), 1)

        def tok_act(act):
            act.wait_ge(sg("eps"), 2)
            norm_act(act, "tok", emb_blocks, bank[2:6], 0)

        def tok_dve(dve):
            dve.wait_ge(sg("taps_in"), 16)
            for s in range(1, SHIFTS):
                reach(dve, "taps_sum", s - 1)
                dve.tensor_tensor(taps[:, 0], taps[:, 0], taps[:, s], ALU.add).then_inc(sg("taps_sum"), 1)
            dve.wait_ge(sg("cols_in"), 16)
            for j in range(2):
                dve.wait_ge(sg("conv"), j + 1)
                dve.tensor_scalar(conv_blocks[j], bank[j][:, 0:EBLK], col(CONV_B), None, ALU.add
                                  ).then_inc(sg("conv_sb"), 1)
            dve.wait_ge(sg("conv_sb"), 2)
            norm_dve(dve, "tok", conv_blocks, emb_blocks, bank[2:6])
            for j in range(2):
                normed(dve, "tok", j + 1)
                dve.tensor_scalar(emb_blocks[j], emb_blocks[j], col(GAMMA), col(BETA), ALU.mult, ALU.add
                                  ).then_inc(sg("emb"), 1)
            for j in range(2):
                dve.wait_ge(sg("dense"), j + 1)
                dve.tensor_scalar(stream[:, j * EBLK:(j + 1) * EBLK], bank[6 + j][:, 0:EBLK], col(DENSE_B), None,
                                  ALU.add).then_inc(sg("embedded"), 1)

        xn_images = xn[:, :].rearrange("p (t b) -> p t b", b=BATCH)

        def here(m, first, last):
            return not isinstance(m, int) or first <= m <= last

        def at_image(t, b):
            return t[:, :, b] if isinstance(b, int) else t[:, :, bass.ds(b, 1)].rearrange("p t b -> p (t b)")

        def each_step(eng, body):
            for m in range(4):
                body(m, m % 2)
            with eng.Fori(2, BATCH // 2) as i:
                for u in range(2):
                    body(i * 2 + u, u)
            body(BATCH, 0)
            body(BATCH + 1, 1)

        def att_pool(pool):
            normed(pool, "ln1")

            def step(m, u):
                if here(m, 0, BATCH - 1):
                    if here(m, 2, BATCH):
                        pool.wait_ge(sg("values"), m - 1)
                    settle(pool)
                    pool.tensor_copy(xb[:, u, :], at_image(xn_images, m)).then_inc(sg("xb"), 1)
                if here(m - 1 if isinstance(m, int) else m, 0, BATCH - 1):
                    v = 1 - u
                    pool.wait_ge(sg("smax"), m)
                    pool.tensor_tensor(att[:, v], att[:, v],
                                       smax[:, v, :].rearrange("p (h z) -> p h z", z=1).broadcast_to(
                                           [SEQ, HEADS, SEQ]), ALU.subtract).then_inc(sg("shifted"), 1)
                    pool.wait_ge(sg("srec"), m)
                    pool.tensor_tensor(att[:, v, 0:HALF], att[:, v, 0:HALF],
                                       srec[:, v, 0:HALF].rearrange("p (h z) -> p h z", z=1).broadcast_to(
                                           [SEQ, HALF, SEQ]), ALU.mult).then_inc(sg("soft0"), 1)
            each_step(pool, step)

        def att_pe(pe):
            norm_pe(pe, "ln1", st_blocks, bank, lambda e, j: (e.wait_ge(sg("embedded"), 2),
                                                             e.wait_ge(sg("words_in"), 16)))
            pe.wait_ge(sg("att_w_in"), 32)
            pe.wait_ge(sg("const_in"), 16)
            normed(pe, "ln1")

            def step(m, u):
                if here(m, 0, BATCH - 1):
                    pe.wait_ge(sg("xb"), m + 1)
                    if here(m, 1, BATCH):
                        pe.wait_ge(sg("qk"), m)
                    for w in range(4):
                        mm = pe.matmul(bank[0][:, w * SEQ:(w + 1) * SEQ], qkv_w[:, w, :], xb[:, u, :],
                                       start=True, stop=True)
                    mm.then_inc(sg("qk_ps"), 1)
                if here(m, 2, BATCH + 1):
                    pe.wait_ge(sg("soft0"), m - 1)
                    pe.wait_ge(sg("soft1"), m - 1)
                    for a in range(2):
                        if here(m, 3, BATCH + 1):
                            reach(pe, f"attT{a}", m - 2)
                        for j in range(HALF):
                            mm = pe.transpose(bank[2 + a][0:SEQ, j * SEQ:(j + 1) * SEQ],
                                              att[:, u, 2 * j + a, :], ident[0:SEQ, 0:SEQ])
                        mm.then_inc(sg(f"attT_ps{a}"), 1)
                    if isinstance(m, int) and m > BATCH:
                        pe.wait_ge(sg("heads"), m - 2)
                    elif isinstance(m, int) and m == BATCH:
                        pe.wait_ge(sg("vb"), BATCH)
                    else:
                        pe.wait_ge(sg("vb"), m)
                    for a in range(2):
                        pe.wait_ge(sg(f"attT{a}"), m - 1)
                        for j in range(HALF):
                            h = a * HALF + j
                            mm = pe.matmul(bank[1][PAD * j:PAD * (j + 1), a * SEQ:(a + 1) * SEQ],
                                           vb[:, u, PAD * h:PAD * (h + 1)], attT[:, a, j, :], start=True, stop=True)
                    mm.then_inc(sg("heads_ps"), 1)
                if here(m, 0, BATCH - 1):
                    if here(m, 2, BATCH):
                        pe.wait_ge(sg("heads"), m - 1)
                    elif m == 1:
                        pe.wait_ge(sg("vb"), 1)
                    pe.matmul(bank[1][0:SEQ, 0:2 * P], xb[:, u, :], qkv_w[:, 4:6, :], start=True, stop=True
                              ).then_inc(sg("values"), 1)
                    pe.wait_ge(sg("qk"), m + 1)
                    if here(m, 1, BATCH):
                        pe.wait_ge(sg("scaled"), m)
                    for h in range(HEADS):
                        a, j = divmod(h, HALF)
                        rows = slice(PAD * j, PAD * (j + 1))
                        mm = pe.matmul(quad[0:SEQ, j, a * SEQ:(a + 1) * SEQ], qk[rows, u, a, :], qk[rows, u, 2 + a, :],
                                       start=True, stop=True)
                    mm.then_inc(sg("scores"), 1)
            each_step(pe, step)
            for j in range(NBLK):
                pe.wait_ge(sg("heads"), BATCH)
                for a in range(2):
                    mm = pe.matmul(bank[2 + j][:, 0:BLK], out_w[:, a, :],
                                   blk(headsT[:, a].rearrange("p t b -> p (t b)"), j),
                                   start=(a == 0), stop=(a == 1))
                mm.then_inc(sg("projected"), 1)

        def att_act(act):
            norm_act(act, "ln1", xn_blocks, bank, 1)
            act.wait_ge(sg("warm"), 1)
            act.activation(warm[:, :], warm[:, :], ACT.Exp)

            def step(m, u):
                if here(m, 0, BATCH - 1):
                    act.wait_ge(sg("qk_ps"), m + 1)
                    if here(m, 2, BATCH):
                        act.wait_ge(sg("scores"), m - 1)
                    for w in range(4):
                        ins = act.activation(qk[:, u, w, :], bank[0][:, w * SEQ:(w + 1) * SEQ], ACT.Identity,
                                             bias=col(QKV_B + w))
                    ins.then_inc(sg("qk"), 1)
                if here(m, 2, BATCH + 1):
                    for a in range(2):
                        act.wait_ge(sg(f"attT_ps{a}"), m - 1)
                        if here(m, 3, BATCH + 1):
                            reach(act, "heads_ps", m - 2)
                        act.activation(attT[:, a].rearrange("p j k -> p (j k)"), bank[2 + a][0:SEQ, 0:HALF * SEQ],
                                       ACT.Copy).then_inc(sg(f"attT{a}"), 1)
                    act.wait_ge(sg("heads_ps"), m - 1)
                    settle(act)
                    for a in range(2):
                        ins = act.activation(at_image(headsT[:, a], m - 2), bank[1][:, a * SEQ:(a + 1) * SEQ],
                                             ACT.Identity, bias=col(QKV_B + 4 + a))
                    ins.then_inc(sg("heads"), 1)
                if here(m, 1, BATCH):
                    v = 1 - u
                    act.wait_ge(sg("shifted"), m)
                    act.activation(att[:, v].rearrange("p h k -> p (h k)"), att[:, v].rearrange("p h k -> p (h k)"),
                                   ACT.Exp).then_inc(sg("expd"), 1)
            each_step(act, step)

        def att_dve(dve):
            dve.wait_ge(sg("slope_in"), 16)
            dve.tensor_tensor(slope[:, 1, :], slope[:, 0, :], slope[:, 0, :], ALU.mult).then_inc(sg("slope"), 1)
            dve.wait_ge(sg("slope"), 1)
            dve.tensor_tensor(slope[:, 2, :], slope[:, 1, :], slope[:, 1, :], ALU.mult).then_inc(sg("slope"), 1)
            dve.wait_ge(sg("slope"), 2)
            dve.tensor_scalar(slope[:, 2, :], slope[:, 2, :], 2.0, None, ALU.mult).then_inc(sg("slope"), 1)
            dve.wait_ge(sg("slope"), 3)
            dve.reciprocal(slope[:, 3, :], slope[:, 2, :]).then_inc(sg("slope"), 1)
            dve.wait_ge(sg("slope"), 4)
            dve.wait_ge(sg("const_in"), 16)
            for h in range(HEADS):
                ins = dve.tensor_scalar(decay[:, h % HALF * 2 + h // HALF, :], const[0:SEQ, C_DIST:C_DIST + SEQ], slope[:, 3, h:h + 1], None,
                                        ALU.mult)
            ins.then_inc(sg("decay"), 1)
            norm_dve(dve, "ln1", st_blocks, xn_blocks, bank)
            dve.wait_ge(sg("decay"), 1)

            def step(m, u):
                v = 1 - u
                if here(m, 1, BATCH):
                    dve.wait_ge(sg("scores"), m)
                    if here(m, 3, BATCH):
                        reach(dve, "attT_ps1", m - 2)
                    dve.scalar_tensor_tensor(out=att[:, v].rearrange("p (j a) k -> p j (a k)", a=2), scalar=0.25, op0=ALU.mult, op1=ALU.add,
                                             in0=quad[0:SEQ, :, 0:2 * SEQ],
                                             in1=decay.rearrange("p (j a) k -> p j (a k)", a=2)).then_inc(sg("scaled"), 1)
                    dve.wait_ge(sg("scaled"), m)
                    dve.tensor_reduce(smax[:, v, :], att[:, v], AX, ALU.max).then_inc(sg("smax"), 1)
                if here(m, 0, BATCH - 1):
                    dve.wait_ge(sg("values"), m + 1)
                    if here(m, 2, BATCH):
                        dve.wait_ge(sg("heads_ps"), m - 1)
                    dve.tensor_copy(vb[:, u, :], bank[1][0:SEQ, 0:2 * P]).then_inc(sg("vb"), 1)
                if here(m, 1, BATCH):
                    dve.wait_ge(sg("expd"), m)
                    dve.tensor_reduce(ssum[:, v, :], att[:, v], AX, ALU.add).then_inc(sg("ssum"), 1)
                    dve.wait_ge(sg("ssum"), m)
                    dve.reciprocal(srec[:, v, :], ssum[:, v, :]).then_inc(sg("srec"), 1)
                    dve.wait_ge(sg("srec"), m)
                    dve.tensor_tensor(att[:, v, HALF:], att[:, v, HALF:],
                                      srec[:, v, HALF:].rearrange("p (h z) -> p h z", z=1).broadcast_to(
                                          [SEQ, HALF, SEQ]), ALU.mult).then_inc(sg("soft1"), 1)
            each_step(dve, step)
            for j in range(NBLK):
                dve.wait_ge(sg("projected"), j + 1)
                dve.scalar_tensor_tensor(out=st_blocks[j], in0=bank[2 + j][:, 0:BLK], scalar=col(OUT_B),
                                         in1=st_blocks[j], op0=ALU.add, op1=ALU.add).then_inc(sg("attended"), 1)

        ITEMS0 = NBLK * C0

        def experts(body):
            def run(eng, count):
                body(0, 0, 0)
                with eng.Fori(0, count // 2 - 1) as i:
                    body(i * 2 + 1, 1, i)
                    body(i * 2 + 2, 0, i + 1)
                body(count - 1, 1, count // 2 - 1)
            return run

        def split_x(tag, before):
            def on_act(act):
                for j in range(NBLK):
                    normed(act, tag, j + 1)
                    act.activation(blk(xnH, j), xn_blocks[j], ACT.Copy).then_inc(sg("x_high"), 1)

            def on_dve(dve):
                for j in range(NBLK):
                    dve.wait_ge(sg("x_high"), before + j + 1)
                    dve.tensor_tensor(blk(xnL, j), xn_blocks[j], blk(xnH, j).bitcast(F32), ALU.subtract
                                      ).then_inc(sg("x_low"), 1)
            return on_act, on_dve

        ln2_high, ln2_low = split_x("ln2", 0)

        def ffn_sp(sp):
            sp.wait_ge(sg("conv"), 2)
            for u in range(2):
                sp.dma_start(w_raw[:, u, :], w0_in[u]).then_inc(sg(f"w_in{u}"), 16)
            sp.wait_ge(sg("attended"), NBLK)
            sp.dma_start(route_w, route_in).then_inc(sg("route_in"), 16)
            sp.dma_start(route_b, routeb_in.broadcast_to([SEQ, 20])).then_inc(sg("route_in"), 16)
            sp.wait_ge(sg("shareT"), 4)
            sp.dma_start(share_dram, shareT).then_inc(sg("share_out"), 16)
            sp.wait_ge(sg("share_out"), 16)
            for u in range(2):
                sp.dma_start(share[:, u, :], share_dram[u:u + 1, :].broadcast_to([P, TOKENS])
                             ).then_inc(sg(f"share_in{u}"), 16)
            with sp.Fori(1, E0 // 2) as i:
                for u in range(2):
                    e = i * 2 + u
                    sp.wait_ge(sg("w_low"), (e - 1) * 3)
                    sp.dma_start(w_raw[:, u, :], w0_in[bass.ds(e, 1)].rearrange("e p n -> (e p) n")
                                 ).then_inc(sg(f"w_in{u}"), 16)
                    sp.wait_ge(sg("xe"), (e - 1) * NBLK)
                    sp.dma_start(share[:, u, :], share_dram[bass.ds(e, 1), :].broadcast_to([P, TOKENS])
                                 ).then_inc(sg(f"share_in{u}"), 16)

        def xe_low(pool, g, b):
            pool.wait_ge(sg("xe_high"), g + 1)
            pool.tensor_tensor(xeL[:, b, :], xe[:, b, :], xeH[:, b, :].bitcast(F32), ALU.subtract
                               ).then_inc(sg("xe_low"), 1)

        def w_split(pool, e, u, half, piece):
            part = slice(piece * H0, (piece + 1) * H0)
            if piece == 0:
                pool.wait_ge(sg(f"w_in{u}"), half * 16 + 16)
                if not isinstance(e, int) or e >= 2:
                    pool.wait_ge(sg("down"), (e - 1) * ITEMS0)
                settle(pool)
            pool.tensor_tensor(wH[:, u, part], w_raw[:, u, part], one[:, :].broadcast_to([P, H0]), ALU.mult
                               ).then_inc(sg("w_high"), 1)
            pool.wait_ge(sg("w_high"), e * 3 + piece + 1)
            pool.tensor_tensor(wL[:, u, part], w_raw[:, u, part], wH[:, u, part].bitcast(F32), ALU.subtract
                               ).then_inc(sg("w_low"), 1)

        def rec_sub(pool, w, s):
            pool.wait_ge(sg("rec_part"), w * 2 + s + 1)
            part = rec_w[:, bass.ds(w, 1), s, :].rearrange("p w n -> p (w n)")
            pool.tensor_tensor(rec_raw, rec_raw, part, ALU.subtract).then_inc(sg("rec_rest"), 1)

        def ffn_pool(pool):
            pool.wait_ge(sg("ones"), 2)
            for e in range(2):
                for piece in range(3):
                    w_split(pool, e, e, 0, piece)
            xe_low(pool, 0, 0)

            def expert(e, u, half):
                last = isinstance(e, int) and e == E0 - 1
                ahead = not isinstance(e, int)
                for j in range(NBLK):
                    if not (last and j == NBLK - 1):
                        xe_low(pool, e * NBLK + j + 1, (j + 1) % 2)
                    if j < 3 and ahead:
                        w_split(pool, e + 1, 1 - u, half + u, j)
                    if ahead and u == 1 and j == 0:
                        pool.wait_ge(sg("shareT"), 4)
                        pool.wait_ge(sg("rec_free"), half + 1)
                        pool.dma_start(rec_raw, rec_in[bass.ds(half, 1)].rearrange("w p n -> (w p) n")
                                       ).then_inc(sg("rec_in"), 16)
                    if ahead and u == 1 and j == 3:
                        rec_sub(pool, half, 0)
                    if ahead and u == 0 and j == 1:
                        rec_sub(pool, half - 1, 1)
            experts(expert)(pool, E0)

        def ffn_pe(pe):
            norm_pe(pe, "ln2", st_blocks, bank, lambda e, j: e.wait_ge(sg("attended"), j + 1))
            normed(pe, "ln2")
            pe.wait_ge(sg("route_in"), 32)
            for t in range(TILES):
                mm = pe.matmul(bank[0][0:SEQ, t * 20:(t + 1) * 20], xn[:, t * SEQ:(t + 1) * SEQ], route_w,
                               start=True, stop=True)
            mm.then_inc(sg("logits"), 1)
            pe.wait_ge(sg("weights"), GROUPS)
            for t in range(TILES):
                mm = pe.transpose(bank[t // 4][0:E0, t % 4 * SEQ:(t % 4 + 1) * SEQ],
                                  weight[:, t].rearrange("p g e -> p (g e)"), ident[0:SEQ, 0:SEQ])
                if t % 4 == 3:
                    mm.then_inc(sg("shareT_ps"), 1)
            pe.wait_ge(sg("shareT"), 4)

            def down(n, k, u, first):
                j, c = divmod(k, C0)
                w = 2 * H0 + c * P
                pe.wait_ge(sg("hid_low"), n + 1)
                split3(pe, bank[j][:, 0:BLK], wH[:, u, w:w + P], wL[:, u, w:w + P], hidH[:, k % 4, :],
                       hidL[:, k % 4, :], start=(first and c == 0), stop=False).then_inc(sg("down"), 1)

            def expert(e, u, half):
                first = isinstance(e, int) and e == 0
                for k in range(ITEMS0):
                    j, c = divmod(k, C0)
                    n = e * ITEMS0 + k
                    if k == 0:
                        pe.wait_ge(sg("w_low"), e * 3 + 3)
                    if first and c == 0:
                        pe.wait_ge(sg("x_low"), j + 1)
                    if not (first and k < 2):
                        pe.wait_ge(sg("silu"), n - 1)
                        pe.wait_ge(sg("gated"), n - 1)
                    w = c * P
                    split3(pe, bank[4 + k % 2][:, 0:BLK], wH[:, u, w:w + P], wL[:, u, w:w + P], blk(xnH, j),
                           blk(xnL, j), start=True, stop=True).then_inc(sg("gate_ps"), 1)
                    if c == 0:
                        pe.wait_ge(sg("xe_low"), e * NBLK + j + 1)
                    w = H0 + c * P
                    split3(pe, bank[6 + k % 2][:, 0:BLK], wH[:, u, w:w + P], wL[:, u, w:w + P], xeH[:, j % 2, :],
                           xeL[:, j % 2, :], start=True, stop=True).then_inc(sg("up_ps"), 1)
                    if k >= LAG:
                        down(n - LAG, k - LAG, u, first)
                    elif not first:
                        down(n - LAG, k - LAG + ITEMS0, 1 - u, isinstance(e, int) and e == 1)
            experts(expert)(pe, E0)
            for k in range(ITEMS0 - LAG, ITEMS0):
                down((E0 - 1) * ITEMS0 + k, k, 1, False)

        def xe_high(act, g, b):
            act.wait_ge(sg("xe"), g + 1)
            if not isinstance(g, int) or g >= 2:
                act.wait_ge(sg("up_ps"), (g - 1) * C0)
            act.activation(xeH[:, b, :], xe[:, b, :], ACT.Copy).then_inc(sg("xe_high"), 1)

        def ffn_act(act):
            norm_act(act, "ln2", xn_blocks, bank, 1)
            ln2_high(act)
            act.wait_ge(sg("routing"), 3)
            act.activation(prob.rearrange("p n k -> p (n k)"), prob.rearrange("p n k -> p (n k)"), ACT.Exp
                           ).then_inc(sg("route_exp"), 1)
            for j in range(4):
                act.wait_ge(sg("shareT_ps"), j + 1)
                act.activation(blk(shareT, j), bank[j][0:E0, 0:BLK], ACT.Copy).then_inc(sg("shareT"), 1)
            act.activation(warm[:, :], warm[:, :], ACT.Silu).then_inc(sg("rec_free"), 1)
            xe_high(act, 0, 0)

            def high(n, k):
                act.wait_ge(sg("gated"), n + 1)
                if not isinstance(n, int) or n >= 4:
                    act.wait_ge(sg("down"), n - 3)
                act.activation(hidH[:, k % 4, :], hid[:, k % 2, :], ACT.Copy).then_inc(sg("hid_high"), 1)

            def rec_cast(w, s):
                if s == 0:
                    act.wait_ge(sg("rec_in"), w * 16 + 16)
                    act.activation(rec_raw, rec_raw, ACT.Copy, scale=1.0 / H_SCALE).then_inc(sg("rec_scaled"), 1)
                    act.wait_ge(sg("rec_scaled"), w + 1)
                else:
                    act.wait_ge(sg("rec_rest"), w * 2 + s)
                settle(act)
                act.activation(rec_w[:, bass.ds(w, 1), s, :].rearrange("p w n -> p (w n)"), rec_raw, ACT.Copy
                               ).then_inc(sg("rec_free" if s == 2 else "rec_part"), 1)

            def expert(e, u, half):
                first = isinstance(e, int) and e == 0
                last = isinstance(e, int) and e == E0 - 1
                for k in range(ITEMS0):
                    n = e * ITEMS0 + k
                    act.wait_ge(sg("gate_ps"), n + 1)
                    if not (first and k < 2):
                        act.wait_ge(sg("gated"), n - 1)
                    act.activation(silu[:, k % 2, :], bank[4 + k % 2][:, 0:BLK], ACT.Silu).then_inc(sg("silu"), 1)
                    if not (first and k == 0):
                        high(n - 1, (k - 1) % ITEMS0)
                    if k % C0 == 1 and not (last and k > 3 * C0):
                        xe_high(act, e * NBLK + k // C0 + 1, (k // C0 + 1) % 2)
                    if not isinstance(e, int):
                        if u == 1 and k == 8:
                            rec_cast(half, 0)
                        if u == 0 and k == 2:
                            rec_cast(half - 1, 1)
                        if u == 0 and k == 14:
                            rec_cast(half - 1, 2)
            experts(expert)(act, E0)
            high(E0 * ITEMS0 - 1, ITEMS0 - 1)

        def route(dve):
            steps = [0]

            def link(ins):
                steps[0] += 1
                ins.then_inc(sg("routing"), 1)
                dve.wait_ge(sg("routing"), steps[0])

            def spread(v):
                return v.rearrange("p (n z) -> p n z", z=1).broadcast_to([SEQ, n_soft, 4])

            dve.wait_ge(sg("route_in"), 32)
            dve.wait_ge(sg("logits"), 1)
            link(dve.tensor_tensor(prob.rearrange("p (t i) k -> p t (i k)", t=TILES),
                                   bank[0][0:SEQ, 0:TILES * 20].rearrange("p (t i) -> p t i", t=TILES),
                                   route_b.rearrange("p (z i) -> p z i", z=1).broadcast_to([SEQ, TILES, 20]),
                                   ALU.add))
            link(dve.tensor_reduce(top[:, 0, :], prob, AX, ALU.max))
            link(dve.tensor_tensor(prob, prob, spread(top[:, 0, :]), ALU.subtract))
            dve.wait_ge(sg("route_exp"), 1)
            link(dve.tensor_reduce(top[:, 0, :], prob, AX, ALU.add))
            link(dve.reciprocal(top[:, 1, :], top[:, 0, :]))
            link(dve.tensor_tensor(prob, prob, spread(top[:, 1, :]), ALU.mult))
            pair = {}
            for i in range(4):
                for j in range(i + 1, 4):
                    b = pair[i, j] = beat[:, len(pair), :]
                    ins = dve.tensor_tensor(b, prob[:, :, j], prob[:, :, i], ALU.is_gt)
            link(ins)
            r = [rank[:, :, i] for i in range(4)]
            dve.tensor_tensor(r[0], pair[0, 1], pair[0, 2], ALU.add)
            dve.scalar_tensor_tensor(out=r[1], in0=pair[0, 1], scalar=-1.0, in1=pair[1, 2], op0=ALU.mult, op1=ALU.add)
            dve.tensor_tensor(r[2], pair[0, 2], pair[1, 2], ALU.add)
            link(dve.tensor_tensor(r[3], pair[0, 3], pair[1, 3], ALU.add))
            dve.tensor_tensor(r[0], r[0], pair[0, 3], ALU.add)
            dve.scalar_tensor_tensor(out=r[1], in0=r[1], scalar=1.0, in1=pair[1, 3], op0=ALU.add, op1=ALU.add)
            dve.scalar_tensor_tensor(out=r[2], in0=r[2], scalar=-1.0, in1=pair[2, 3], op0=ALU.mult, op1=ALU.add)
            link(dve.scalar_tensor_tensor(out=r[3], in0=r[3], scalar=-1.0, in1=pair[2, 3], op0=ALU.mult,
                                          op1=ALU.subtract))
            dve.tensor_scalar(r[2], r[2], 2.0, None, ALU.add)
            link(dve.tensor_scalar(r[3], r[3], 3.0, None, ALU.add))
            second = beat[:, 0:4, :].rearrange("p a n -> p (a n)").rearrange("p (n k) -> p n k", k=4)
            dve.scalar_tensor_tensor(out=pick, in0=rank, scalar=0.0, in1=prob, op0=ALU.is_equal, op1=ALU.mult)
            link(dve.scalar_tensor_tensor(out=second, in0=rank, scalar=1.0, in1=prob, op0=ALU.is_equal,
                                          op1=ALU.mult))
            dve.tensor_reduce(top[:, 0, :], pick, AX, ALU.add)
            link(dve.tensor_reduce(top[:, 1, :], second, AX, ALU.add))
            link(dve.tensor_tensor(top[:, 2, :], top[:, 0, :], top[:, 1, :], ALU.add))
            link(dve.tensor_scalar(top[:, 2, :], top[:, 2, :], 0.9, None, ALU.is_le))
            dve.tensor_tensor(top[:, 1, :], top[:, 1, :], top[:, 2, :], ALU.mult)
            link(dve.tensor_tensor(second, second, spread(top[:, 2, :]), ALU.mult))
            dve.tensor_tensor(pick, pick, second, ALU.add)
            link(dve.scalar_tensor_tensor(out=top[:, 0, :], in0=top[:, 0, :], scalar=1e-9, in1=top[:, 1, :],
                                          op0=ALU.add, op1=ALU.add))
            link(dve.reciprocal(top[:, 1, :], top[:, 0, :]))
            link(dve.tensor_tensor(pick, pick, spread(top[:, 1, :]), ALU.mult))
            by_tile = pick.rearrange("p (t i) k -> p t i k", t=TILES)
            for g in range(GROUPS):
                dve.scalar_tensor_tensor(out=weight[:, :, g, :], in0=by_tile[:, :, 1 + g, :],
                                         scalar=1.0 / float(GROUPS) ** 0.5,
                                         in1=by_tile[:, :, 0, g:g + 1].broadcast_to([SEQ, TILES, 4]),
                                         op0=ALU.mult, op1=ALU.mult).then_inc(sg("weights"), 1)

        def ffn_dve(dve):
            norm_dve(dve, "ln2", st_blocks, xn_blocks, bank)
            ln2_low(dve)
            route(dve)

            def scale_x(g, b, j, u, loads):
                dve.wait_ge(sg(f"share_in{u}"), loads)
                if not isinstance(g, int) or g >= 2:
                    dve.wait_ge(sg("xe_low"), g - 1)
                dve.tensor_tensor(xe[:, b, :], xn_blocks[j], blk(share[:, u], j), ALU.mult).then_inc(sg("xe"), 1)

            def low(n, k):
                dve.wait_ge(sg("hid_high"), n + 1)
                dve.tensor_tensor(hidL[:, k % 4, :], hid[:, k % 2, :], hidH[:, k % 4, :].bitcast(F32), ALU.subtract
                                  ).then_inc(sg("hid_low"), 1)

            scale_x(0, 0, 0, 0, 16)

            def expert(e, u, half):
                first = isinstance(e, int) and e == 0
                last = isinstance(e, int) and e == E0 - 1
                for k in range(ITEMS0):
                    n = e * ITEMS0 + k
                    j = k // C0
                    if k % C0 == 0 and not (last and j == NBLK - 1):
                        if j < NBLK - 1:
                            scale_x(e * NBLK + j + 1, (j + 1) % 2, j + 1, u, half * 16 + 16)
                        else:
                            scale_x(e * NBLK + j + 1, 0, 0, 1 - u, (half + u) * 16 + 16)
                    dve.wait_ge(sg("silu"), n + 1)
                    dve.wait_ge(sg("up_ps"), n + 1)
                    if not (first and k < 2):
                        dve.wait_ge(sg("hid_low"), n - 1)
                    dve.tensor_tensor(hid[:, k % 2, :], silu[:, k % 2, :], bank[6 + k % 2][:, 0:BLK], ALU.mult
                                      ).then_inc(sg("gated"), 1)
                    if not (first and k == 0):
                        low(n - 1, (k - 1) % ITEMS0)
            experts(expert)(dve, E0)
            low(E0 * ITEMS0 - 1, ITEMS0 - 1)
            dve.wait_ge(sg("down"), E0 * ITEMS0)
            for j in range(NBLK):
                dve.tensor_tensor(st_blocks[j], st_blocks[j], bank[j][:, 0:BLK], ALU.add).then_inc(sg("routed"), 1)

        PLACE = [(0, 1, 3, 2, 4)[m // KH] * KH + m % KH for m in range(GCH)]
        SIG, CAND, CELL, MEM = 0, 3 * SW, 4 * SW, 5 * SW
        HALF_SEQ = SEQ // 2
        hist_k = hist.rearrange("p t n -> p (t n)").rearrange("p (k t b) -> p k t b", k=KH, b=BATCH)

        def wave(eng, both):
            for t in range(4):
                both(t, t % 2)
            with eng.Fori(2, SEQ // 2 - 1) as i:
                for u in range(2):
                    both(i * 2 + u, u)
            both(SEQ - 2, 0)
            both(SEQ - 1, 1)
            both(SEQ, 0)

        def rec_sp(sp):
            sp.wait_ge(sg("routed"), NBLK)
            sp.dma_start(bias_raw[0:96], recb_in).then_inc(sg("recb_in"), 16)
            sp.dma_start(fc_w, fcw_in).then_inc(sg("fcw_in"), 16)
            sp.dma_start(fb2, fb2_in).then_inc(sg("fg_in"), 16)
            sp.dma_start(fg_w, fg_in).then_inc(sg("fg_in"), 16)
            sp.dma_start(fg_b, fgb_in.broadcast_to([SEQ, E1])).then_inc(sg("fg_in"), 16)
            for u in range(2):
                sp.dma_start(f_raw[:, u, :], f_in[u]).then_inc(sg(f"f_in{u}"), 16)

        def rec_pool(pool):
            pool.wait_ge(sg("xpair"), 2)

            def load(t, u):
                if here(t, 2, SEQ):
                    pool.wait_ge(sg("pre_ps0"), t - 1)
                settle(pool)
                pool.tensor_copy(xcur[:, u].rearrange("p g b -> p (g b)"),
                                 xpair[:, bass.ds(t, 1)].rearrange("p t g b -> p (t g b)")
                                 ).then_inc(sg("xcur"), 1)

            load(0, 0)

            def both(t, u):
                if here(t, 0, SEQ - 2):
                    load(t + 1, 1 - u)
                if here(t, 1, SEQ):
                    pool.wait_ge(sg("state1"), t)
                    settle(pool)
                    pool.tensor_copy(hist_k[:, :, bass.ds(t - 1, 1), :].rearrange("p k t b -> p k (t b)"),
                                     hfull[:, 1, 1 - u, :].rearrange("p (k b) -> p k b", k=KH)
                                     ).then_inc(sg("hist"), 1)
            wave(pool, both)

        def rec_pe(pe):
            norm_pe(pe, "ln3", st_blocks, bank, lambda e, j: e.wait_ge(sg("routed"), j + 1))
            normed(pe, "ln3")
            pe.wait_ge(sg("bias"), 1)
            pe.wait_ge(sg("rec_free"), 7 + 1)
            pe.wait_ge(sg("rec_part"), 7 * 2)

            def product(l, u, w, pair):
                to = bank[2 * l + u][:, 0:2 * GW].rearrange("p (g m b) -> p g m b", g=2, m=GCH)
                for m in range(GCH):
                    for s in range(3):
                        mm = pe.matmul(to[:, :, PLACE[m], :], rec_w[:, w, s, m * P:(m + 1) * P], pair,
                                       start=False, stop=False, skip_group_check=True)
                return mm

            def start_bias(l, u):
                pe.matmul(bank[2 * l + u][:, 0:GW], bias_part[0:96, l, :], bias_sel[0:96, :], start=True, stop=False,
                          skip_group_check=True)

            def open0(t, u):
                if here(t, 2, SEQ):
                    pe.wait_ge(sg("sum0"), t - 1)
                start_bias(0, u)
                pe.wait_ge(sg("xcur"), t + 1)
                return product(0, u, WX0, xcur[:, u])

            open0(0, 0).then_inc(sg("pre_ps0"), 1)
            open0(1, 1)

            def both(t, u):
                v = 1 - u
                if here(t, 1, SEQ - 1):
                    pe.wait_ge(sg("state0"), t)
                    for k in range(KH):
                        mm = product(0, u, WH0 + k, hpair[:, 0, v, k])
                    mm.then_inc(sg("pre_ps0"), 1)
                if here(t, 1, SEQ):
                    if here(t, 3, SEQ):
                        reach(pe, "sum1", t - 2)
                    start_bias(1, v)
                    if isinstance(t, int) and t == SEQ:
                        pe.wait_ge(sg("state0"), t)
                    for k in range(KH):
                        mm = product(1, v, WX1 + k, hpair[:, 0, v, k])
                    if here(t, 2, SEQ):
                        pe.wait_ge(sg("state1"), t - 1)
                        for k in range(KH):
                            mm = product(1, v, WH1 + k, hpair[:, 1, u, k])
                    mm.then_inc(sg("pre_ps1"), 1)
                if here(t, 1, SEQ - 2):
                    open0(t + 1, v)
            wave(pe, both)
            pe.wait_ge(sg("fcw_in"), 16)
            pe.wait_ge(sg("hist"), SEQ)
            for j in range(NBLK):
                for k in range(KH):
                    mm = pe.matmul(bank[4 + j][:, 0:BLK], fc_w[:, k, :],
                                   blk(hist_k[:, k].rearrange("p t b -> p (t b)"), j),
                                   start=(k == 0), stop=(k == KH - 1))
                mm.then_inc(sg("fc"), 1)

        def rec_act(act):
            norm_act(act, "ln3", xn_blocks, bank, 1)
            act.activation(warm[:, :], warm[:, :], ACT.Sigmoid)

            def layer(l, n):
                act.wait_ge(sg(f"sum{l}"), n)
                act.activation(gates[:, l, SIG:3 * SW], pre[:, l, 0:3 * SW], ACT.Sigmoid)
                act.activation(gates[:, l, CAND:CAND + 4 * SW].rearrange("p (a n) -> p a n", a=2)[:, :, 0:SW],
                               pre[:, l, 3 * SW:5 * SW].rearrange("p (a n) -> p a n", a=2), ACT.Tanh
                               ).then_inc(sg(f"gates{l}"), 1)
                act.wait_ge(sg(f"cell{l}"), n)
                act.activation(tanh_c[:, l], gates[:, l, CELL:CELL + SW], ACT.Tanh).then_inc(sg(f"tanh_c{l}"), 1)

            def both(t, u):
                if here(t, 0, SEQ - 1):
                    layer(0, t + 1)
                if here(t, 1, SEQ):
                    layer(1, t)
            wave(act, both)
            for j in range(NBLK):
                act.wait_ge(sg("fc"), j + 1)
                if j >= 2:
                    act.wait_ge(sg("recurred"), j - 1)
                act.activation(fc_sb[:, j % 2], bank[4 + j][:, 0:BLK], ACT.Identity, bias=col(FC_B),
                               scale=1.0 / H_SCALE).then_inc(sg("fc_sb"), 1)

        def rec_dve(dve):
            norm_dve(dve, "ln3", st_blocks, xn_blocks, bank)
            steps = [0]

            def link(ins):
                steps[0] += 1
                ins.then_inc(sg("bias_step"), 1)
                dve.wait_ge(sg("bias_step"), steps[0])

            dve.wait_ge(sg("recb_in"), 16)
            for s in range(3):
                link(dve.tensor_copy(bias_cast[0:96, :, s, :], bias_raw[0:96]))
                if s < 2:
                    link(dve.tensor_tensor(bias_raw[0:96], bias_raw[0:96], bias_cast[0:96, :, s, :], ALU.subtract))
            for s in range(3):
                dve.tensor_copy(bias_part[32 * s:32 * s + 32], bias_cast[32 * s:32 * s + 32, :, s, :])
            dve.tensor_copy(bias_sel[0:96, :], const[0:96, C_SEL:C_SEL + GW]).then_inc(sg("bias"), 1)
            xn_steps = xn[:, :].rearrange("p (t b) -> p t b", b=BATCH)
            for q in range(2):
                part = slice(q * HALF_SEQ, (q + 1) * HALF_SEQ)
                normed(dve, "ln3")
                dve.tensor_scalar(xpair[:, part, 0, :], xn_steps[:, part], H_SCALE, None, ALU.mult
                                  ).then_inc(sg("xpair_high"), 1)
                dve.wait_ge(sg("xpair_high"), q + 1)
                dve.scalar_tensor_tensor(out=xpair[:, part, 1, :], in0=xn_steps[:, part], scalar=H_SCALE,
                                         in1=xpair[:, part, 0, :], op0=ALU.mult, op1=ALU.subtract
                                         ).then_inc(sg("xpair"), 1)
            for l in range(2):
                dve.memset(gates[:, l, CELL:CELL + SW], 0.0).then_inc(sg("cell_zero"), 1)
            dve.wait_ge(sg("cell_zero"), 2)

            def layer(l, n, u):
                dve.wait_ge(sg(f"pre_ps{l}"), n)
                dve.tensor_reduce(pre[:, l].rearrange("p (n z) -> p n z", z=1), bank[2 * l + u][:, 0:2 * GW].rearrange("p (g n) -> p n g", g=2), AX, ALU.add
                                  ).then_inc(sg(f"sum{l}"), 1)
                dve.wait_ge(sg(f"gates{l}"), n)
                dve.tensor_tensor(prod[:, l], gates[:, l, SIG:2 * SW], gates[:, l, CAND:CAND + 2 * SW], ALU.mult
                                  ).then_inc(sg(f"prod{l}"), 1)
                dve.wait_ge(sg(f"prod{l}"), n)
                dve.tensor_tensor(gates[:, l, CELL:CELL + SW], prod[:, l, 0:SW], prod[:, l, SW:2 * SW], ALU.add
                                  ).then_inc(sg(f"cell{l}"), 1)
                dve.wait_ge(sg(f"tanh_c{l}"), n)
                dve.scalar_tensor_tensor(out=out_h[:, l], in0=gates[:, l, 2 * SW:3 * SW], scalar=H_SCALE,
                                         in1=tanh_c[:, l], op0=ALU.mult, op1=ALU.mult).then_inc(sg(f"out{l}"), 1)
                dve.wait_ge(sg(f"out{l}"), n)
                if l == 0 and here(n, 3, SEQ):
                    dve.wait_ge(sg("pre_ps1"), n - 2)
                if l == 1 and here(n, 3, SEQ):
                    dve.wait_ge(sg("hist"), n - 2)
                high = hpair[:, l, u, :, 0, :]
                low = hpair[:, l, u, :, 1, :]
                full = hfull[:, l, u, :].rearrange("p (k b) -> p k b", k=KH)
                mem = gates[:, l, MEM:MEM + SW].rearrange("p (k b) -> p k b", k=KH)
                scaled = out_h[:, l].rearrange("p (k b) -> p k b", k=KH)
                dve.scalar_tensor_tensor(out=high, in0=mem, scalar=H_SCALE, in1=scaled, op0=ALU.mult, op1=ALU.add)
                dve.scalar_tensor_tensor(out=full, in0=mem, scalar=H_SCALE, in1=scaled, op0=ALU.mult, op1=ALU.add
                                         ).then_inc(sg(f"full{l}"), 1)
                dve.wait_ge(sg(f"full{l}"), n)
                dve.tensor_tensor(low, full, high, ALU.subtract).then_inc(sg(f"state{l}"), 1)

            def both(t, u):
                if here(t, 0, SEQ - 1):
                    layer(0, t + 1, u)
                if here(t, 1, SEQ):
                    layer(1, t, 1 - u)
            wave(dve, both)
            for j in range(NBLK):
                dve.wait_ge(sg("fc_sb"), j + 1)
                dve.tensor_tensor(st_blocks[j], st_blocks[j], fc_sb[:, j % 2], ALU.add).then_inc(sg("recurred"), 1)

        ITEMS1 = NBLK * C1
        ln4_high, ln4_low = split_x("ln4", NBLK)

        def last_sp(sp):
            sp.wait_ge(sg("mask_T"), NBLK)
            sp.dma_start(mask_dram, mask_T).then_inc(sg("mask_out"), 16)
            sp.wait_ge(sg("mask_out"), 16)
            for u in range(2):
                sp.dma_start(mask_b[:, u, :], mask_dram[u:u + 1, :].broadcast_to([P, TOKENS])
                             ).then_inc(sg(f"mask_in{u}"), 16)
            with sp.Fori(1, E1 // 2) as i:
                for u in range(2):
                    e = i * 2 + u
                    sp.wait_ge(sg("f_low"), e - 1)
                    sp.dma_start(f_raw[:, u, :], f_in[bass.ds(e, 1)].rearrange("e p n -> (e p) n")
                                 ).then_inc(sg(f"f_in{u}"), 16)
                    sp.wait_ge(sg("masked"), (e - 1) * ITEMS1)
                    sp.dma_start(mask_b[:, u, :], mask_dram[bass.ds(e, 1), :].broadcast_to([P, TOKENS])
                                 ).then_inc(sg(f"mask_in{u}"), 16)
            for j in range(NBLK):
                sp.wait_ge(sg("final"), j + 1)
                sp.dma_start(blk(out, j), st_blocks[j]).then_inc(sg("out"), 16)
            sp.wait_ge(sg("out"), NBLK * 16)

        def last_pool(pool):
            pool.wait_ge(sg("recurred"), NBLK)

            def f_split(e, u, half):
                pool.wait_ge(sg(f"f_in{u}"), half * 16 + 16)
                if not isinstance(e, int) or e >= 2:
                    pool.wait_ge(sg("f_down"), (e - 1) * ITEMS1)
                settle(pool)
                pool.tensor_tensor(wH[:, u, 0:F0], f_raw[:, u, :], one[:, :].broadcast_to([P, F0]), ALU.mult
                                   ).then_inc(sg("f_high"), 1)
                pool.wait_ge(sg("f_high"), e + 1)
                pool.tensor_tensor(wL[:, u, 0:F0], f_raw[:, u, :], wH[:, u, 0:F0].bitcast(F32), ALU.subtract
                                   ).then_inc(sg("f_low"), 1)
                at = slice(FB1 + e * C1, FB1 + (e + 1) * C1) if isinstance(e, int) else bass.ds(e * C1 + FB1, C1)
                pool.tensor_tensor(f_bias[:, u, :], cols[:, at], one[:, :].broadcast_to([P, C1]), ALU.mult
                                   ).then_inc(sg("f_bias"), 1)

            def expert(e, u, half):
                if isinstance(e, int) and e == 0:
                    f_split(0, 0, 0)
                if not (isinstance(e, int) and e == E1 - 1):
                    f_split(e + 1, 1 - u, half + u)
            experts(expert)(pool, E1)

        def last_pe(pe):
            norm_pe(pe, "ln4", st_blocks, bank, lambda e, j: e.wait_ge(sg("recurred"), j + 1))
            normed(pe, "ln4")
            pe.wait_ge(sg("fg_in"), 48)
            for t in range(TILES):
                mm = pe.matmul(bank[7][0:SEQ, t * E1:(t + 1) * E1], xn[:, t * SEQ:(t + 1) * SEQ], fg_w,
                               start=True, stop=True)
            mm.then_inc(sg("f_logits"), 1)
            pe.wait_ge(sg("mask"), 1)
            for t in range(TILES):
                mm = pe.transpose(bank[t // 4][0:E1, t % 4 * SEQ:(t % 4 + 1) * SEQ], chosen[:, t],
                                  ident[0:SEQ, 0:SEQ])
                if t % 4 == 3:
                    mm.then_inc(sg("mask_ps"), 1)
            for j in range(NBLK):
                pe.wait_ge(sg("mask_T"), j + 1)
                pe.matmul(bank[j][:, 0:BLK], fb2, blk(mask_T, j), start=True, stop=False, skip_group_check=True)

            def down(n, k, u):
                j, c = divmod(k, C1)
                w = H1 + c * P
                pe.wait_ge(sg("f_hid_low"), n + 1)
                split3(pe, bank[j][:, 0:BLK], wH[:, u, w:w + P], wL[:, u, w:w + P], hidH[:, k % 4, :],
                       hidL[:, k % 4, :], start=False, stop=False).then_inc(sg("f_down"), 1)

            def expert(e, u, half):
                first = isinstance(e, int) and e == 0
                for k in range(ITEMS1):
                    j, c = divmod(k, C1)
                    n = e * ITEMS1 + k
                    if k == 0:
                        pe.wait_ge(sg("f_low"), e + 1)
                    if first and c == 0:
                        pe.wait_ge(sg("x_low"), NBLK + j + 1)
                    if not (first and k < 4):
                        pe.wait_ge(sg("relu"), n - 3)
                    w = c * P
                    split3(pe, bank[4 + k % 4][:, 0:BLK], wH[:, u, w:w + P], wL[:, u, w:w + P], blk(xnH, j),
                           blk(xnL, j), start=True, stop=True).then_inc(sg("f_up"), 1)
                    if k >= LAG:
                        down(n - LAG, k - LAG, u)
                    elif not first:
                        down(n - LAG, k - LAG + ITEMS1, 1 - u)
            experts(expert)(pe, E1)
            for k in range(ITEMS1 - LAG, ITEMS1):
                down((E1 - 1) * ITEMS1 + k, k, 1)

        def last_act(act):
            norm_act(act, "ln4", xn_blocks, bank, 1)
            ln4_high(act)
            for j in range(NBLK):
                act.wait_ge(sg("mask_ps"), j + 1)
                act.activation(blk(mask_T, j), bank[j][0:E1, 0:BLK], ACT.Copy).then_inc(sg("mask_T"), 1)
            act.activation(warm[:, :], warm[:, :], ACT.Relu)

            def high(n, k):
                act.wait_ge(sg("masked"), n + 1)
                if not isinstance(n, int) or n >= 4:
                    act.wait_ge(sg("f_down"), n - 3)
                act.activation(hidH[:, k % 4, :], fhid[:, k % 2, :], ACT.Copy).then_inc(sg("f_hid_high"), 1)

            def expert(e, u, half):
                first = isinstance(e, int) and e == 0
                for k in range(ITEMS1):
                    n = e * ITEMS1 + k
                    c = k % C1
                    if c == 0 and k == 0:
                        act.wait_ge(sg("f_bias"), e + 1)
                    act.wait_ge(sg("f_up"), n + 1)
                    if not (first and k < 2):
                        act.wait_ge(sg("masked"), n - 1)
                    act.activation(relu[:, k % 2, :], bank[4 + k % 4][:, 0:BLK], ACT.Relu,
                                   bias=f_bias[:, u, c:c + 1]
                                   ).then_inc(sg("relu"), 1)
                    if not (first and k == 0):
                        high(n - 1, (k - 1) % ITEMS1)
            experts(expert)(act, E1)
            high(E1 * ITEMS1 - 1, ITEMS1 - 1)

        def last_dve(dve):
            norm_dve(dve, "ln4", st_blocks, xn_blocks, bank)
            ln4_low(dve)
            steps = [0]

            def link(ins):
                steps[0] += 1
                ins.then_inc(sg("mask_step"), 1)
                dve.wait_ge(sg("mask_step"), steps[0])

            def spread(v):
                return v.rearrange("p (t z) -> p t z", z=1).broadcast_to([SEQ, TILES, E1])

            dve.wait_ge(sg("f_logits"), 1)
            dve.wait_ge(sg("fg_in"), 48)
            link(dve.tensor_tensor(logit, bank[7][0:SEQ, 0:TILES * E1].rearrange("p (t e) -> p t e", t=TILES),
                                   fg_b.rearrange("p (z e) -> p z e", z=1).broadcast_to([SEQ, TILES, E1]), ALU.add))
            link(dve.tensor_reduce(best[:, 0], logit, AX, ALU.max))
            link(dve.tensor_tensor(chosen, logit, spread(best[:, 0]), ALU.is_equal))
            link(dve.tensor_tensor(chosen, chosen,
                                   const[0:SEQ, C_PRI:C_PRI + E1].rearrange("p (z e) -> p z e", z=1).broadcast_to(
                                       [SEQ, TILES, E1]), ALU.mult))
            link(dve.tensor_reduce(best[:, 1], chosen, AX, ALU.max))
            dve.tensor_tensor(chosen, chosen, spread(best[:, 1]), ALU.is_equal).then_inc(sg("mask"), 1)

            def low(n, k):
                dve.wait_ge(sg("f_hid_high"), n + 1)
                dve.tensor_tensor(hidL[:, k % 4, :], fhid[:, k % 2, :], hidH[:, k % 4, :].bitcast(F32), ALU.subtract
                                  ).then_inc(sg("f_hid_low"), 1)

            def expert(e, u, half):
                first = isinstance(e, int) and e == 0
                for k in range(ITEMS1):
                    n = e * ITEMS1 + k
                    if k == 0:
                        dve.wait_ge(sg(f"mask_in{u}"), half * 16 + 16)
                    dve.wait_ge(sg("relu"), n + 1)
                    if not (first and k < 2):
                        dve.wait_ge(sg("f_hid_low"), n - 1)
                    dve.tensor_tensor(fhid[:, k % 2, :], relu[:, k % 2, :], blk(mask_b[:, u], k // C1), ALU.mult
                                      ).then_inc(sg("masked"), 1)
                    if not (first and k == 0):
                        low(n - 1, (k - 1) % ITEMS1)
            experts(expert)(dve, E1)
            low(E1 * ITEMS1 - 1, ITEMS1 - 1)
            dve.wait_ge(sg("f_down"), E1 * ITEMS1)
            for j in range(NBLK):
                dve.tensor_tensor(st_blocks[j], st_blocks[j], bank[j][:, 0:BLK], ALU.add).then_inc(sg("final"), 1)


        block = ctx.enter_context(nc.Block())

        @block.sync
        def _(sp):
            tok_sp(sp)
            ffn_sp(sp)
            rec_sp(sp)
            last_sp(sp)

        @block.gpsimd
        def _(pool):
            tok_pool(pool)
            att_pool(pool)
            ffn_pool(pool)
            rec_pool(pool)
            last_pool(pool)

        @block.tensor
        def _(pe):
            tok_pe(pe)
            att_pe(pe)
            ffn_pe(pe)
            rec_pe(pe)
            last_pe(pe)

        @block.scalar
        def _(act):
            tok_act(act)
            att_act(act)
            ffn_act(act)
            rec_act(act)
            last_act(act)

        @block.vector
        def _(dve):
            tok_dve(dve)
            att_dve(dve)
            ffn_dve(dve)
            rec_dve(dve)
            last_dve(dve)


def kernel(**inputs):
    import numpy as np
    import concourse.bacc as bacc
    from concourse.bass_utils import run_bass_kernel_spmd

    a = {k: np.asarray(v) for k, v in inputs.items()}

    def padded_heads(v):
        v = v.reshape(v.shape[:-1] + (HEADS, HD))
        z = np.zeros(v.shape[:-1] + (PAD,), v.dtype)
        z[..., :HD] = v
        return z.reshape(v.shape[:-2] + (2, P))

    img = np.zeros((BATCH, SIDE + 2, SIDE + 2, COLORS), a["x"].dtype)
    img[:, 1:-1, 1:-1] = a["x"]
    grid = np.stack([img[:, PATCH * p:PATCH * p + WIDE, PATCH * q:PATCH * q + WIDE]
                     for p in range(GRID) for q in range(GRID)])
    patches = grid.reshape(PATCHES, BATCH, RCH, ROWS2).transpose(3, 2, 0, 1).reshape(ROWS2, RCH, EMB)
    taps = np.zeros((SHIFTS, WIDE, WIDE, COLORS, D), a["L0_tok_conv_w"].dtype)
    for s, (di, dj) in enumerate(((0, 0), (0, -1), (0, 1), (-1, 0), (1, 0))):
        taps[s, 1 + di:1 + di + PATCH, 1 + dj:1 + dj + PATCH] = a["L0_tok_conv_w"][:, :, 3 * s:3 * s + 3]
    taps = taps.reshape(SHIFTS, RCH, ROWS2, D).transpose(2, 0, 1, 3)

    wq, wk, wv = (padded_heads(a["L0_attn_in_proj_w"][i * D:(i + 1) * D].T) for i in range(3))
    qkvw = np.concatenate([wq, wk, wv], axis=1)
    bq, bk, bv = (padded_heads(a["L0_attn_in_proj_b"][i * D:(i + 1) * D]) for i in range(3))
    outw = padded_heads(a["L0_attn_out_proj_w"]).transpose(2, 1, 0)

    cols = np.zeros((P, NCOLS), np.float32)
    for i, v in ((CONV_B, a["L0_tok_conv_b"]), (GAMMA, a["L0_tok_gamma"]), (BETA, a["L0_tok_beta"]),
                 (DENSE_B, a["L0_tok_dense_b"]), (OUT_B, a["L0_attn_out_proj_b"]), (FC_B, a["L1_attn_bfc"])):
        cols[:, i] = v
    cols[:, QKV_B:QKV_B + 6] = np.concatenate([bq, bk, bv]).T
    cols[:, FB1:] = a["L1_ffn_b1"].reshape(E1 * C1, P).T

    const = np.zeros((P, NCONST), np.float32)
    const[:, C_ID:C_ID + P] = np.eye(P)
    i = np.arange(SEQ)
    const[:SEQ, C_DIST:C_DIST + SEQ] = -(i[None, :] - i[:, None]).astype(np.float32) ** 2
    gate_place = [(0, 1, 3, 2, 4)[m // KH] * KH + m % KH for m in range(GCH)]
    for s in range(3):
        for m in range(GCH):
            const[32 * s + m, C_SEL + gate_place[m] * BATCH:C_SEL + (gate_place[m] + 1) * BATCH] = 1.0

    const[:, C_PRI:C_PRI + E1] = np.arange(E1, 0, -1)

    w2 = a["L0_ffn_W2"].reshape(E0, C0, P, D).transpose(0, 2, 1, 3).reshape(E0, P, H0)
    w0 = np.concatenate([a["L0_ffn_W1"], a["L0_ffn_W3"], w2], axis=2)
    route = np.concatenate([a["L0_ffn_Wr"], a["L0_ffn_Wgate"].transpose(1, 0, 2).reshape(D, E0)], axis=1)
    routeb = np.concatenate([a["L0_ffn_br"], a["L0_ffn_bgate"].reshape(E0)])[None]
    rec = np.concatenate([a["L1_attn_Wx0"], a["L1_attn_Wh0"], a["L1_attn_Wx1"], a["L1_attn_Wh1"]])
    recb = np.zeros((96, 2, P), np.float32)
    for s in range(3):
        for l in range(2):
            recb[32 * s:32 * s + GCH, l] = a[f"L1_attn_b{l}"].reshape(GCH, P)
    f2 = a["L1_ffn_W2"].reshape(E1, C1, P, D).transpose(0, 2, 1, 3).reshape(E1, P, H1)
    f = np.concatenate([a["L1_ffn_W1"], f2], axis=2)

    arrays = {
        "taps": taps, "patches": patches, "txt": a["txt"].transpose(2, 1, 0).reshape(D, WORDS * BATCH),
        "cols": cols, "const": const, "dense": a["L0_tok_dense_w"], "qkvw": qkvw, "outw": outw,
        "heads": a["L0_attn_t"][None], "w0": w0, "route": route, "routeb": routeb,
        "rec": rec.reshape(7, P, GP), "recb": recb,
        "fcw": a["L1_attn_Wfc"].reshape(KH, P, D).transpose(1, 0, 2), "f": f, "fb2": a["L1_ffn_b2"],
        "fg": a["L1_ffn_Wg"], "fgb": a["L1_ffn_bg"][None],
    }
    arrays = {f"in_{k}": np.ascontiguousarray(v) for k, v in arrays.items()}
    nc = bacc.Bacc("TRN2", target_bir_lowering=False, num_devices=1)
    args = [nc.dram_tensor(k, v.shape, mybir.dt.from_np(v.dtype), kind="ExternalInput").ap()
            for k, v in arrays.items()]
    args.append(nc.dram_tensor("out_stream", (D, TOKENS), F32, kind="ExternalOutput").ap())
    build(nc, *args)
    r = run_bass_kernel_spmd(nc, [arrays], core_ids=[0])
    got = r.results[0]["out_stream"].reshape(D, SEQ, BATCH)
    return np.ascontiguousarray(got.transpose(2, 1, 0))
```

```python
from contextlib import ExitStack

import concourse.bass as bass
from concourse import mybir

F32 = mybir.dt.float32
F32R = mybir.dt.float32r
BF16 = mybir.dt.bfloat16
F16 = mybir.dt.float16
ALU = mybir.AluOpType
ACT = mybir.ActivationFunctionType
AX = mybir.AxisListType.X

P = 128
BATCH, SIDE, COLORS = 16, 112, 3
PATCH = 16
GRID = SIDE // PATCH
WIDE = PATCH + 2
WORDS = 77
PATCHES = GRID * GRID
SEQ = PATCHES + WORDS
TOKENS = SEQ * BATCH
NBLK = 4
BLK = TOKENS // NBLK
TILES = TOKENS // SEQ
D = 128
ROWS2 = 2 * WIDE * COLORS
RCH = WIDE // 2
EMB = PATCHES * BATCH
EBLK = EMB // 2
SHIFTS = 5
HEADS, HD = 8, 16
HALF = HEADS // 2
PAD = P // HALF
E0, GROUPS, H0 = 16, 4, 512
C0 = H0 // P
W0 = 3 * H0
E1, H1 = 8, 256
C1 = H1 // P
F0 = 2 * H1
RH = 256
KH = RH // P
GCH = 5 * RH // P
GP = GCH * P
GW = GCH * BATCH
SW = KH * BATCH
WX0, WH0, WX1, WH1 = 0, 1, 3, 5
H_SCALE = 1024.0
W_SCALE = 64.0
ROUND = 4
LAG = 2
CONV_B, GAMMA, BETA, DENSE_B, OUT_B, FC_B, QKV_B = 0, 1, 2, 3, 4, 5, 6
FB1 = QKV_B + 6
NCOLS = FB1 + E1 * C1
C_ID, C_DIST, C_SEL = 0, P, P + SEQ
C_PRI = C_SEL + GW
NCONST = C_PRI + E1


def build(nc, taps_in, patches_in, txt_in, cols_in, const_in, dense_in, qkvw_in, outw_in, heads_in, w0_in,
          route_in, routeb_in, rec_in, recb_in, fcw_in, f_in, fb2_in, fg_in, fgb_in, out):
    share_dram = nc.dram_tensor("share_scratch", (E0, TOKENS), F32, kind="Internal").ap()
    mask_dram = nc.dram_tensor("mask_scratch", (E1, TOKENS), F32, kind="Internal").ap()

    with ExitStack() as ctx:
        def sb(name, shape, dt=F32):
            return ctx.enter_context(nc.sbuf_tensor(name, shape, dt))

        sems = {}

        def sg(name):
            if name not in sems:
                sems[name] = ctx.enter_context(nc.semaphore(name))
            return sems[name]

        def reach(eng, name, value):
            if not isinstance(value, int) or value > 0:
                eng.wait_ge(sg(name), value)

        def settle(eng):
            eng.wait_ge(sg("warm"), 1)

        low_banks = [ctx.enter_context(nc.psum_tensor(f"bank{i}", [P, 512], F32)) for i in range(4)]
        quad = ctx.enter_context(nc.psum_tensor("quad", [P, 4, 512], F32))
        bank = [b[:, :] for b in low_banks] + [quad[:, i, :] for i in range(4)]

        stream = sb("stream", [P, TOKENS])
        xn = sb("xn", [P, TOKENS])
        mean_mat = sb("mean_mat", [P, P])
        cols = sb("cols", [P, NCOLS])
        const = sb("const", [P, NCONST])
        eps = sb("eps", [P, 2])
        spread_row = sb("spread_row", [P, P])
        warm = sb("warm", [P, 1])
        one = sb("one", [P, 1])
        ident = const[:, C_ID:C_ID + P]

        wH = sb("wH", [P, 2, W0], F32R)
        wL = sb("wL", [P, 2, W0], F32R)
        xnH = sb("xnH", [P, TOKENS], F32R)
        xnL = sb("xnL", [P, TOKENS], F32R)
        xeH = sb("xeH", [P, 2, BLK], F32R)
        xeL = sb("xeL", [P, 2, BLK], F32R)
        hidH = sb("hidH", [P, 4, BLK], F32R)
        hidL = sb("hidL", [P, 4, BLK], F32R)

        AREA = 30000
        area = sb("area", [P, AREA])

        def region(start, size=AREA):
            at = [start]

            def view(words, parts=P):
                a = area[0:parts, at[0]:at[0] + words]
                at[0] += words
                assert at[0] <= min(AREA, size), (at[0], size)
                return a
            return view, at

        view, at = region(0)
        sq = view(NBLK * BLK).rearrange("p (u n) -> p u n", u=NBLK)
        STAGE = at[0]
        taps = view(SHIFTS * RCH * D, ROWS2).rearrange("p (s k d) -> p s k d", s=SHIFTS, k=RCH)
        patches = view(RCH * EMB, ROWS2).rearrange("p (k n) -> p k n", k=RCH)
        conv = view(EMB)
        emb = view(EMB)
        dense_w = view(D)
        LOADED = AREA - (6 * P + 2 * P + 4 * HEADS)
        view, at = region(LOADED)
        qkv_w = view(6 * P).rearrange("p (w n) -> p w n", w=6)
        out_w = view(2 * P).rearrange("p (a o) -> p a o", a=2)
        slope = view(4 * HEADS, SEQ).rearrange("p (a h) -> p a h", a=4)
        view, at = region(STAGE + 2 * W0, LOADED)
        decay = view(HEADS * SEQ, SEQ).rearrange("p (h k) -> p h k", h=HEADS)
        headsT = view(2 * TOKENS).rearrange("p (a t b) -> p a t b", a=2, b=BATCH)
        xb = view(2 * SEQ).rearrange("p (u n) -> p u n", u=2)
        qk = view(2 * 4 * SEQ).rearrange("p (u w n) -> p u w n", u=2, w=4)
        vb = view(ROUND * 2 * P, SEQ).rearrange("p (u n) -> p u n", u=ROUND)
        att = view(ROUND * HEADS * SEQ, SEQ).rearrange("p (u h k) -> p u h k", u=ROUND, h=HEADS)
        attT = view(2 * HALF * SEQ, SEQ).rearrange("p (a j k) -> p a j k", a=2, j=HALF)
        smax = view(ROUND * HEADS, SEQ).rearrange("p (u h) -> p u h", u=ROUND)
        ssum = view(ROUND * HEADS, SEQ).rearrange("p (u h) -> p u h", u=ROUND)
        srec = view(ROUND * HEADS, SEQ).rearrange("p (u h) -> p u h", u=ROUND)

        view, at = region(STAGE)
        w_raw = view(2 * W0).rearrange("p (u n) -> p u n", u=2)
        assert at[0] <= STAGE + SHIFTS * RCH * D
        share = view(2 * TOKENS).rearrange("p (u n) -> p u n", u=2)
        xe = view(2 * BLK).rearrange("p (u n) -> p u n", u=2)
        silu = view(2 * BLK).rearrange("p (u n) -> p u n", u=2)
        hid = view(2 * BLK).rearrange("p (u n) -> p u n", u=2)
        n_soft = TILES * (1 + GROUPS)
        route_w = view(20)
        route_b = view(20, SEQ)
        route_at = at[0]
        prob = view(n_soft * 4, SEQ).rearrange("p (n k) -> p n k", k=4)
        rank = view(n_soft * 4, SEQ).rearrange("p (n k) -> p n k", k=4)
        pick = view(n_soft * 4, SEQ).rearrange("p (n k) -> p n k", k=4)
        beat = view(n_soft * 6, SEQ).rearrange("p (a n) -> p a n", a=6)
        top = view(n_soft * 3, SEQ).rearrange("p (a n) -> p a n", a=3)
        weight = view(TILES * E0, SEQ).rearrange("p (t g e) -> p t g e", t=TILES, g=GROUPS)
        shareT = view(TOKENS, E0)
        REC_AT = at[0]
        rec_w = view(7 * 2 * GP // 2).bitcast(F16).rearrange("p (w s n) -> p w s n", w=7, s=2)
        rec_raw = area[:, route_at:route_at + GP]
        assert route_at + GP <= REC_AT

        view, at = region(STAGE, REC_AT)
        xpair = view(SEQ * 2 * BATCH // 2).bitcast(F16).rearrange("p (t g b) -> p t g b", t=SEQ, g=2)
        hist = view(KH * TOKENS).rearrange("p (t n) -> p t n", t=SEQ)
        xcur = view(2 * 2 * BATCH // 2).bitcast(F16).rearrange("p (u g b) -> p u g b", u=2, g=2)
        hpair = view(4 * KH * 2 * BATCH // 2).bitcast(F16).rearrange(
            "p (l u k g b) -> p l u k g b", l=2, u=2, k=KH, g=2)
        pre = view(2 * GW).rearrange("p (l n) -> p l n", l=2)
        gates = view(2 * 7 * SW).rearrange("p (l n) -> p l n", l=2)
        prod = view(2 * 2 * SW).rearrange("p (l n) -> p l n", l=2)
        tanh_c = view(2 * SW).rearrange("p (l n) -> p l n", l=2)
        out_h = view(2 * SW).rearrange("p (l n) -> p l n", l=2)
        hfull = view(2 * 2 * SW).rearrange("p (l u n) -> p l u n", l=2, u=2)
        bias_raw = view(2 * P).rearrange("p (l n) -> p l n", l=2)
        bias_cast = view(2 * 3 * P // 2).bitcast(BF16).rearrange("p (l s n) -> p l s n", l=2, s=3)
        bias_part = view(2 * P // 2).bitcast(BF16).rearrange("p (l n) -> p l n", l=2)
        bias_sel = view(GW // 2).bitcast(BF16)
        fc_w = view(KH * D).rearrange("p (k n) -> p k n", k=KH)
        f_raw = view(2 * F0).rearrange("p (u n) -> p u n", u=2)
        fb2 = view(D, E1)
        fg_w = view(E1)
        fg_b = view(E1, SEQ)
        view, at = region(REC_AT)
        fc_sb = view(2 * BLK).rearrange("p (u n) -> p u n", u=2)
        logit = view(TILES * E1, SEQ).rearrange("p (t e) -> p t e", t=TILES)
        chosen = view(TILES * E1, SEQ).rearrange("p (t e) -> p t e", t=TILES)
        best = view(2 * TILES, SEQ).rearrange("p (a t) -> p a t", a=2)
        mask_T = view(TOKENS, E1)
        relu = view(2 * BLK).rearrange("p (u n) -> p u n", u=2)
        fhid = view(2 * BLK).rearrange("p (u n) -> p u n", u=2)
        f_bias = view(2 * C1).rearrange("p (u n) -> p u n", u=2)
        mask_b = view(2 * TOKENS).rearrange("p (u n) -> p u n", u=2)

        def col(i):
            return cols[:, i:i + 1]

        def blk(t, j):
            return t[:, j * BLK:(j + 1) * BLK]

        def split3(eng, acc, aH, aL, bH, bL, start, stop):
            eng.matmul(acc, aH, bH, start=start, stop=False, skip_group_check=True)
            eng.matmul(acc, aH, bL, start=False, stop=False, skip_group_check=True)
            return eng.matmul(acc, aL, bH, start=False, stop=stop, skip_group_check=True)

        STAGES = {"tok": 1, "ln1": 2, "ln2": 3, "ln3": 4, "ln4": 5}
        NORM = {"tok": 0, "ln1": 2, "ln2": 2 + NBLK, "ln3": 2 + 2 * NBLK, "ln4": 2 + 3 * NBLK}

        def normed(eng, tag, blocks=NBLK):
            eng.wait_ge(sg("normed"), NORM[tag] + blocks)

        def norm_pe(pe, tag, src, banks, wait):
            n = len(src)
            for j in range(n):
                wait(pe, j)
                pe.matmul(banks[j][:, 0:src[j].shape[1]], mean_mat[:, :], src[j], start=True, stop=True
                          ).then_inc(sg("mean"), 1)
            for j in range(n):
                pe.wait_ge(sg("squared"), NORM[tag] + j + 1)
                pe.matmul(banks[n][32 * j:32 * j + 32, 0:src[j].shape[1]], mean_mat[:, 0:32],
                          sq[:, j, 0:src[j].shape[1]], start=True, stop=True).then_inc(sg("variance"), 1)
            pe.wait_ge(sg("spread_row"), 1 + NBLK)
            pe.wait_ge(sg("inverted"), STAGES[tag])
            for j in range(n):
                part = slice(32 * j, 32 * j + 32)
                pe.matmul(banks[j][:, 0:src[j].shape[1]], spread_row[part, :], sq[part, 0, 0:src[j].shape[1]],
                          start=True, stop=True).then_inc(sg("scale_ps"), 1)

        def norm_act(act, tag, dst, banks, e):
            n = len(dst)
            for j in range(n):
                act.wait_ge(sg("centred"), NORM[tag] + j + 1)
                act.activation(sq[:, j, 0:dst[j].shape[1]], dst[j], ACT.Square).then_inc(sg("squared"), 1)
            act.wait_ge(sg("variance"), NORM[tag] + n)
            act.activation(sq[0:32 * n, 0, 0:dst[0].shape[1]], banks[n][0:32 * n, 0:dst[0].shape[1]], ACT.Sqrt,
                           bias=eps[0:32 * n, e:e + 1]).then_inc(sg("deviation"), 1)

        def norm_dve(dve, tag, src, dst, banks):
            n = len(dst)
            for j in range(n):
                dve.wait_ge(sg("mean"), NORM[tag] + j + 1)
                dve.tensor_tensor(dst[j], src[j], banks[j][:, 0:src[j].shape[1]], ALU.subtract
                                  ).then_inc(sg("centred"), 1)
            r = sq[0:32 * n, 0, 0:dst[0].shape[1]]
            dve.wait_ge(sg("deviation"), STAGES[tag])
            dve.reciprocal(r, r).then_inc(sg("inverted"), 1)
            for j in range(n):
                dve.wait_ge(sg("scale_ps"), NORM[tag] + j + 1)
                dve.tensor_tensor(dst[j], dst[j], banks[j][:, 0:src[j].shape[1]], ALU.mult).then_inc(sg("normed"), 1)

        xn_blocks = [blk(xn, j) for j in range(NBLK)]
        st_blocks = [blk(stream, j) for j in range(NBLK)]

        conv_blocks = [conv[:, j * EBLK:(j + 1) * EBLK] for j in range(2)]
        emb_blocks = [emb[:, j * EBLK:(j + 1) * EBLK] for j in range(2)]

        def tok_sp(sp):
            sp.dma_start(taps, taps_in).then_inc(sg("taps_in"), 16)
            for j in range(2):
                sp.dma_start(patches[:, :, j * EBLK:(j + 1) * EBLK], patches_in[:, :, j * EBLK:(j + 1) * EBLK]
                             ).then_inc(sg(f"patches_in{j}"), 16)
            sp.dma_start(cols[:, :], cols_in).then_inc(sg("cols_in"), 16)
            sp.dma_start(dense_w, dense_in).then_inc(sg("dense_in"), 16)
            sp.dma_start(stream[:, EMB:TOKENS], txt_in).then_inc(sg("words_in"), 16)
            sp.dma_start(const[:, :], const_in).then_inc(sg("const_in"), 16)
            sp.dma_start(qkv_w, qkvw_in).then_inc(sg("att_w_in"), 16)
            sp.dma_start(out_w, outw_in).then_inc(sg("att_w_in"), 16)
            sp.dma_start(slope[:, 0, :], heads_in.broadcast_to([SEQ, HEADS])).then_inc(sg("slope_in"), 16)

        def tok_pool(pool):
            pool.memset(mean_mat[:, :], 1.0 / D).then_inc(sg("mean_mat"), 1)
            pool.memset(eps[:, 0:1], 1e-3).then_inc(sg("eps"), 1)
            pool.memset(eps[:, 1:2], 1e-5).then_inc(sg("eps"), 1)
            pool.memset(spread_row[:, :], 0.0).then_inc(sg("spread_row"), 1)
            pool.memset(one[:, :], 1.0).then_inc(sg("ones"), 1)
            pool.memset(warm[:, :], 0.0).then_inc(sg("warm"), 1)

        def tok_pe(pe):
            pe.wait_ge(sg("taps_sum"), SHIFTS - 1)
            for j in range(2):
                pe.wait_ge(sg(f"patches_in{j}"), 16)
                for k in range(RCH):
                    mm = pe.matmul(bank[j][:, 0:EBLK], taps[:, 0, k, :], patches[:, k, j * EBLK:(j + 1) * EBLK],
                                   start=(k == 0), stop=(k == RCH - 1))
                mm.then_inc(sg("conv"), 1)
            pe.wait_ge(sg("mean_mat"), 1)
            norm_pe(pe, "tok", conv_blocks, bank[2:6], lambda e, j: e.wait_ge(sg("conv_sb"), j + 1))
            pe.wait_ge(sg("dense_in"), 16)
            for j in range(2):
                pe.wait_ge(sg("emb"), j + 1)
                pe.matmul(bank[6 + j][:, 0:EBLK], dense_w, emb_blocks[j], start=True, stop=True
                          ).then_inc(sg("dense"), 1)

        def tok_act(act):
            act.wait_ge(sg("eps"), 2)
            norm_act(act, "tok", emb_blocks, bank[2:6], 0)

        def tok_dve(dve):
            dve.wait_ge(sg("spread_row"), 1)
            for j in range(NBLK):
                dve.memset(spread_row[32 * j:32 * j + 1, :], 1.0).then_inc(sg("spread_row"), 1)
            dve.wait_ge(sg("taps_in"), 16)
            for s in range(1, SHIFTS):
                reach(dve, "taps_sum", s - 1)
                dve.tensor_tensor(taps[:, 0], taps[:, 0], taps[:, s], ALU.add).then_inc(sg("taps_sum"), 1)
            dve.wait_ge(sg("cols_in"), 16)
            for j in range(2):
                dve.wait_ge(sg("conv"), j + 1)
                dve.tensor_scalar(conv_blocks[j], bank[j][:, 0:EBLK], col(CONV_B), None, ALU.add
                                  ).then_inc(sg("conv_sb"), 1)
            dve.wait_ge(sg("conv_sb"), 2)
            norm_dve(dve, "tok", conv_blocks, emb_blocks, bank[2:6])
            for j in range(2):
                normed(dve, "tok", j + 1)
                dve.tensor_scalar(emb_blocks[j], emb_blocks[j], col(GAMMA), col(BETA), ALU.mult, ALU.add
                                  ).then_inc(sg("emb"), 1)
            for j in range(2):
                dve.wait_ge(sg("dense"), j + 1)
                dve.tensor_scalar(stream[:, j * EBLK:(j + 1) * EBLK], bank[6 + j][:, 0:EBLK], col(DENSE_B), None,
                                  ALU.add).then_inc(sg("embedded"), 1)

        xn_images = xn[:, :].rearrange("p (t b) -> p t b", b=BATCH)

        def here(m, first, last):
            return not isinstance(m, int) or first <= m <= last

        def at_image(t, b):
            return t[:, :, b] if isinstance(b, int) else t[:, :, bass.ds(b, 1)].rearrange("p t b -> p (t b)")

        def each_step(eng, body):
            for m in range(ROUND):
                body(m, m)
            with eng.Fori(1, BATCH // ROUND - 1) as i:
                for u in range(ROUND):
                    body(i * ROUND + u, u)
            for m in range(BATCH - ROUND, BATCH + 3):
                body(m, m % ROUND)

        def per_head(t, heads):
            return t.rearrange("p (h z) -> p h z", z=1).broadcast_to([SEQ, heads, SEQ])

        def att_pool(pool):
            normed(pool, "ln1")

            def gather(m, u):
                if here(m, 2, BATCH):
                    pool.wait_ge(sg("qk_ps"), m - 1)
                settle(pool)
                pool.tensor_copy(xb[:, u % 2, :], at_image(xn_images, m)).then_inc(sg("xb"), 1)

            gather(0, 0)

            def step(m, u):
                if here(m, 0, BATCH - 2):
                    gather(m + 1, u + 1)
                if here(m, 1, BATCH):
                    v = (u - 1) % ROUND
                    pool.wait_ge(sg("smax"), m)
                    pool.tensor_tensor(att[:, v], att[:, v], per_head(smax[:, v, :], HEADS), ALU.subtract
                                       ).then_inc(sg("shifted"), 1)
                if here(m, 2, BATCH + 1):
                    v = (u - 2) % ROUND
                    pool.wait_ge(sg("srec"), m - 1)
                    pool.tensor_tensor(att[:, v, 0:HALF], att[:, v, 0:HALF], per_head(srec[:, v, 0:HALF], HALF),
                                       ALU.mult).then_inc(sg("soft0"), 1)
            each_step(pool, step)

        def att_pe(pe):
            norm_pe(pe, "ln1", st_blocks, bank, lambda e, j: (e.wait_ge(sg("embedded"), 2),
                                                             e.wait_ge(sg("words_in"), 16)))
            pe.wait_ge(sg("att_w_in"), 32)
            pe.wait_ge(sg("const_in"), 16)
            normed(pe, "ln1")

            def step(m, u):
                project, weigh = here(m, 0, BATCH - 1), here(m, 3, BATCH + 2)
                w = (u - 3) % ROUND
                if here(m, 1, BATCH):
                    pe.wait_ge(sg("qk"), m)
                    pe.wait_ge(sg("vb"), m)
                    if here(m, 2, BATCH):
                        pe.wait_ge(sg("scaled"), m - 1)
                    for h in range(HEADS):
                        a, j = divmod(h, HALF)
                        rows = slice(PAD * j, PAD * (j + 1))
                        mm = pe.matmul(quad[0:SEQ, j, a * SEQ:(a + 1) * SEQ], qk[rows, (u - 1) % 2, a, :],
                                       qk[rows, (u - 1) % 2, 2 + a, :], start=True, stop=True)
                    mm.then_inc(sg("scores"), 1)
                if project:
                    pe.wait_ge(sg("xb"), m + 1)
                    pe.matmul(quad[0:SEQ, 0, 2 * SEQ:2 * SEQ + 2 * P], xb[:, u % 2, :], qkv_w[:, 4:6, :],
                              start=True, stop=True).then_inc(sg("values"), 1)
                if weigh:
                    pe.wait_ge(sg("soft0"), m - 2)
                    pe.wait_ge(sg("soft1"), m - 2)
                    for a in range(2):
                        if here(m, 4, BATCH + 2):
                            pe.wait_ge(sg(f"attT{a}"), m - 3)
                        for j in range(HALF):
                            mm = pe.transpose(bank[2 + a][0:SEQ, j * SEQ:(j + 1) * SEQ],
                                              att[:, w, 2 * j + a, :], ident[0:SEQ, 0:SEQ])
                        mm.then_inc(sg(f"attT_ps{a}"), 1)
                if project:
                    for i in range(4):
                        mm = pe.matmul(bank[0][:, i * SEQ:(i + 1) * SEQ], qkv_w[:, i, :], xb[:, u % 2, :],
                                       start=True, stop=True)
                    mm.then_inc(sg("qk_ps"), 1)
                if weigh:
                    if here(m, 4, BATCH + 2):
                        pe.wait_ge(sg("heads"), m - 3)
                    for a in range(2):
                        pe.wait_ge(sg(f"attT{a}"), m - 2)
                        for j in range(HALF):
                            h = a * HALF + j
                            mm = pe.matmul(bank[1][PAD * j:PAD * (j + 1), a * SEQ:(a + 1) * SEQ],
                                           vb[:, w, PAD * h:PAD * (h + 1)], attT[:, a, j, :], start=True, stop=True)
                    mm.then_inc(sg("heads_ps"), 1)
            each_step(pe, step)
            for j in range(NBLK):
                pe.wait_ge(sg("heads"), BATCH)
                for a in range(2):
                    mm = pe.matmul(bank[2 + j][:, 0:BLK], out_w[:, a, :],
                                   blk(headsT[:, a].rearrange("p t b -> p (t b)"), j),
                                   start=(a == 0), stop=(a == 1))
                mm.then_inc(sg("projected"), 1)

        def att_act(act):
            norm_act(act, "ln1", xn_blocks, bank, 1)
            act.wait_ge(sg("warm"), 1)
            act.activation(warm[:, :], warm[:, :], ACT.Exp)

            def step(m, u):
                if here(m, 2, BATCH + 1):
                    v = (u - 2) % ROUND
                    act.wait_ge(sg("shifted"), m - 1)
                    act.activation(att[:, v].rearrange("p h k -> p (h k)"), att[:, v].rearrange("p h k -> p (h k)"),
                                   ACT.Exp).then_inc(sg("expd"), 1)
                if here(m, 3, BATCH + 2):
                    for a in range(2):
                        act.wait_ge(sg(f"attT_ps{a}"), m - 2)
                        if here(m, 4, BATCH + 2):
                            act.wait_ge(sg("heads_ps"), m - 3)
                        act.activation(attT[:, a].rearrange("p j k -> p (j k)"), bank[2 + a][0:SEQ, 0:HALF * SEQ],
                                       ACT.Copy).then_inc(sg(f"attT{a}"), 1)
                if here(m, 0, BATCH - 1):
                    act.wait_ge(sg("qk_ps"), m + 1)
                    if here(m, 2, BATCH):
                        act.wait_ge(sg("scores"), m - 1)
                    for w in range(4):
                        ins = act.activation(qk[:, u % 2, w, :], bank[0][:, w * SEQ:(w + 1) * SEQ], ACT.Identity,
                                             bias=col(QKV_B + w))
                    ins.then_inc(sg("qk"), 1)
                if here(m, 3, BATCH + 2):
                    act.wait_ge(sg("heads_ps"), m - 2)
                    settle(act)
                    for a in range(2):
                        ins = act.activation(at_image(headsT[:, a], m - 3), bank[1][:, a * SEQ:(a + 1) * SEQ],
                                             ACT.Identity, bias=col(QKV_B + 4 + a))
                    ins.then_inc(sg("heads"), 1)
            each_step(act, step)

        def att_dve(dve):
            dve.wait_ge(sg("slope_in"), 16)
            dve.tensor_tensor(slope[:, 1, :], slope[:, 0, :], slope[:, 0, :], ALU.mult).then_inc(sg("slope"), 1)
            dve.wait_ge(sg("slope"), 1)
            dve.tensor_tensor(slope[:, 2, :], slope[:, 1, :], slope[:, 1, :], ALU.mult).then_inc(sg("slope"), 1)
            dve.wait_ge(sg("slope"), 2)
            dve.tensor_scalar(slope[:, 2, :], slope[:, 2, :], 2.0, None, ALU.mult).then_inc(sg("slope"), 1)
            dve.wait_ge(sg("slope"), 3)
            dve.reciprocal(slope[:, 3, :], slope[:, 2, :]).then_inc(sg("slope"), 1)
            dve.wait_ge(sg("slope"), 4)
            dve.wait_ge(sg("const_in"), 16)
            for h in range(HEADS):
                ins = dve.tensor_scalar(decay[:, h % HALF * 2 + h // HALF, :], const[0:SEQ, C_DIST:C_DIST + SEQ], slope[:, 3, h:h + 1], None,
                                        ALU.mult)
            ins.then_inc(sg("decay"), 1)
            norm_dve(dve, "ln1", st_blocks, xn_blocks, bank)
            dve.wait_ge(sg("decay"), 1)

            def step(m, u):
                if here(m, 4, BATCH + 2):
                    dve.wait_ge(sg("heads_ps"), m - 3)
                if here(m, 1, BATCH):
                    v = (u - 1) % ROUND
                    dve.wait_ge(sg("scores"), m)
                    if here(m, 0, BATCH - 1):
                        dve.wait_ge(sg("values"), m + 1)
                    dve.scalar_tensor_tensor(out=att[:, v].rearrange("p (j a) k -> p j (a k)", a=2),
                                             in0=quad[0:SEQ, :, 0:2 * SEQ], scalar=0.25,
                                             in1=decay.rearrange("p (j a) k -> p j (a k)", a=2),
                                             op0=ALU.mult, op1=ALU.add).then_inc(sg("scaled"), 1)
                    dve.wait_ge(sg("scaled"), m)
                    dve.tensor_reduce(smax[:, v, :], att[:, v], AX, ALU.max).then_inc(sg("smax"), 1)
                if here(m, 0, BATCH - 1):
                    dve.wait_ge(sg("values"), m + 1)
                    dve.tensor_copy(vb[:, u, :], quad[0:SEQ, 0, 2 * SEQ:2 * SEQ + 2 * P]).then_inc(sg("vb"), 1)
                if here(m, 2, BATCH + 1):
                    v = (u - 2) % ROUND
                    dve.wait_ge(sg("expd"), m - 1)
                    dve.tensor_reduce(ssum[:, v, :], att[:, v], AX, ALU.add).then_inc(sg("ssum"), 1)
                    dve.wait_ge(sg("ssum"), m - 1)
                    dve.reciprocal(srec[:, v, :], ssum[:, v, :]).then_inc(sg("srec"), 1)
                    dve.wait_ge(sg("srec"), m - 1)
                    dve.tensor_tensor(att[:, v, HALF:], att[:, v, HALF:], per_head(srec[:, v, HALF:], HALF),
                                      ALU.mult).then_inc(sg("soft1"), 1)
            each_step(dve, step)
            for j in range(NBLK):
                dve.wait_ge(sg("projected"), j + 1)
                dve.scalar_tensor_tensor(out=st_blocks[j], in0=bank[2 + j][:, 0:BLK], scalar=col(OUT_B),
                                         in1=st_blocks[j], op0=ALU.add, op1=ALU.add).then_inc(sg("attended"), 1)

        ITEMS0 = NBLK * C0

        def experts(body):
            def run(eng, count):
                body(0, 0, 0)
                with eng.Fori(0, count // 2 - 1) as i:
                    body(i * 2 + 1, 1, i)
                    body(i * 2 + 2, 0, i + 1)
                body(count - 1, 1, count // 2 - 1)
            return run

        def split_x(tag, before):
            def on_act(act):
                for j in range(NBLK):
                    normed(act, tag, j + 1)
                    act.activation(blk(xnH, j), xn_blocks[j], ACT.Copy).then_inc(sg("x_high"), 1)

            def on_dve(dve):
                for j in range(NBLK):
                    dve.wait_ge(sg("x_high"), before + j + 1)
                    dve.tensor_tensor(blk(xnL, j), xn_blocks[j], blk(xnH, j).bitcast(F32), ALU.subtract
                                      ).then_inc(sg("x_low"), 1)
            return on_act, on_dve

        ln2_high, ln2_low = split_x("ln2", 0)

        def ffn_sp(sp):
            sp.wait_ge(sg("conv"), 2)
            for u in range(2):
                sp.dma_start(w_raw[:, u, :], w0_in[u]).then_inc(sg(f"w_in{u}"), 16)
            sp.wait_ge(sg("attended"), NBLK)
            sp.dma_start(route_w, route_in).then_inc(sg("route_in"), 16)
            sp.dma_start(route_b, routeb_in.broadcast_to([SEQ, 20])).then_inc(sg("route_in"), 16)
            sp.wait_ge(sg("shareT"), 4)
            sp.dma_start(share_dram, shareT).then_inc(sg("share_out"), 16)
            sp.wait_ge(sg("share_out"), 16)
            for u in range(2):
                sp.dma_start(share[:, u, :], share_dram[u:u + 1, :].broadcast_to([P, TOKENS])
                             ).then_inc(sg(f"share_in{u}"), 16)
            with sp.Fori(1, E0 // 2) as i:
                for u in range(2):
                    e = i * 2 + u
                    sp.wait_ge(sg("w_low"), (e - 1) * 3)
                    sp.dma_start(w_raw[:, u, :], w0_in[bass.ds(e, 1)].rearrange("e p n -> (e p) n")
                                 ).then_inc(sg(f"w_in{u}"), 16)
                    sp.wait_ge(sg("xe"), (e - 1) * NBLK)
                    sp.dma_start(share[:, u, :], share_dram[bass.ds(e, 1), :].broadcast_to([P, TOKENS])
                                 ).then_inc(sg(f"share_in{u}"), 16)

        def xe_low(pool, g, b):
            pool.wait_ge(sg("xe_high"), g + 1)
            pool.tensor_tensor(xeL[:, b, :], xe[:, b, :], xeH[:, b, :].bitcast(F32), ALU.subtract
                               ).then_inc(sg("xe_low"), 1)

        def w_split(pool, e, u, half, piece):
            part = slice(piece * H0, (piece + 1) * H0)
            if piece == 0:
                pool.wait_ge(sg(f"w_in{u}"), half * 16 + 16)
                if not isinstance(e, int) or e >= 2:
                    pool.wait_ge(sg("down"), (e - 1) * ITEMS0)
                settle(pool)
            pool.tensor_tensor(wH[:, u, part], w_raw[:, u, part], one[:, :].broadcast_to([P, H0]), ALU.mult
                               ).then_inc(sg("w_high"), 1)
            pool.wait_ge(sg("w_high"), e * 3 + piece + 1)
            pool.tensor_tensor(wL[:, u, part], w_raw[:, u, part], wH[:, u, part].bitcast(F32), ALU.subtract
                               ).then_inc(sg("w_low"), 1)

        def rec_sub(pool, w):
            pool.wait_ge(sg("rec_part"), w + 1)
            part = rec_w[:, bass.ds(w, 1), 0, :].rearrange("p w n -> p (w n)")
            pool.tensor_tensor(rec_raw, rec_raw, part, ALU.subtract).then_inc(sg("rec_rest"), 1)

        def ffn_pool(pool):
            pool.wait_ge(sg("ones"), 1)
            for e in range(2):
                for piece in range(3):
                    w_split(pool, e, e, 0, piece)
            xe_low(pool, 0, 0)

            def expert(e, u, half):
                last = isinstance(e, int) and e == E0 - 1
                ahead = not isinstance(e, int)
                for j in range(NBLK):
                    if not (last and j == NBLK - 1):
                        xe_low(pool, e * NBLK + j + 1, (j + 1) % 2)
                    if j < 3 and ahead:
                        w_split(pool, e + 1, 1 - u, half + u, j)
                    if ahead and u == 1 and j == 0:
                        pool.wait_ge(sg("shareT"), 4)
                        pool.wait_ge(sg("rec_free"), half + 1)
                        pool.dma_start(rec_raw, rec_in[bass.ds(half, 1)].rearrange("w p n -> (w p) n")
                                       ).then_inc(sg("rec_in"), 16)
                    if ahead and u == 1 and j == 3:
                        rec_sub(pool, half)
            experts(expert)(pool, E0)

        def ffn_pe(pe):
            norm_pe(pe, "ln2", st_blocks, bank, lambda e, j: e.wait_ge(sg("attended"), j + 1))
            normed(pe, "ln2")
            pe.wait_ge(sg("route_in"), 32)
            for t in range(TILES):
                mm = pe.matmul(bank[0][0:SEQ, t * 20:(t + 1) * 20], xn[:, t * SEQ:(t + 1) * SEQ], route_w,
                               start=True, stop=True)
            mm.then_inc(sg("logits"), 1)
            pe.wait_ge(sg("weights"), GROUPS)
            for t in range(TILES):
                mm = pe.transpose(bank[t // 4][0:E0, t % 4 * SEQ:(t % 4 + 1) * SEQ],
                                  weight[:, t].rearrange("p g e -> p (g e)"), ident[0:SEQ, 0:SEQ])
                if t % 4 == 3:
                    mm.then_inc(sg("shareT_ps"), 1)
            pe.wait_ge(sg("shareT"), 4)

            def down(n, k, u, first):
                j, c = divmod(k, C0)
                w = 2 * H0 + c * P
                pe.wait_ge(sg("hid_low"), n + 1)
                split3(pe, bank[j][:, 0:BLK], wH[:, u, w:w + P], wL[:, u, w:w + P], hidH[:, k % 4, :],
                       hidL[:, k % 4, :], start=(first and c == 0), stop=False).then_inc(sg("down"), 1)

            def expert(e, u, half):
                first = isinstance(e, int) and e == 0
                for k in range(ITEMS0):
                    j, c = divmod(k, C0)
                    n = e * ITEMS0 + k
                    if k == 0:
                        pe.wait_ge(sg("w_low"), e * 3 + 3)
                    if first and c == 0:
                        pe.wait_ge(sg("x_low"), j + 1)
                    if not (first and k < 2):
                        pe.wait_ge(sg("silu"), n - 1)
                        pe.wait_ge(sg("gated"), n - 1)
                    w = c * P
                    split3(pe, bank[4 + k % 2][:, 0:BLK], wH[:, u, w:w + P], wL[:, u, w:w + P], blk(xnH, j),
                           blk(xnL, j), start=True, stop=True).then_inc(sg("gate_ps"), 1)
                    if c == 0:
                        pe.wait_ge(sg("xe_low"), e * NBLK + j + 1)
                    w = H0 + c * P
                    split3(pe, bank[6 + k % 2][:, 0:BLK], wH[:, u, w:w + P], wL[:, u, w:w + P], xeH[:, j % 2, :],
                           xeL[:, j % 2, :], start=True, stop=True).then_inc(sg("up_ps"), 1)
                    if k >= LAG:
                        down(n - LAG, k - LAG, u, first)
                    elif not first:
                        down(n - LAG, k - LAG + ITEMS0, 1 - u, isinstance(e, int) and e == 1)
            experts(expert)(pe, E0)
            for k in range(ITEMS0 - LAG, ITEMS0):
                down((E0 - 1) * ITEMS0 + k, k, 1, False)

        def xe_high(act, g, b):
            act.wait_ge(sg("xe"), g + 1)
            if not isinstance(g, int) or g >= 2:
                act.wait_ge(sg("up_ps"), (g - 1) * C0)
            act.activation(xeH[:, b, :], xe[:, b, :], ACT.Copy).then_inc(sg("xe_high"), 1)

        def ffn_act(act):
            norm_act(act, "ln2", xn_blocks, bank, 1)
            ln2_high(act)
            act.wait_ge(sg("routing"), 3)
            act.activation(prob.rearrange("p n k -> p (n k)"), prob.rearrange("p n k -> p (n k)"), ACT.Exp
                           ).then_inc(sg("route_exp"), 1)
            for j in range(4):
                act.wait_ge(sg("shareT_ps"), j + 1)
                act.activation(blk(shareT, j), bank[j][0:E0, 0:BLK], ACT.Copy).then_inc(sg("shareT"), 1)
            act.activation(warm[:, :], warm[:, :], ACT.Silu).then_inc(sg("rec_free"), 1)
            xe_high(act, 0, 0)

            def high(n, k):
                act.wait_ge(sg("gated"), n + 1)
                if not isinstance(n, int) or n >= 4:
                    act.wait_ge(sg("down"), n - 3)
                act.activation(hidH[:, k % 4, :], hid[:, k % 2, :], ACT.Copy).then_inc(sg("hid_high"), 1)

            def rec_cast(w, s):
                if s == 0:
                    act.wait_ge(sg("rec_in"), w * 16 + 16)
                    act.activation(rec_raw, rec_raw, ACT.Copy, scale=W_SCALE).then_inc(sg("rec_scaled"), 1)
                    act.wait_ge(sg("rec_scaled"), w + 1)
                else:
                    act.wait_ge(sg("rec_rest"), w + 1)
                settle(act)
                act.activation(rec_w[:, bass.ds(w, 1), s, :].rearrange("p w n -> p (w n)"), rec_raw, ACT.Copy
                               ).then_inc(sg("rec_free" if s == 1 else "rec_part"), 1)

            def expert(e, u, half):
                first = isinstance(e, int) and e == 0
                last = isinstance(e, int) and e == E0 - 1
                for k in range(ITEMS0):
                    n = e * ITEMS0 + k
                    act.wait_ge(sg("gate_ps"), n + 1)
                    if not (first and k < 2):
                        act.wait_ge(sg("gated"), n - 1)
                    act.activation(silu[:, k % 2, :], bank[4 + k % 2][:, 0:BLK], ACT.Silu).then_inc(sg("silu"), 1)
                    if not (first and k == 0):
                        high(n - 1, (k - 1) % ITEMS0)
                    if k % C0 == 1 and not (last and k > 3 * C0):
                        xe_high(act, e * NBLK + k // C0 + 1, (k // C0 + 1) % 2)
                    if not isinstance(e, int):
                        if u == 1 and k == 8:
                            rec_cast(half, 0)
                        if u == 0 and k == 2:
                            rec_cast(half - 1, 1)
            experts(expert)(act, E0)
            high(E0 * ITEMS0 - 1, ITEMS0 - 1)

        def route(dve):
            steps = [0]

            def link(ins):
                steps[0] += 1
                ins.then_inc(sg("routing"), 1)
                dve.wait_ge(sg("routing"), steps[0])

            def spread(v):
                return v.rearrange("p (n z) -> p n z", z=1).broadcast_to([SEQ, n_soft, 4])

            dve.wait_ge(sg("route_in"), 32)
            dve.wait_ge(sg("logits"), 1)
            link(dve.tensor_tensor(prob.rearrange("p (t i) k -> p t (i k)", t=TILES),
                                   bank[0][0:SEQ, 0:TILES * 20].rearrange("p (t i) -> p t i", t=TILES),
                                   route_b.rearrange("p (z i) -> p z i", z=1).broadcast_to([SEQ, TILES, 20]),
                                   ALU.add))
            link(dve.tensor_reduce(top[:, 0, :], prob, AX, ALU.max))
            link(dve.tensor_tensor(prob, prob, spread(top[:, 0, :]), ALU.subtract))
            dve.wait_ge(sg("route_exp"), 1)
            link(dve.tensor_reduce(top[:, 0, :], prob, AX, ALU.add))
            link(dve.reciprocal(top[:, 1, :], top[:, 0, :]))
            link(dve.tensor_tensor(prob, prob, spread(top[:, 1, :]), ALU.mult))
            pair = {}
            for i in range(4):
                for j in range(i + 1, 4):
                    b = pair[i, j] = beat[:, len(pair), :]
                    ins = dve.tensor_tensor(b, prob[:, :, j], prob[:, :, i], ALU.is_gt)
            link(ins)
            r = [rank[:, :, i] for i in range(4)]
            dve.tensor_tensor(r[0], pair[0, 1], pair[0, 2], ALU.add)
            dve.scalar_tensor_tensor(out=r[1], in0=pair[0, 1], scalar=-1.0, in1=pair[1, 2], op0=ALU.mult, op1=ALU.add)
            dve.tensor_tensor(r[2], pair[0, 2], pair[1, 2], ALU.add)
            link(dve.tensor_tensor(r[3], pair[0, 3], pair[1, 3], ALU.add))
            dve.tensor_tensor(r[0], r[0], pair[0, 3], ALU.add)
            dve.scalar_tensor_tensor(out=r[1], in0=r[1], scalar=1.0, in1=pair[1, 3], op0=ALU.add, op1=ALU.add)
            dve.scalar_tensor_tensor(out=r[2], in0=r[2], scalar=-1.0, in1=pair[2, 3], op0=ALU.mult, op1=ALU.add)
            link(dve.scalar_tensor_tensor(out=r[3], in0=r[3], scalar=-1.0, in1=pair[2, 3], op0=ALU.mult,
                                          op1=ALU.subtract))
            dve.tensor_scalar(r[2], r[2], 2.0, None, ALU.add)
            link(dve.tensor_scalar(r[3], r[3], 3.0, None, ALU.add))
            second = beat[:, 0:4, :].rearrange("p a n -> p (a n)").rearrange("p (n k) -> p n k", k=4)
            dve.scalar_tensor_tensor(out=pick, in0=rank, scalar=0.0, in1=prob, op0=ALU.is_equal, op1=ALU.mult)
            link(dve.scalar_tensor_tensor(out=second, in0=rank, scalar=1.0, in1=prob, op0=ALU.is_equal,
                                          op1=ALU.mult))
            dve.tensor_reduce(top[:, 0, :], pick, AX, ALU.add)
            link(dve.tensor_reduce(top[:, 1, :], second, AX, ALU.add))
            link(dve.tensor_tensor(top[:, 2, :], top[:, 0, :], top[:, 1, :], ALU.add))
            link(dve.tensor_scalar(top[:, 2, :], top[:, 2, :], 0.9, None, ALU.is_le))
            dve.tensor_tensor(top[:, 1, :], top[:, 1, :], top[:, 2, :], ALU.mult)
            link(dve.tensor_tensor(second, second, spread(top[:, 2, :]), ALU.mult))
            dve.tensor_tensor(pick, pick, second, ALU.add)
            link(dve.scalar_tensor_tensor(out=top[:, 0, :], in0=top[:, 0, :], scalar=1e-9, in1=top[:, 1, :],
                                          op0=ALU.add, op1=ALU.add))
            link(dve.reciprocal(top[:, 1, :], top[:, 0, :]))
            link(dve.tensor_tensor(pick, pick, spread(top[:, 1, :]), ALU.mult))
            by_tile = pick.rearrange("p (t i) k -> p t i k", t=TILES)
            for g in range(GROUPS):
                dve.scalar_tensor_tensor(out=weight[:, :, g, :], in0=by_tile[:, :, 1 + g, :],
                                         scalar=1.0 / float(GROUPS) ** 0.5,
                                         in1=by_tile[:, :, 0, g:g + 1].broadcast_to([SEQ, TILES, 4]),
                                         op0=ALU.mult, op1=ALU.mult).then_inc(sg("weights"), 1)

        def ffn_dve(dve):
            norm_dve(dve, "ln2", st_blocks, xn_blocks, bank)
            ln2_low(dve)
            route(dve)

            def scale_x(g, b, j, u, loads):
                dve.wait_ge(sg(f"share_in{u}"), loads)
                if not isinstance(g, int) or g >= 2:
                    dve.wait_ge(sg("xe_low"), g - 1)
                dve.tensor_tensor(xe[:, b, :], xn_blocks[j], blk(share[:, u], j), ALU.mult).then_inc(sg("xe"), 1)

            def low(n, k):
                dve.wait_ge(sg("hid_high"), n + 1)
                dve.tensor_tensor(hidL[:, k % 4, :], hid[:, k % 2, :], hidH[:, k % 4, :].bitcast(F32), ALU.subtract
                                  ).then_inc(sg("hid_low"), 1)

            scale_x(0, 0, 0, 0, 16)

            def expert(e, u, half):
                first = isinstance(e, int) and e == 0
                last = isinstance(e, int) and e == E0 - 1
                for k in range(ITEMS0):
                    n = e * ITEMS0 + k
                    j = k // C0
                    if k % C0 == 0 and not (last and j == NBLK - 1):
                        if j < NBLK - 1:
                            scale_x(e * NBLK + j + 1, (j + 1) % 2, j + 1, u, half * 16 + 16)
                        else:
                            scale_x(e * NBLK + j + 1, 0, 0, 1 - u, (half + u) * 16 + 16)
                    dve.wait_ge(sg("silu"), n + 1)
                    dve.wait_ge(sg("up_ps"), n + 1)
                    if not (first and k < 2):
                        dve.wait_ge(sg("hid_low"), n - 1)
                    dve.tensor_tensor(hid[:, k % 2, :], silu[:, k % 2, :], bank[6 + k % 2][:, 0:BLK], ALU.mult
                                      ).then_inc(sg("gated"), 1)
                    if not (first and k == 0):
                        low(n - 1, (k - 1) % ITEMS0)
            experts(expert)(dve, E0)
            low(E0 * ITEMS0 - 1, ITEMS0 - 1)
            dve.wait_ge(sg("down"), E0 * ITEMS0)
            for j in range(NBLK):
                dve.tensor_tensor(st_blocks[j], st_blocks[j], bank[j][:, 0:BLK], ALU.add).then_inc(sg("routed"), 1)

        PLACE = [(0, 1, 3, 2, 4)[m // KH] * KH + m % KH for m in range(GCH)]
        SIG, CAND, CELL, MEM = 0, 3 * SW, 4 * SW, 5 * SW
        HALF_SEQ = SEQ // 2
        hist_k = hist.rearrange("p t n -> p (t n)").rearrange("p (k t b) -> p k t b", k=KH, b=BATCH)

        def wave(eng, both):
            for t in range(4):
                both(t, t % 2)
            with eng.Fori(2, SEQ // 2 - 1) as i:
                for u in range(2):
                    both(i * 2 + u, u)
            for t in range(SEQ - 2, SEQ + 3):
                both(t, t % 2)

        def rec_sp(sp):
            sp.wait_ge(sg("routed"), NBLK)
            sp.dma_start(bias_raw[0:96], recb_in).then_inc(sg("recb_in"), 16)
            sp.dma_start(fc_w, fcw_in).then_inc(sg("fcw_in"), 16)
            sp.dma_start(fb2, fb2_in).then_inc(sg("fg_in"), 16)
            sp.dma_start(fg_w, fg_in).then_inc(sg("fg_in"), 16)
            sp.dma_start(fg_b, fgb_in.broadcast_to([SEQ, E1])).then_inc(sg("fg_in"), 16)
            for u in range(2):
                sp.dma_start(f_raw[:, u, :], f_in[u]).then_inc(sg(f"f_in{u}"), 16)

        def rec_pool(pool):
            pool.wait_ge(sg("xpair"), 2)

            def load(t, u):
                if here(t, 2, SEQ):
                    pool.wait_ge(sg("pre_ps0"), t - 1)
                settle(pool)
                pool.tensor_copy(xcur[:, u].rearrange("p g b -> p (g b)"),
                                 xpair[:, bass.ds(t, 1)].rearrange("p t g b -> p (t g b)")
                                 ).then_inc(sg("xcur"), 1)

            load(0, 0)

            def both(t, u):
                if here(t, 0, SEQ - 2):
                    load(t + 1, 1 - u)
                if here(t, 3, SEQ + 2):
                    pool.wait_ge(sg("state1"), t - 2)
                    settle(pool)
                    pool.tensor_copy(hist_k[:, :, bass.ds(t - 3, 1), :].rearrange("p k t b -> p k (t b)"),
                                     hfull[:, 1, 1 - u, :].rearrange("p (k b) -> p k b", k=KH)
                                     ).then_inc(sg("hist"), 1)
            wave(pool, both)

        def rec_pe(pe):
            norm_pe(pe, "ln3", st_blocks, bank, lambda e, j: e.wait_ge(sg("routed"), j + 1))
            normed(pe, "ln3")
            pe.wait_ge(sg("bias"), 1)
            pe.wait_ge(sg("rec_free"), 7 + 1)
            pe.wait_ge(sg("rec_part"), 7)

            def product(l, u, w, pair):
                to = bank[2 * l + u][:, 0:2 * GW].rearrange("p (g m b) -> p g m b", g=2, m=GCH)
                for m in range(GCH):
                    for s in range(2):
                        mm = pe.matmul(to[:, :, PLACE[m], :], rec_w[:, w, s, m * P:(m + 1) * P], pair,
                                       start=False, stop=False, skip_group_check=True)
                return mm

            def start_bias(l, u):
                pe.matmul(bank[2 * l + u][:, 0:GW], bias_part[0:96, l, :], bias_sel[0:96, :], start=True, stop=False,
                          skip_group_check=True)

            def open0(t, u):
                if here(t, 2, SEQ):
                    pe.wait_ge(sg("sum0"), t - 1)
                start_bias(0, u)
                pe.wait_ge(sg("xcur"), t + 1)
                return product(0, u, WX0, xcur[:, u])

            open0(0, 0).then_inc(sg("pre_ps0"), 1)
            open0(1, 1)

            def both(t, u):
                v = 1 - u
                if here(t, 1, SEQ - 1):
                    pe.wait_ge(sg("state0"), t)
                    for k in range(KH):
                        mm = product(0, u, WH0 + k, hpair[:, 0, v, k])
                    mm.then_inc(sg("pre_ps0"), 1)
                if here(t, 3, SEQ + 1):
                    pe.wait_ge(sg("state1"), t - 2)
                    for k in range(KH):
                        mm = product(1, u, WH1 + k, hpair[:, 1, v, k])
                    mm.then_inc(sg("pre_ps1"), 1)
                if here(t, 1, SEQ):
                    if here(t, 3, SEQ):
                        pe.wait_ge(sg("sum1"), t - 2)
                    start_bias(1, v)
                    if isinstance(t, int) and t == SEQ:
                        pe.wait_ge(sg("state0"), t)
                    for k in range(KH):
                        mm = product(1, v, WX1 + k, hpair[:, 0, v, k])
                    if isinstance(t, int) and t == 1:
                        mm.then_inc(sg("pre_ps1"), 1)
                if here(t, 1, SEQ - 2):
                    open0(t + 1, v)
            wave(pe, both)
            pe.wait_ge(sg("fcw_in"), 16)
            pe.wait_ge(sg("hist"), SEQ)
            for j in range(NBLK):
                for k in range(KH):
                    mm = pe.matmul(bank[4 + j][:, 0:BLK], fc_w[:, k, :],
                                   blk(hist_k[:, k].rearrange("p t b -> p (t b)"), j),
                                   start=(k == 0), stop=(k == KH - 1))
                mm.then_inc(sg("fc"), 1)

        UNSCALE = 1.0 / (H_SCALE * W_SCALE)

        def rec_act(act):
            norm_act(act, "ln3", xn_blocks, bank, 1)
            act.activation(warm[:, :], warm[:, :], ACT.Sigmoid)

            def gates_of(l, n):
                act.wait_ge(sg(f"sum{l}"), n)
                act.activation(gates[:, l, SIG:3 * SW], pre[:, l, 0:3 * SW], ACT.Sigmoid, scale=UNSCALE)
                act.activation(gates[:, l, CAND:CAND + 4 * SW].rearrange("p (a n) -> p a n", a=2)[:, :, 0:SW],
                               pre[:, l, 3 * SW:5 * SW].rearrange("p (a n) -> p a n", a=2), ACT.Tanh, scale=UNSCALE
                               ).then_inc(sg(f"gates{l}"), 1)

            def cell_of(l, n):
                act.wait_ge(sg(f"cell{l}"), n)
                act.activation(tanh_c[:, l], gates[:, l, CELL:CELL + SW], ACT.Tanh).then_inc(sg(f"tanh_c{l}"), 1)

            def both(t, u):
                if here(t, 0, SEQ - 1):
                    gates_of(0, t + 1)
                    cell_of(0, t + 1)
                if here(t, 2, SEQ + 1):
                    gates_of(1, t - 1)
                    cell_of(1, t - 1)
            wave(act, both)
            for j in range(NBLK):
                act.wait_ge(sg("fc"), j + 1)
                if j >= 2:
                    act.wait_ge(sg("recurred"), j - 1)
                act.activation(fc_sb[:, j % 2], bank[4 + j][:, 0:BLK], ACT.Identity, bias=col(FC_B),
                               scale=1.0 / H_SCALE).then_inc(sg("fc_sb"), 1)

        def rec_dve(dve):
            norm_dve(dve, "ln3", st_blocks, xn_blocks, bank)
            steps = [0]

            def link(ins):
                steps[0] += 1
                ins.then_inc(sg("bias_step"), 1)
                dve.wait_ge(sg("bias_step"), steps[0])

            dve.wait_ge(sg("recb_in"), 16)
            for s in range(3):
                link(dve.tensor_copy(bias_cast[0:96, :, s, :], bias_raw[0:96]))
                if s < 2:
                    link(dve.tensor_tensor(bias_raw[0:96], bias_raw[0:96], bias_cast[0:96, :, s, :], ALU.subtract))
            for s in range(3):
                dve.tensor_copy(bias_part[32 * s:32 * s + 32], bias_cast[32 * s:32 * s + 32, :, s, :])
            dve.tensor_scalar(bias_sel[0:96, :], const[0:96, C_SEL:C_SEL + GW], H_SCALE * W_SCALE, None, ALU.mult
                              ).then_inc(sg("bias"), 1)
            xn_steps = xn[:, :].rearrange("p (t b) -> p t b", b=BATCH)
            for q in range(2):
                part = slice(q * HALF_SEQ, (q + 1) * HALF_SEQ)
                normed(dve, "ln3")
                dve.tensor_scalar(xpair[:, part, 0, :], xn_steps[:, part], H_SCALE, None, ALU.mult
                                  ).then_inc(sg("xpair_high"), 1)
                dve.wait_ge(sg("xpair_high"), q + 1)
                dve.scalar_tensor_tensor(out=xpair[:, part, 1, :], in0=xn_steps[:, part], scalar=H_SCALE,
                                         in1=xpair[:, part, 0, :], op0=ALU.mult, op1=ALU.subtract
                                         ).then_inc(sg("xpair"), 1)
            for l in range(2):
                dve.memset(gates[:, l, CELL:CELL + SW], 0.0).then_inc(sg("cell_zero"), 1)
            dve.wait_ge(sg("cell_zero"), 2)

            def sum_gates(l, n, u):
                dve.wait_ge(sg(f"pre_ps{l}"), n)
                dve.tensor_reduce(pre[:, l].rearrange("p (n z) -> p n z", z=1),
                                  bank[2 * l + u][:, 0:2 * GW].rearrange("p (g n) -> p n g", g=2), AX, ALU.add
                                  ).then_inc(sg(f"sum{l}"), 1)

            def products(l, n):
                dve.wait_ge(sg(f"gates{l}"), n)
                dve.tensor_tensor(prod[:, l], gates[:, l, SIG:2 * SW], gates[:, l, CAND:CAND + 2 * SW], ALU.mult
                                  ).then_inc(sg(f"prod{l}"), 1)

            def new_cell(l, n):
                dve.wait_ge(sg(f"prod{l}"), n)
                dve.tensor_tensor(gates[:, l, CELL:CELL + SW], prod[:, l, 0:SW], prod[:, l, SW:2 * SW], ALU.add
                                  ).then_inc(sg(f"cell{l}"), 1)

            def new_state(l, n, u):
                dve.wait_ge(sg(f"tanh_c{l}"), n)
                dve.scalar_tensor_tensor(out=out_h[:, l], in0=gates[:, l, 2 * SW:3 * SW], scalar=H_SCALE,
                                         in1=tanh_c[:, l], op0=ALU.mult, op1=ALU.mult).then_inc(sg(f"out{l}"), 1)
                if l == 1 and here(n, 3, SEQ):
                    dve.wait_ge(sg("hist"), n - 2)
                dve.wait_ge(sg(f"out{l}"), n)
                high = hpair[:, l, u, :, 0, :]
                full = hfull[:, l, u, :].rearrange("p (k b) -> p k b", k=KH)
                mem = gates[:, l, MEM:MEM + SW].rearrange("p (k b) -> p k b", k=KH)
                scaled = out_h[:, l].rearrange("p (k b) -> p k b", k=KH)
                dve.scalar_tensor_tensor(out=high, in0=mem, scalar=H_SCALE, in1=scaled, op0=ALU.mult, op1=ALU.add)
                dve.scalar_tensor_tensor(out=full, in0=mem, scalar=H_SCALE, in1=scaled, op0=ALU.mult, op1=ALU.add
                                         ).then_inc(sg(f"full{l}"), 1)

            def state_low(l, n, u):
                dve.wait_ge(sg(f"full{l}"), n)
                dve.tensor_tensor(hpair[:, l, u, :, 1, :], hfull[:, l, u, :].rearrange("p (k b) -> p k b", k=KH),
                                  hpair[:, l, u, :, 0, :], ALU.subtract).then_inc(sg(f"state{l}"), 1)

            def both(t, u):
                first_layer, second_layer = here(t, 0, SEQ - 1), here(t, 2, SEQ + 1)
                if here(t, 3, SEQ + 2):
                    new_state(1, t - 2, 1 - u)
                    state_low(1, t - 2, 1 - u)
                if first_layer:
                    sum_gates(0, t + 1, u)
                    products(0, t + 1)
                    new_cell(0, t + 1)
                if second_layer:
                    sum_gates(1, t - 1, u)
                if first_layer:
                    new_state(0, t + 1, u)
                if second_layer:
                    products(1, t - 1)
                if first_layer:
                    state_low(0, t + 1, u)
                if second_layer:
                    new_cell(1, t - 1)
            wave(dve, both)
            for j in range(NBLK):
                dve.wait_ge(sg("fc_sb"), j + 1)
                dve.tensor_tensor(st_blocks[j], st_blocks[j], fc_sb[:, j % 2], ALU.add).then_inc(sg("recurred"), 1)

        ITEMS1 = NBLK * C1
        ln4_high, ln4_low = split_x("ln4", NBLK)

        def last_sp(sp):
            sp.wait_ge(sg("mask_T"), NBLK)
            sp.dma_start(mask_dram, mask_T).then_inc(sg("mask_out"), 16)
            sp.wait_ge(sg("mask_out"), 16)
            for u in range(2):
                sp.dma_start(mask_b[:, u, :], mask_dram[u:u + 1, :].broadcast_to([P, TOKENS])
                             ).then_inc(sg(f"mask_in{u}"), 16)
            with sp.Fori(1, E1 // 2) as i:
                for u in range(2):
                    e = i * 2 + u
                    sp.wait_ge(sg("f_low"), e - 1)
                    sp.dma_start(f_raw[:, u, :], f_in[bass.ds(e, 1)].rearrange("e p n -> (e p) n")
                                 ).then_inc(sg(f"f_in{u}"), 16)
                    sp.wait_ge(sg("masked"), (e - 1) * ITEMS1)
                    sp.dma_start(mask_b[:, u, :], mask_dram[bass.ds(e, 1), :].broadcast_to([P, TOKENS])
                                 ).then_inc(sg(f"mask_in{u}"), 16)
            for j in range(NBLK):
                sp.wait_ge(sg("final"), j + 1)
                sp.dma_start(blk(out, j), st_blocks[j]).then_inc(sg("out"), 16)
            sp.wait_ge(sg("out"), NBLK * 16)

        def last_pool(pool):
            pool.wait_ge(sg("recurred"), NBLK)

            def f_split(e, u, half):
                pool.wait_ge(sg(f"f_in{u}"), half * 16 + 16)
                if not isinstance(e, int) or e >= 2:
                    pool.wait_ge(sg("f_down"), (e - 1) * ITEMS1)
                settle(pool)
                pool.tensor_tensor(wH[:, u, 0:F0], f_raw[:, u, :], one[:, :].broadcast_to([P, F0]), ALU.mult
                                   ).then_inc(sg("f_high"), 1)
                pool.wait_ge(sg("f_high"), e + 1)
                pool.tensor_tensor(wL[:, u, 0:F0], f_raw[:, u, :], wH[:, u, 0:F0].bitcast(F32), ALU.subtract
                                   ).then_inc(sg("f_low"), 1)
                at = slice(FB1 + e * C1, FB1 + (e + 1) * C1) if isinstance(e, int) else bass.ds(e * C1 + FB1, C1)
                pool.tensor_tensor(f_bias[:, u, :], cols[:, at], one[:, :].broadcast_to([P, C1]), ALU.mult
                                   ).then_inc(sg("f_bias"), 1)

            def expert(e, u, half):
                if isinstance(e, int) and e == 0:
                    f_split(0, 0, 0)
                if not (isinstance(e, int) and e == E1 - 1):
                    f_split(e + 1, 1 - u, half + u)
            experts(expert)(pool, E1)

        def last_pe(pe):
            norm_pe(pe, "ln4", st_blocks, bank, lambda e, j: e.wait_ge(sg("recurred"), j + 1))
            normed(pe, "ln4")
            pe.wait_ge(sg("fg_in"), 48)
            for t in range(TILES):
                mm = pe.matmul(bank[7][0:SEQ, t * E1:(t + 1) * E1], xn[:, t * SEQ:(t + 1) * SEQ], fg_w,
                               start=True, stop=True)
            mm.then_inc(sg("f_logits"), 1)
            pe.wait_ge(sg("mask"), 1)
            for t in range(TILES):
                mm = pe.transpose(bank[t // 4][0:E1, t % 4 * SEQ:(t % 4 + 1) * SEQ], chosen[:, t],
                                  ident[0:SEQ, 0:SEQ])
                if t % 4 == 3:
                    mm.then_inc(sg("mask_ps"), 1)
            for j in range(NBLK):
                pe.wait_ge(sg("mask_T"), j + 1)
                pe.matmul(bank[j][:, 0:BLK], fb2, blk(mask_T, j), start=True, stop=False, skip_group_check=True)

            def down(n, k, u):
                j, c = divmod(k, C1)
                w = H1 + c * P
                pe.wait_ge(sg("f_hid_low"), n + 1)
                split3(pe, bank[j][:, 0:BLK], wH[:, u, w:w + P], wL[:, u, w:w + P], hidH[:, k % 4, :],
                       hidL[:, k % 4, :], start=False, stop=False).then_inc(sg("f_down"), 1)

            def expert(e, u, half):
                first = isinstance(e, int) and e == 0
                for k in range(ITEMS1):
                    j, c = divmod(k, C1)
                    n = e * ITEMS1 + k
                    if k == 0:
                        pe.wait_ge(sg("f_low"), e + 1)
                    if first and c == 0:
                        pe.wait_ge(sg("x_low"), NBLK + j + 1)
                    if not (first and k < 4):
                        pe.wait_ge(sg("relu"), n - 3)
                    w = c * P
                    split3(pe, bank[4 + k % 4][:, 0:BLK], wH[:, u, w:w + P], wL[:, u, w:w + P], blk(xnH, j),
                           blk(xnL, j), start=True, stop=True).then_inc(sg("f_up"), 1)
                    if k >= LAG:
                        down(n - LAG, k - LAG, u)
                    elif not first:
                        down(n - LAG, k - LAG + ITEMS1, 1 - u)
            experts(expert)(pe, E1)
            for k in range(ITEMS1 - LAG, ITEMS1):
                down((E1 - 1) * ITEMS1 + k, k, 1)

        def last_act(act):
            norm_act(act, "ln4", xn_blocks, bank, 1)
            ln4_high(act)
            for j in range(NBLK):
                act.wait_ge(sg("mask_ps"), j + 1)
                act.activation(blk(mask_T, j), bank[j][0:E1, 0:BLK], ACT.Copy).then_inc(sg("mask_T"), 1)
            act.activation(warm[:, :], warm[:, :], ACT.Relu)

            def high(n, k):
                act.wait_ge(sg("masked"), n + 1)
                if not isinstance(n, int) or n >= 4:
                    act.wait_ge(sg("f_down"), n - 3)
                act.activation(hidH[:, k % 4, :], fhid[:, k % 2, :], ACT.Copy).then_inc(sg("f_hid_high"), 1)

            def expert(e, u, half):
                first = isinstance(e, int) and e == 0
                for k in range(ITEMS1):
                    n = e * ITEMS1 + k
                    c = k % C1
                    if c == 0 and k == 0:
                        act.wait_ge(sg("f_bias"), e + 1)
                    act.wait_ge(sg("f_up"), n + 1)
                    if not (first and k < 2):
                        act.wait_ge(sg("masked"), n - 1)
                    act.activation(relu[:, k % 2, :], bank[4 + k % 4][:, 0:BLK], ACT.Relu,
                                   bias=f_bias[:, u, c:c + 1]
                                   ).then_inc(sg("relu"), 1)
                    if not (first and k == 0):
                        high(n - 1, (k - 1) % ITEMS1)
            experts(expert)(act, E1)
            high(E1 * ITEMS1 - 1, ITEMS1 - 1)

        def last_dve(dve):
            norm_dve(dve, "ln4", st_blocks, xn_blocks, bank)
            ln4_low(dve)
            steps = [0]

            def link(ins):
                steps[0] += 1
                ins.then_inc(sg("mask_step"), 1)
                dve.wait_ge(sg("mask_step"), steps[0])

            def spread(v):
                return v.rearrange("p (t z) -> p t z", z=1).broadcast_to([SEQ, TILES, E1])

            dve.wait_ge(sg("f_logits"), 1)
            dve.wait_ge(sg("fg_in"), 48)
            link(dve.tensor_tensor(logit, bank[7][0:SEQ, 0:TILES * E1].rearrange("p (t e) -> p t e", t=TILES),
                                   fg_b.rearrange("p (z e) -> p z e", z=1).broadcast_to([SEQ, TILES, E1]), ALU.add))
            link(dve.tensor_reduce(best[:, 0], logit, AX, ALU.max))
            link(dve.tensor_tensor(chosen, logit, spread(best[:, 0]), ALU.is_equal))
            link(dve.tensor_tensor(chosen, chosen,
                                   const[0:SEQ, C_PRI:C_PRI + E1].rearrange("p (z e) -> p z e", z=1).broadcast_to(
                                       [SEQ, TILES, E1]), ALU.mult))
            link(dve.tensor_reduce(best[:, 1], chosen, AX, ALU.max))
            dve.tensor_tensor(chosen, chosen, spread(best[:, 1]), ALU.is_equal).then_inc(sg("mask"), 1)

            def low(n, k):
                dve.wait_ge(sg("f_hid_high"), n + 1)
                dve.tensor_tensor(hidL[:, k % 4, :], fhid[:, k % 2, :], hidH[:, k % 4, :].bitcast(F32), ALU.subtract
                                  ).then_inc(sg("f_hid_low"), 1)

            def expert(e, u, half):
                first = isinstance(e, int) and e == 0
                for k in range(ITEMS1):
                    n = e * ITEMS1 + k
                    if k == 0:
                        dve.wait_ge(sg(f"mask_in{u}"), half * 16 + 16)
                    dve.wait_ge(sg("relu"), n + 1)
                    if not (first and k < 2):
                        dve.wait_ge(sg("f_hid_low"), n - 1)
                    dve.tensor_tensor(fhid[:, k % 2, :], relu[:, k % 2, :], blk(mask_b[:, u], k // C1), ALU.mult
                                      ).then_inc(sg("masked"), 1)
                    if not (first and k == 0):
                        low(n - 1, (k - 1) % ITEMS1)
            experts(expert)(dve, E1)
            low(E1 * ITEMS1 - 1, ITEMS1 - 1)
            dve.wait_ge(sg("f_down"), E1 * ITEMS1)
            for j in range(NBLK):
                dve.tensor_tensor(st_blocks[j], st_blocks[j], bank[j][:, 0:BLK], ALU.add).then_inc(sg("final"), 1)


        block = ctx.enter_context(nc.Block())

        @block.sync
        def _(sp):
            tok_sp(sp)
            ffn_sp(sp)
            rec_sp(sp)
            last_sp(sp)

        @block.gpsimd
        def _(pool):
            tok_pool(pool)
            att_pool(pool)
            ffn_pool(pool)
            rec_pool(pool)
            last_pool(pool)

        @block.tensor
        def _(pe):
            tok_pe(pe)
            att_pe(pe)
            ffn_pe(pe)
            rec_pe(pe)
            last_pe(pe)

        @block.scalar
        def _(act):
            tok_act(act)
            att_act(act)
            ffn_act(act)
            rec_act(act)
            last_act(act)

        @block.vector
        def _(dve):
            tok_dve(dve)
            att_dve(dve)
            ffn_dve(dve)
            rec_dve(dve)
            last_dve(dve)


def kernel(**inputs):
    import numpy as np
    import concourse.bacc as bacc
    from concourse.bass_utils import run_bass_kernel_spmd

    a = {k: np.asarray(v) for k, v in inputs.items()}

    def padded_heads(v):
        v = v.reshape(v.shape[:-1] + (HEADS, HD))
        z = np.zeros(v.shape[:-1] + (PAD,), v.dtype)
        z[..., :HD] = v
        return z.reshape(v.shape[:-2] + (2, P))

    img = np.zeros((BATCH, SIDE + 2, SIDE + 2, COLORS), a["x"].dtype)
    img[:, 1:-1, 1:-1] = a["x"]
    grid = np.stack([img[:, PATCH * p:PATCH * p + WIDE, PATCH * q:PATCH * q + WIDE]
                     for p in range(GRID) for q in range(GRID)])
    patches = grid.reshape(PATCHES, BATCH, RCH, ROWS2).transpose(3, 2, 0, 1).reshape(ROWS2, RCH, EMB)
    taps = np.zeros((SHIFTS, WIDE, WIDE, COLORS, D), a["L0_tok_conv_w"].dtype)
    for s, (di, dj) in enumerate(((0, 0), (0, -1), (0, 1), (-1, 0), (1, 0))):
        taps[s, 1 + di:1 + di + PATCH, 1 + dj:1 + dj + PATCH] = a["L0_tok_conv_w"][:, :, 3 * s:3 * s + 3]
    taps = taps.reshape(SHIFTS, RCH, ROWS2, D).transpose(2, 0, 1, 3)

    wq, wk, wv = (padded_heads(a["L0_attn_in_proj_w"][i * D:(i + 1) * D].T) for i in range(3))
    qkvw = np.concatenate([wq, wk, wv], axis=1)
    bq, bk, bv = (padded_heads(a["L0_attn_in_proj_b"][i * D:(i + 1) * D]) for i in range(3))
    outw = padded_heads(a["L0_attn_out_proj_w"]).transpose(2, 1, 0)

    cols = np.zeros((P, NCOLS), np.float32)
    for i, v in ((CONV_B, a["L0_tok_conv_b"]), (GAMMA, a["L0_tok_gamma"]), (BETA, a["L0_tok_beta"]),
                 (DENSE_B, a["L0_tok_dense_b"]), (OUT_B, a["L0_attn_out_proj_b"]), (FC_B, a["L1_attn_bfc"])):
        cols[:, i] = v
    cols[:, QKV_B:QKV_B + 6] = np.concatenate([bq, bk, bv]).T
    cols[:, FB1:] = a["L1_ffn_b1"].reshape(E1 * C1, P).T

    const = np.zeros((P, NCONST), np.float32)
    const[:, C_ID:C_ID + P] = np.eye(P)
    i = np.arange(SEQ)
    const[:SEQ, C_DIST:C_DIST + SEQ] = -(i[None, :] - i[:, None]).astype(np.float32) ** 2
    gate_place = [(0, 1, 3, 2, 4)[m // KH] * KH + m % KH for m in range(GCH)]
    for s in range(3):
        for m in range(GCH):
            const[32 * s + m, C_SEL + gate_place[m] * BATCH:C_SEL + (gate_place[m] + 1) * BATCH] = 1.0

    const[:, C_PRI:C_PRI + E1] = np.arange(E1, 0, -1)

    w2 = a["L0_ffn_W2"].reshape(E0, C0, P, D).transpose(0, 2, 1, 3).reshape(E0, P, H0)
    w0 = np.concatenate([a["L0_ffn_W1"], a["L0_ffn_W3"], w2], axis=2)
    route = np.concatenate([a["L0_ffn_Wr"], a["L0_ffn_Wgate"].transpose(1, 0, 2).reshape(D, E0)], axis=1)
    routeb = np.concatenate([a["L0_ffn_br"], a["L0_ffn_bgate"].reshape(E0)])[None]
    rec = np.concatenate([a["L1_attn_Wx0"], a["L1_attn_Wh0"], a["L1_attn_Wx1"], a["L1_attn_Wh1"]])
    recb = np.zeros((96, 2, P), np.float32)
    for s in range(3):
        for l in range(2):
            recb[32 * s:32 * s + GCH, l] = a[f"L1_attn_b{l}"].reshape(GCH, P)
    f2 = a["L1_ffn_W2"].reshape(E1, C1, P, D).transpose(0, 2, 1, 3).reshape(E1, P, H1)
    f = np.concatenate([a["L1_ffn_W1"], f2], axis=2)

    arrays = {
        "taps": taps, "patches": patches, "txt": a["txt"].transpose(2, 1, 0).reshape(D, WORDS * BATCH),
        "cols": cols, "const": const, "dense": a["L0_tok_dense_w"], "qkvw": qkvw, "outw": outw,
        "heads": a["L0_attn_t"][None], "w0": w0, "route": route, "routeb": routeb,
        "rec": rec.reshape(7, P, GP), "recb": recb,
        "fcw": a["L1_attn_Wfc"].reshape(KH, P, D).transpose(1, 0, 2), "f": f, "fb2": a["L1_ffn_b2"],
        "fg": a["L1_ffn_Wg"], "fgb": a["L1_ffn_bg"][None],
    }
    arrays = {f"in_{k}": np.ascontiguousarray(v) for k, v in arrays.items()}
    nc = bacc.Bacc("TRN2", target_bir_lowering=False, num_devices=1)
    args = [nc.dram_tensor(k, v.shape, mybir.dt.from_np(v.dtype), kind="ExternalInput").ap()
            for k, v in arrays.items()]
    args.append(nc.dram_tensor("out_stream", (D, TOKENS), F32, kind="ExternalOutput").ap())
    build(nc, *args)
    r = run_bass_kernel_spmd(nc, [arrays], core_ids=[0])
    got = r.results[0]["out_stream"].reshape(D, SEQ, BATCH)
    return np.ascontiguousarray(got.transpose(2, 1, 0))
```

```python
from contextlib import ExitStack

import concourse.bass as bass
from concourse import mybir

F32 = mybir.dt.float32
F32R = mybir.dt.float32r
BF16 = mybir.dt.bfloat16
F16 = mybir.dt.float16
ALU = mybir.AluOpType
ACT = mybir.ActivationFunctionType
AX = mybir.AxisListType.X

P = 128
BATCH, SIDE, COLORS = 16, 112, 3
PATCH = 16
GRID = SIDE // PATCH
WIDE = PATCH + 2
WORDS = 77
PATCHES = GRID * GRID
SEQ = PATCHES + WORDS
TOKENS = SEQ * BATCH
NBLK = 4
BLK = TOKENS // NBLK
TILES = TOKENS // SEQ
D = 128
ROWS2 = 2 * WIDE * COLORS
RCH = WIDE // 2
EMB = PATCHES * BATCH
EBLK = EMB // 2
SHIFTS = 5
HEADS, HD = 8, 16
HALF = HEADS // 2
PAD = P // HALF
E0, GROUPS, H0 = 16, 4, 512
C0 = H0 // P
W0 = 3 * H0
E1, H1 = 8, 256
C1 = H1 // P
F0 = 2 * H1
RH = 256
KH = RH // P
GCH = 5 * RH // P
GP = GCH * P
GW = GCH * BATCH
SW = KH * BATCH
PAIR = 2
XCH = 3 * KH
XW = XCH * BATCH
WX0, WH0, WX1, WH1 = 0, 1, 3, 5
H_SCALE = 1024.0
W_SCALE = 64.0
ROUND = 4
LAG = 3
CONV_B, GAMMA, BETA, DENSE_B, OUT_B, FC_B, QKV_B = 0, 1, 2, 3, 4, 5, 6
FB1 = QKV_B + 6
NCOLS = FB1 + E1 * C1
C_ID, C_DIST, C_SEL = 0, P, P + SEQ
C_PRI = C_SEL + GW
NCONST = C_PRI + E1


def build(nc, taps_in, patches_in, txt_in, cols_in, const_in, dense_in, qkvw_in, outw_in, heads_in, w0_in,
          route_in, routeb_in, rec_in, recb_in, fcw_in, f_in, fb2_in, fg_in, fgb_in, out):
    share_dram = nc.dram_tensor("share_scratch", (E0, TOKENS), F32, kind="Internal").ap()
    mask_dram = nc.dram_tensor("mask_scratch", (E1, TOKENS), F32, kind="Internal").ap()

    with ExitStack() as ctx:
        def sb(name, shape, dt=F32):
            return ctx.enter_context(nc.sbuf_tensor(name, shape, dt))

        sems = {}

        def sg(name):
            if name not in sems:
                sems[name] = ctx.enter_context(nc.semaphore(name))
            return sems[name]

        def reach(eng, name, value):
            if not isinstance(value, int) or value > 0:
                eng.wait_ge(sg(name), value)

        def settle(eng):
            eng.wait_ge(sg("warm"), 1)

        low_banks = [ctx.enter_context(nc.psum_tensor(f"bank{i}", [P, 512], F32)) for i in range(4)]
        quad = ctx.enter_context(nc.psum_tensor("quad", [P, 4, 512], F32))
        bank = [b[:, :] for b in low_banks] + [quad[:, i, :] for i in range(4)]

        stream = sb("stream", [P, TOKENS])
        xn = sb("xn", [P, TOKENS])
        mean_mat = sb("mean_mat", [P, P])
        cols = sb("cols", [P, NCOLS])
        const = sb("const", [P, NCONST])
        eps = sb("eps", [P, 2])
        spread_row = sb("spread_row", [P, P])
        warm = sb("warm", [P, 1])
        one = sb("one", [P, 1])
        ident = const[:, C_ID:C_ID + P]

        wH = sb("wH", [P, 2, W0], F32R)
        wL = sb("wL", [P, 2, W0], F32R)
        xnH = sb("xnH", [P, TOKENS], F32R)
        xnL = sb("xnL", [P, TOKENS], F32R)
        xeH = sb("xeH", [P, 2, BLK], F32R)
        xeL = sb("xeL", [P, 2, BLK], F32R)
        hidH = sb("hidH", [P, 4, BLK], F32R)
        hidL = sb("hidL", [P, 4, BLK], F32R)

        AREA = 30000
        area = sb("area", [P, AREA])

        def region(start, size=AREA):
            at = [start]

            def view(words, parts=P):
                a = area[0:parts, at[0]:at[0] + words]
                at[0] += words
                assert at[0] <= min(AREA, size), (at[0], size)
                return a
            return view, at

        view, at = region(0)
        sq = view(NBLK * BLK).rearrange("p (u n) -> p u n", u=NBLK)
        STAGE = at[0]
        taps = view(SHIFTS * RCH * D, ROWS2).rearrange("p (s k d) -> p s k d", s=SHIFTS, k=RCH)
        patches = view(RCH * EMB, ROWS2).rearrange("p (k n) -> p k n", k=RCH)
        conv = view(EMB)
        emb = view(EMB)
        dense_w = view(D)
        LOADED = AREA - (6 * P + 2 * P + 4 * HEADS)
        view, at = region(LOADED)
        qkv_w = view(6 * P).rearrange("p (w n) -> p w n", w=6)
        out_w = view(2 * P).rearrange("p (a o) -> p a o", a=2)
        slope = view(4 * HEADS, SEQ).rearrange("p (a h) -> p a h", a=4)
        view, at = region(STAGE + 2 * W0, LOADED)
        decay = view(HEADS * SEQ, SEQ).rearrange("p (h k) -> p h k", h=HEADS)
        headsT = view(2 * TOKENS).rearrange("p (a t b) -> p a t b", a=2, b=BATCH)
        xb = view(2 * SEQ).rearrange("p (u n) -> p u n", u=2)
        qk = view(2 * 4 * SEQ).rearrange("p (u w n) -> p u w n", u=2, w=4)
        vb = view(ROUND * 2 * P, SEQ).rearrange("p (u n) -> p u n", u=ROUND)
        att = view(ROUND * HEADS * SEQ, SEQ).rearrange("p (u h k) -> p u h k", u=ROUND, h=HEADS)
        attT = view(2 * HALF * SEQ, SEQ).rearrange("p (a j k) -> p a j k", a=2, j=HALF)
        smax = view(ROUND * HEADS, SEQ).rearrange("p (u h) -> p u h", u=ROUND)
        ssum = view(ROUND * HEADS, SEQ).rearrange("p (u h) -> p u h", u=ROUND)
        srec = view(ROUND * HEADS, SEQ).rearrange("p (u h) -> p u h", u=ROUND)

        view, at = region(STAGE)
        w_raw = view(2 * W0).rearrange("p (u n) -> p u n", u=2)
        assert at[0] <= STAGE + SHIFTS * RCH * D
        share = view(2 * TOKENS).rearrange("p (u n) -> p u n", u=2)
        xe = view(2 * BLK).rearrange("p (u n) -> p u n", u=2)
        silu = view(2 * BLK).rearrange("p (u n) -> p u n", u=2)
        hid = view(2 * BLK).rearrange("p (u n) -> p u n", u=2)
        n_soft = TILES * (1 + GROUPS)
        route_w = view(20)
        route_b = view(20, SEQ)
        route_at = at[0]
        prob = view(n_soft * 4, SEQ).rearrange("p (n k) -> p n k", k=4)
        rank = view(n_soft * 4, SEQ).rearrange("p (n k) -> p n k", k=4)
        pick = view(n_soft * 4, SEQ).rearrange("p (n k) -> p n k", k=4)
        beat = view(n_soft * 6, SEQ).rearrange("p (a n) -> p a n", a=6)
        top = view(n_soft * 3, SEQ).rearrange("p (a n) -> p a n", a=3)
        weight = view(TILES * E0, SEQ).rearrange("p (t g e) -> p t g e", t=TILES, g=GROUPS)
        shareT = view(TOKENS, E0)
        REC_AT = at[0]
        rec_w = view(7 * 2 * GP // 2).bitcast(F16).rearrange("p (w s n) -> p w s n", w=7, s=2)
        rec_raw = area[:, route_at:route_at + GP]
        assert route_at + GP <= REC_AT

        view, at = region(STAGE, REC_AT)
        xpair = view(SEQ * 2 * BATCH // 2).bitcast(F16).rearrange("p (t g b) -> p t g b", t=SEQ, g=2)
        hist = view(KH * TOKENS).rearrange("p (t n) -> p t n", t=SEQ)
        xcur = view(2 * PAIR * 2 * BATCH // 2).bitcast(F16).rearrange("p (q n) -> p q n", q=2)
        hpair0 = view(2 * KH * PAIR * 2 * BATCH // 2).bitcast(F16).rearrange(
            "p (q k s g b) -> p q k s g b", q=2, k=KH, s=PAIR, g=2)
        hpair1 = view(2 * KH * 2 * BATCH // 2).bitcast(F16).rearrange("p (u k g b) -> p u k g b", u=2, k=KH, g=2)
        pre = view(2 * GW).rearrange("p (l n) -> p l n", l=2)
        gates = view(2 * 7 * SW).rearrange("p (l n) -> p l n", l=2)
        prod = view(2 * 2 * SW).rearrange("p (l n) -> p l n", l=2)
        tanh_c = view(2 * SW).rearrange("p (l n) -> p l n", l=2)
        out_h = view(2 * SW).rearrange("p (l n) -> p l n", l=2)
        hfull = view(2 * 4 * SW).rearrange("p (l u n) -> p l u n", l=2, u=4)
        bias_raw = view(2 * P).rearrange("p (l n) -> p l n", l=2)
        bias_cast = view(2 * 3 * P // 2).bitcast(BF16).rearrange("p (l s n) -> p l s n", l=2, s=3)
        bias_part = view(2 * P // 2).bitcast(BF16).rearrange("p (l n) -> p l n", l=2)
        bias_sel = view(PAIR * GW // 2).bitcast(BF16)
        fc_w = view(KH * D).rearrange("p (k n) -> p k n", k=KH)
        f_raw = view(2 * F0).rearrange("p (u n) -> p u n", u=2)
        fb2 = view(D, E1)
        fg_w = view(E1)
        fg_b = view(E1, SEQ)
        view, at = region(REC_AT)
        fc_sb = view(2 * BLK).rearrange("p (u n) -> p u n", u=2)
        logit = view(TILES * E1, SEQ).rearrange("p (t e) -> p t e", t=TILES)
        chosen = view(TILES * E1, SEQ).rearrange("p (t e) -> p t e", t=TILES)
        best = view(2 * TILES, SEQ).rearrange("p (a t) -> p a t", a=2)
        mask_T = view(TOKENS, E1)
        relu = view(2 * BLK).rearrange("p (u n) -> p u n", u=2)
        fhid = view(2 * BLK).rearrange("p (u n) -> p u n", u=2)
        f_bias = view(2 * C1).rearrange("p (u n) -> p u n", u=2)
        mask_b = view(2 * TOKENS).rearrange("p (u n) -> p u n", u=2)

        def col(i):
            return cols[:, i:i + 1]

        def blk(t, j):
            return t[:, j * BLK:(j + 1) * BLK]

        def split3(eng, acc, aH, aL, bH, bL, start, stop):
            eng.matmul(acc, aH, bH, start=start, stop=False, skip_group_check=True)
            eng.matmul(acc, aH, bL, start=False, stop=False, skip_group_check=True)
            return eng.matmul(acc, aL, bH, start=False, stop=stop, skip_group_check=True)

        STAGES = {"tok": 1, "ln1": 2, "ln2": 3, "ln3": 4, "ln4": 5}
        NORM = {"tok": 0, "ln1": 2, "ln2": 2 + NBLK, "ln3": 2 + 2 * NBLK, "ln4": 2 + 3 * NBLK}

        def normed(eng, tag, blocks=NBLK):
            eng.wait_ge(sg("normed"), NORM[tag] + blocks)

        def norm_pe(pe, tag, src, banks, wait):
            n = len(src)
            for j in range(n):
                wait(pe, j)
                pe.matmul(banks[j][:, 0:src[j].shape[1]], mean_mat[:, :], src[j], start=True, stop=True
                          ).then_inc(sg("mean"), 1)
            for j in range(n):
                pe.wait_ge(sg("squared"), NORM[tag] + j + 1)
                pe.matmul(banks[n][32 * j:32 * j + 32, 0:src[j].shape[1]], mean_mat[:, 0:32],
                          sq[:, j, 0:src[j].shape[1]], start=True, stop=True).then_inc(sg("variance"), 1)
            pe.wait_ge(sg("spread_row"), 1 + NBLK)
            for h in range(2):
                pe.wait_ge(sg("inverted"), 2 * STAGES[tag] - 1 + h)
                for j in range(n):
                    part, width = slice(32 * j, 32 * j + 32), src[j].shape[1] // 2
                    ins = pe.matmul(banks[j][:, h * width:(h + 1) * width], spread_row[part, :],
                                    sq[part, 0, h * width:(h + 1) * width], start=True, stop=True)
                    if h == 1:
                        ins.then_inc(sg("scale_ps"), 1)

        def norm_act(act, tag, dst, banks, e):
            n = len(dst)
            act.wait_ge(sg("warm"), 1)
            act.activation(warm[:, :], warm[:, :], ACT.Sqrt)
            for j in range(n):
                act.wait_ge(sg("centred"), NORM[tag] + j + 1)
                act.activation(sq[:, j, 0:dst[j].shape[1]], dst[j], ACT.Square).then_inc(sg("squared"), 1)
            act.wait_ge(sg("variance"), NORM[tag] + n)
            act.activation(sq[0:32 * n, 0, 0:dst[0].shape[1]], banks[n][0:32 * n, 0:dst[0].shape[1]], ACT.Sqrt,
                           bias=eps[0:32 * n, e:e + 1]).then_inc(sg("deviation"), 1)

        def norm_dve(dve, tag, src, dst, banks, between=lambda: None):
            n = len(dst)
            for j in range(n):
                dve.wait_ge(sg("mean"), NORM[tag] + j + 1)
                dve.tensor_tensor(dst[j], src[j], banks[j][:, 0:src[j].shape[1]], ALU.subtract
                                  ).then_inc(sg("centred"), 1)
            dve.wait_ge(sg("deviation"), STAGES[tag])
            width = dst[0].shape[1] // 2
            for h in range(2):
                r = sq[0:32 * n, 0, h * width:(h + 1) * width]
                dve.reciprocal(r, r).then_inc(sg("inverted"), 1)
            between()
            for j in range(n):
                dve.wait_ge(sg("scale_ps"), NORM[tag] + j + 1)
                dve.tensor_tensor(dst[j], dst[j], banks[j][:, 0:src[j].shape[1]], ALU.mult).then_inc(sg("normed"), 1)

        xn_blocks = [blk(xn, j) for j in range(NBLK)]
        st_blocks = [blk(stream, j) for j in range(NBLK)]

        conv_blocks = [conv[:, j * EBLK:(j + 1) * EBLK] for j in range(2)]
        emb_blocks = [emb[:, j * EBLK:(j + 1) * EBLK] for j in range(2)]

        PARTS = (slice(0, RCH // 2), slice(RCH // 2, RCH))

        def tok_sp(sp):
            sp.dma_start(slope[:, 0, :], heads_in.broadcast_to([SEQ, HEADS])).then_inc(sg("slope_in"), 16)
            for i, rows in enumerate(PARTS):
                sp.dma_start(taps[:, :, rows], taps_in[:, :, rows]).then_inc(sg(f"taps_in{i}"), 16)
                sp.dma_start(patches[:, rows, 0:EBLK], patches_in[:, rows, 0:EBLK]).then_inc(sg(f"patches_in0{i}"), 16)
            sp.dma_start(const[:, :], const_in).then_inc(sg("const_in"), 16)
            sp.dma_start(patches[:, :, EBLK:EMB], patches_in[:, :, EBLK:EMB]).then_inc(sg("patches_in1"), 16)
            sp.dma_start(cols[:, :], cols_in).then_inc(sg("cols_in"), 16)
            sp.dma_start(dense_w, dense_in).then_inc(sg("dense_in"), 16)
            sp.dma_start(stream[:, EMB:TOKENS], txt_in).then_inc(sg("words_in"), 16)
            sp.dma_start(qkv_w, qkvw_in).then_inc(sg("att_w_in"), 16)
            sp.dma_start(out_w, outw_in).then_inc(sg("att_w_in"), 16)

        def tok_pool(pool):
            pool.memset(mean_mat[:, :], 1.0 / D).then_inc(sg("mean_mat"), 1)
            pool.memset(eps[:, 0:1], 1e-3).then_inc(sg("eps"), 1)
            pool.memset(eps[:, 1:2], 1e-5).then_inc(sg("eps"), 1)
            pool.memset(spread_row[:, :], 0.0).then_inc(sg("spread_row"), 1)
            pool.memset(one[:, :], 1.0).then_inc(sg("ones"), 1)
            pool.memset(warm[:, :], 0.0).then_inc(sg("warm"), 1)

        def tok_pe(pe):
            for j in range(2):
                if j == 1:
                    pe.wait_ge(sg("patches_in1"), 16)
                for k in range(RCH):
                    for i, rows in enumerate(PARTS):
                        if j == 0 and k == rows.start:
                            pe.wait_ge(sg("taps_sum"), (SHIFTS - 1) * (i + 1))
                            pe.wait_ge(sg(f"patches_in0{i}"), 16)
                    mm = pe.matmul(bank[j][:, 0:EBLK], taps[:, 0, k, :], patches[:, k, j * EBLK:(j + 1) * EBLK],
                                   start=(k == 0), stop=(k == RCH - 1))
                mm.then_inc(sg("conv"), 1)
            pe.wait_ge(sg("mean_mat"), 1)
            norm_pe(pe, "tok", conv_blocks, bank[2:6], lambda e, j: e.wait_ge(sg("conv_sb"), j + 1))
            pe.wait_ge(sg("dense_in"), 16)
            for j in range(2):
                pe.wait_ge(sg("emb"), j + 1)
                pe.matmul(bank[6 + j][:, 0:EBLK], dense_w, emb_blocks[j], start=True, stop=True
                          ).then_inc(sg("dense"), 1)

        def tok_act(act):
            act.wait_ge(sg("eps"), 2)
            norm_act(act, "tok", emb_blocks, bank[2:6], 0)

        def distance_bias(dve):
            dve.wait_ge(sg("slope_in"), 16)
            dve.tensor_tensor(slope[:, 1, :], slope[:, 0, :], slope[:, 0, :], ALU.mult).then_inc(sg("slope"), 1)
            dve.wait_ge(sg("slope"), 1)
            dve.tensor_tensor(slope[:, 2, :], slope[:, 1, :], slope[:, 1, :], ALU.mult).then_inc(sg("slope"), 1)
            dve.wait_ge(sg("slope"), 2)
            dve.tensor_scalar(slope[:, 2, :], slope[:, 2, :], 2.0, None, ALU.mult).then_inc(sg("slope"), 1)
            dve.wait_ge(sg("slope"), 3)
            dve.reciprocal(slope[:, 3, :], slope[:, 2, :]).then_inc(sg("slope"), 1)
            dve.wait_ge(sg("slope"), 4)
            dve.wait_ge(sg("const_in"), 16)
            for h in range(HEADS):
                ins = dve.tensor_scalar(decay[:, h % HALF * 2 + h // HALF, :], const[0:SEQ, C_DIST:C_DIST + SEQ],
                                        slope[:, 3, h:h + 1], None, ALU.mult)
            ins.then_inc(sg("decay"), 1)

        def tok_dve(dve):
            dve.wait_ge(sg("spread_row"), 1)
            for j in range(NBLK):
                dve.memset(spread_row[32 * j:32 * j + 1, :], 1.0).then_inc(sg("spread_row"), 1)
            for i, rows in enumerate(PARTS):
                dve.wait_ge(sg(f"taps_in{i}"), 16)
                for s in range(1, SHIFTS):
                    reach(dve, "taps_sum", i * (SHIFTS - 1) + s - 1)
                    dve.tensor_tensor(taps[:, 0, rows], taps[:, 0, rows], taps[:, s, rows], ALU.add
                                      ).then_inc(sg("taps_sum"), 1)
            distance_bias(dve)
            dve.wait_ge(sg("cols_in"), 16)
            for j in range(2):
                dve.wait_ge(sg("conv"), j + 1)
                dve.tensor_scalar(conv_blocks[j], bank[j][:, 0:EBLK], col(CONV_B), None, ALU.add
                                  ).then_inc(sg("conv_sb"), 1)
            dve.wait_ge(sg("conv_sb"), 2)
            norm_dve(dve, "tok", conv_blocks, emb_blocks, bank[2:6])
            for j in range(2):
                normed(dve, "tok", j + 1)
                dve.tensor_scalar(emb_blocks[j], emb_blocks[j], col(GAMMA), col(BETA), ALU.mult, ALU.add
                                  ).then_inc(sg("emb"), 1)
            for j in range(2):
                dve.wait_ge(sg("dense"), j + 1)
                dve.tensor_scalar(stream[:, j * EBLK:(j + 1) * EBLK], bank[6 + j][:, 0:EBLK], col(DENSE_B), None,
                                  ALU.add).then_inc(sg("embedded"), 1)

        xn_images = xn[:, :].rearrange("p (t b) -> p t b", b=BATCH)

        def here(m, first, last):
            return not isinstance(m, int) or first <= m <= last

        def at_image(t, b):
            return t[:, :, b] if isinstance(b, int) else t[:, :, bass.ds(b, 1)].rearrange("p t b -> p (t b)")

        def each_step(eng, body):
            for m in range(ROUND):
                body(m, m)
            with eng.Fori(1, BATCH // ROUND - 1) as i:
                for u in range(ROUND):
                    body(i * ROUND + u, u)
            for m in range(BATCH - ROUND, BATCH + 3):
                body(m, m % ROUND)

        def per_head(t, heads):
            return t.rearrange("p (h z) -> p h z", z=1).broadcast_to([SEQ, heads, SEQ])

        WORDS_FIRST = (2, 3, 0, 1)

        def att_pool(pool):
            normed(pool, "ln1")

            def gather(m, u):
                if here(m, 2, BATCH):
                    pool.wait_ge(sg("qk_ps"), m - 1)
                settle(pool)
                pool.tensor_copy(xb[:, u % 2, :], at_image(xn_images, m)).then_inc(sg("xb"), 1)

            gather(0, 0)

            def step(m, u):
                if here(m, 0, BATCH - 2):
                    gather(m + 1, u + 1)
                if here(m, 1, BATCH):
                    v = (u - 1) % ROUND
                    pool.wait_ge(sg("smax"), m)
                    pool.tensor_tensor(att[:, v], att[:, v], per_head(smax[:, v, :], HEADS), ALU.subtract
                                       ).then_inc(sg("shifted"), 1)
                if here(m, 2, BATCH + 1):
                    v = (u - 2) % ROUND
                    pool.wait_ge(sg("srec"), m - 1)
                    pool.tensor_tensor(att[:, v, 0:HALF], att[:, v, 0:HALF], per_head(srec[:, v, 0:HALF], HALF),
                                       ALU.mult).then_inc(sg("soft0"), 1)
            each_step(pool, step)

        def att_pe(pe):
            norm_pe(pe, "ln1", [st_blocks[j] for j in WORDS_FIRST], bank,
                    lambda e, j: e.wait_ge(sg("words_in"), 16) if j < 2 else e.wait_ge(sg("embedded"), 2))
            pe.wait_ge(sg("att_w_in"), 32)
            pe.wait_ge(sg("const_in"), 16)
            normed(pe, "ln1")

            def step(m, u):
                project, weigh = here(m, 0, BATCH - 1), here(m, 3, BATCH + 2)
                w = (u - 3) % ROUND
                if here(m, 1, BATCH):
                    pe.wait_ge(sg("qk"), m)
                    pe.wait_ge(sg("vb"), m)
                    if here(m, 2, BATCH):
                        pe.wait_ge(sg("scaled"), m - 1)
                    for h in range(HEADS):
                        a, j = divmod(h, HALF)
                        rows = slice(PAD * j, PAD * (j + 1))
                        mm = pe.matmul(quad[0:SEQ, j, a * SEQ:(a + 1) * SEQ], qk[rows, (u - 1) % 2, a, :],
                                       qk[rows, (u - 1) % 2, 2 + a, :], start=True, stop=True)
                    mm.then_inc(sg("scores"), 1)
                if project:
                    pe.wait_ge(sg("xb"), m + 1)
                    pe.matmul(quad[0:SEQ, 0, 2 * SEQ:2 * SEQ + 2 * P], xb[:, u % 2, :], qkv_w[:, 4:6, :],
                              start=True, stop=True).then_inc(sg("values"), 1)
                if weigh:
                    pe.wait_ge(sg("soft0"), m - 2)
                    pe.wait_ge(sg("soft1"), m - 2)
                    for a in range(2):
                        if here(m, 4, BATCH + 2):
                            pe.wait_ge(sg(f"attT{a}"), m - 3)
                        for j in range(HALF):
                            mm = pe.transpose(bank[2 + a][0:SEQ, j * SEQ:(j + 1) * SEQ],
                                              att[:, w, 2 * j + a, :], ident[0:SEQ, 0:SEQ])
                        mm.then_inc(sg(f"attT_ps{a}"), 1)
                if project:
                    for i in range(4):
                        mm = pe.matmul(bank[0][:, i * SEQ:(i + 1) * SEQ], qkv_w[:, i, :], xb[:, u % 2, :],
                                       start=True, stop=True)
                    mm.then_inc(sg("qk_ps"), 1)
                if weigh:
                    if here(m, 4, BATCH + 2):
                        pe.wait_ge(sg("heads"), m - 3)
                    for a in range(2):
                        pe.wait_ge(sg(f"attT{a}"), m - 2)
                        for j in range(HALF):
                            h = a * HALF + j
                            mm = pe.matmul(bank[1][PAD * j:PAD * (j + 1), a * SEQ:(a + 1) * SEQ],
                                           vb[:, w, PAD * h:PAD * (h + 1)], attT[:, a, j, :], start=True, stop=True)
                    mm.then_inc(sg("heads_ps"), 1)
            each_step(pe, step)
            for j in range(NBLK):
                pe.wait_ge(sg("heads"), BATCH)
                for a in range(2):
                    mm = pe.matmul(bank[2 + j][:, 0:BLK], out_w[:, a, :],
                                   blk(headsT[:, a].rearrange("p t b -> p (t b)"), j),
                                   start=(a == 0), stop=(a == 1))
                mm.then_inc(sg("projected"), 1)

        def att_act(act):
            norm_act(act, "ln1", [xn_blocks[j] for j in WORDS_FIRST], bank, 1)
            act.activation(warm[:, :], warm[:, :], ACT.Exp)

            def step(m, u):
                if here(m, 2, BATCH + 1):
                    v = (u - 2) % ROUND
                    act.wait_ge(sg("shifted"), m - 1)
                    act.activation(att[:, v].rearrange("p h k -> p (h k)"), att[:, v].rearrange("p h k -> p (h k)"),
                                   ACT.Exp).then_inc(sg("expd"), 1)
                if here(m, 3, BATCH + 2):
                    for a in range(2):
                        act.wait_ge(sg(f"attT_ps{a}"), m - 2)
                        if here(m, 4, BATCH + 2):
                            act.wait_ge(sg("heads_ps"), m - 3)
                        act.activation(attT[:, a].rearrange("p j k -> p (j k)"), bank[2 + a][0:SEQ, 0:HALF * SEQ],
                                       ACT.Copy).then_inc(sg(f"attT{a}"), 1)
                if here(m, 0, BATCH - 1):
                    act.wait_ge(sg("qk_ps"), m + 1)
                    if here(m, 2, BATCH):
                        act.wait_ge(sg("scores"), m - 1)
                    for w in range(4):
                        ins = act.activation(qk[:, u % 2, w, :], bank[0][:, w * SEQ:(w + 1) * SEQ], ACT.Identity,
                                             bias=col(QKV_B + w))
                    ins.then_inc(sg("qk"), 1)
                if here(m, 3, BATCH + 2):
                    act.wait_ge(sg("heads_ps"), m - 2)
                    settle(act)
                    for a in range(2):
                        ins = act.activation(at_image(headsT[:, a], m - 3), bank[1][:, a * SEQ:(a + 1) * SEQ],
                                             ACT.Identity, bias=col(QKV_B + 4 + a))
                    ins.then_inc(sg("heads"), 1)
            each_step(act, step)

        def att_dve(dve):
            norm_dve(dve, "ln1", [st_blocks[j] for j in WORDS_FIRST], [xn_blocks[j] for j in WORDS_FIRST], bank)
            dve.wait_ge(sg("decay"), 1)

            def step(m, u):
                if here(m, 4, BATCH + 2):
                    dve.wait_ge(sg("heads_ps"), m - 3)
                if here(m, 1, BATCH):
                    v = (u - 1) % ROUND
                    dve.wait_ge(sg("scores"), m)
                    if here(m, 0, BATCH - 1):
                        dve.wait_ge(sg("values"), m + 1)
                    dve.scalar_tensor_tensor(out=att[:, v].rearrange("p (j a) k -> p j (a k)", a=2),
                                             in0=quad[0:SEQ, :, 0:2 * SEQ], scalar=0.25,
                                             in1=decay.rearrange("p (j a) k -> p j (a k)", a=2),
                                             op0=ALU.mult, op1=ALU.add).then_inc(sg("scaled"), 1)
                    dve.wait_ge(sg("scaled"), m)
                    dve.tensor_reduce(smax[:, v, :], att[:, v], AX, ALU.max).then_inc(sg("smax"), 1)
                if here(m, 0, BATCH - 1):
                    dve.wait_ge(sg("values"), m + 1)
                    dve.tensor_copy(vb[:, u, :], quad[0:SEQ, 0, 2 * SEQ:2 * SEQ + 2 * P]).then_inc(sg("vb"), 1)
                if here(m, 2, BATCH + 1):
                    v = (u - 2) % ROUND
                    dve.wait_ge(sg("expd"), m - 1)
                    dve.tensor_reduce(ssum[:, v, :], att[:, v], AX, ALU.add).then_inc(sg("ssum"), 1)
                    dve.wait_ge(sg("ssum"), m - 1)
                    dve.reciprocal(srec[:, v, :], ssum[:, v, :]).then_inc(sg("srec"), 1)
                    dve.wait_ge(sg("srec"), m - 1)
                    dve.tensor_tensor(att[:, v, HALF:], att[:, v, HALF:], per_head(srec[:, v, HALF:], HALF),
                                      ALU.mult).then_inc(sg("soft1"), 1)
            each_step(dve, step)
            for j in range(NBLK):
                dve.wait_ge(sg("projected"), j + 1)
                dve.scalar_tensor_tensor(out=st_blocks[j], in0=bank[2 + j][:, 0:BLK], scalar=col(OUT_B),
                                         in1=st_blocks[j], op0=ALU.add, op1=ALU.add).then_inc(sg("attended"), 1)

        ITEMS0 = NBLK * C0

        def experts(body):
            def run(eng, count):
                body(0, 0, 0)
                with eng.Fori(0, count // 2 - 1) as i:
                    body(i * 2 + 1, 1, i)
                    body(i * 2 + 2, 0, i + 1)
                body(count - 1, 1, count // 2 - 1)
            return run

        def split_x(tag, before):
            def on_act(act):
                for j in range(NBLK):
                    normed(act, tag, j + 1)
                    act.activation(blk(xnH, j), xn_blocks[j], ACT.Copy).then_inc(sg("x_high"), 1)

            def on_dve(dve):
                for j in range(NBLK):
                    dve.wait_ge(sg("x_high"), before + j + 1)
                    dve.tensor_tensor(blk(xnL, j), xn_blocks[j], blk(xnH, j).bitcast(F32), ALU.subtract
                                      ).then_inc(sg("x_low"), 1)
            return on_act, on_dve

        ln2_high, ln2_low = split_x("ln2", 0)

        def ffn_sp(sp):
            sp.wait_ge(sg("conv"), 2)
            for u in range(2):
                sp.dma_start(w_raw[:, u, :], w0_in[u]).then_inc(sg(f"w_in{u}"), 16)
            sp.wait_ge(sg("attended"), NBLK)
            sp.dma_start(route_w, route_in).then_inc(sg("route_in"), 16)
            sp.dma_start(route_b, routeb_in.broadcast_to([SEQ, 20])).then_inc(sg("route_in"), 16)
            first, rest = slice(0, BLK), slice(BLK, TOKENS)
            sp.wait_ge(sg("shareT"), 1)
            sp.dma_start(share_dram[:, first], shareT[:, first]).then_inc(sg("share_out"), 16)
            sp.wait_ge(sg("share_out"), 16)
            sp.dma_start(share[:, 0, first], share_dram[0:1, first].broadcast_to([P, BLK])
                         ).then_inc(sg("share_first"), 16)
            sp.wait_ge(sg("shareT"), NBLK)
            sp.dma_start(share_dram[:, rest], shareT[:, rest]).then_inc(sg("share_out"), 16)
            sp.wait_ge(sg("share_out"), 32)
            sp.dma_start(share[:, 0, rest], share_dram[0:1, rest].broadcast_to([P, TOKENS - BLK])
                         ).then_inc(sg("share_in0"), 16)
            sp.dma_start(share[:, 1, :], share_dram[1:2, :].broadcast_to([P, TOKENS])).then_inc(sg("share_in1"), 16)
            with sp.Fori(1, E0 // 2) as i:
                for u in range(2):
                    e = i * 2 + u
                    sp.wait_ge(sg("w_low"), (e - 1) * 3)
                    sp.dma_start(w_raw[:, u, :], w0_in[bass.ds(e, 1)].rearrange("e p n -> (e p) n")
                                 ).then_inc(sg(f"w_in{u}"), 16)
                    sp.wait_ge(sg("xe"), (e - 1) * NBLK)
                    sp.dma_start(share[:, u, :], share_dram[bass.ds(e, 1), :].broadcast_to([P, TOKENS])
                                 ).then_inc(sg(f"share_in{u}"), 16)

        def xe_low(pool, g, b):
            pool.wait_ge(sg("xe_high"), g + 1)
            pool.tensor_tensor(xeL[:, b, :], xe[:, b, :], xeH[:, b, :].bitcast(F32), ALU.subtract
                               ).then_inc(sg("xe_low"), 1)

        def w_split(pool, e, u, half, piece):
            part = slice(piece * H0, (piece + 1) * H0)
            if piece == 0:
                pool.wait_ge(sg(f"w_in{u}"), half * 16 + 16)
                if not isinstance(e, int) or e >= 2:
                    pool.wait_ge(sg("down"), (e - 1) * ITEMS0)
                settle(pool)
            pool.tensor_tensor(wH[:, u, part], w_raw[:, u, part], one[:, :].broadcast_to([P, H0]), ALU.mult
                               ).then_inc(sg("w_high"), 1)
            pool.wait_ge(sg("w_high"), e * 3 + piece + 1)
            pool.tensor_tensor(wL[:, u, part], w_raw[:, u, part], wH[:, u, part].bitcast(F32), ALU.subtract
                               ).then_inc(sg("w_low"), 1)

        def rec_sub(pool, w):
            pool.wait_ge(sg("rec_part"), w + 1)
            part = rec_w[:, bass.ds(w, 1), 0, :].rearrange("p w n -> p (w n)")
            pool.tensor_tensor(rec_raw, rec_raw, part, ALU.subtract).then_inc(sg("rec_rest"), 1)

        def ffn_pool(pool):
            pool.wait_ge(sg("ones"), 1)
            for e in range(2):
                for piece in range(3):
                    w_split(pool, e, e, 0, piece)
            xe_low(pool, 0, 0)

            def expert(e, u, half):
                last = isinstance(e, int) and e == E0 - 1
                ahead = not isinstance(e, int)
                for j in range(NBLK):
                    if not (last and j == NBLK - 1):
                        xe_low(pool, e * NBLK + j + 1, (j + 1) % 2)
                    if j < 3 and ahead:
                        w_split(pool, e + 1, 1 - u, half + u, j)
                    if ahead and u == 1 and j == 0:
                        pool.wait_ge(sg("shareT"), 4)
                        pool.wait_ge(sg("rec_free"), half + 1)
                        pool.dma_start(rec_raw, rec_in[bass.ds(half, 1)].rearrange("w p n -> (w p) n")
                                       ).then_inc(sg("rec_in"), 16)
                    if ahead and u == 1 and j == 3:
                        rec_sub(pool, half)
            experts(expert)(pool, E0)

        def ffn_pe(pe):
            norm_pe(pe, "ln2", st_blocks, bank, lambda e, j: e.wait_ge(sg("attended"), j + 1))
            pe.wait_ge(sg("route_in"), 32)
            for t in range(TILES):
                normed(pe, "ln2", t * NBLK // TILES + 1)
                mm = pe.matmul(bank[0][0:SEQ, t * 20:(t + 1) * 20], xn[:, t * SEQ:(t + 1) * SEQ], route_w,
                               start=True, stop=True)
            mm.then_inc(sg("logits"), 1)
            pe.wait_ge(sg("weights"), GROUPS)
            for t in range(TILES):
                mm = pe.transpose(bank[t // 4][0:E0, t % 4 * SEQ:(t % 4 + 1) * SEQ],
                                  weight[:, t].rearrange("p g e -> p (g e)"), ident[0:SEQ, 0:SEQ])
                if t % 4 == 3:
                    mm.then_inc(sg("shareT_ps"), 1)
            pe.wait_ge(sg("shareT"), 4)

            def down(n, k, u, first):
                j, c = divmod(k, C0)
                w = 2 * H0 + c * P
                pe.wait_ge(sg("hid_low"), n + 1)
                split3(pe, bank[j][:, 0:BLK], wH[:, u, w:w + P], wL[:, u, w:w + P], hidH[:, k % 4, :],
                       hidL[:, k % 4, :], start=(first and c == 0), stop=False).then_inc(sg("down"), 1)

            def expert(e, u, half):
                first = isinstance(e, int) and e == 0
                for k in range(ITEMS0):
                    j, c = divmod(k, C0)
                    n = e * ITEMS0 + k
                    if k == 0:
                        pe.wait_ge(sg("w_low"), e * 3 + 3)
                    if first and c == 0:
                        pe.wait_ge(sg("x_low"), j + 1)
                    if not (first and k < 2):
                        pe.wait_ge(sg("silu"), n - 1)
                        pe.wait_ge(sg("gated"), n - 1)
                    w = c * P
                    split3(pe, bank[4 + k % 2][:, 0:BLK], wH[:, u, w:w + P], wL[:, u, w:w + P], blk(xnH, j),
                           blk(xnL, j), start=True, stop=True).then_inc(sg("gate_ps"), 1)
                    if c == 0:
                        pe.wait_ge(sg("xe_low"), e * NBLK + j + 1)
                    w = H0 + c * P
                    split3(pe, bank[6 + k % 2][:, 0:BLK], wH[:, u, w:w + P], wL[:, u, w:w + P], xeH[:, j % 2, :],
                           xeL[:, j % 2, :], start=True, stop=True).then_inc(sg("up_ps"), 1)
                    if k >= LAG:
                        down(n - LAG, k - LAG, u, first)
                    elif not first:
                        down(n - LAG, k - LAG + ITEMS0, 1 - u, isinstance(e, int) and e == 1)
            experts(expert)(pe, E0)
            for k in range(ITEMS0 - LAG, ITEMS0):
                down((E0 - 1) * ITEMS0 + k, k, 1, False)

        def xe_high(act, g, b):
            act.wait_ge(sg("xe"), g + 1)
            if not isinstance(g, int) or g >= 2:
                act.wait_ge(sg("up_ps"), (g - 1) * C0)
            act.activation(xeH[:, b, :], xe[:, b, :], ACT.Copy).then_inc(sg("xe_high"), 1)

        def ffn_act(act):
            norm_act(act, "ln2", xn_blocks, bank, 1)
            ln2_high(act)
            act.wait_ge(sg("routing"), 3)
            act.activation(prob.rearrange("p n k -> p (n k)"), prob.rearrange("p n k -> p (n k)"), ACT.Exp
                           ).then_inc(sg("route_exp"), 1)
            for j in range(4):
                act.wait_ge(sg("shareT_ps"), j + 1)
                act.activation(blk(shareT, j), bank[j][0:E0, 0:BLK], ACT.Copy).then_inc(sg("shareT"), 1)
            act.activation(warm[:, :], warm[:, :], ACT.Silu).then_inc(sg("rec_free"), 1)
            xe_high(act, 0, 0)

            def high(n, k):
                act.wait_ge(sg("gated"), n + 1)
                if not isinstance(n, int) or n >= 4:
                    act.wait_ge(sg("down"), n - 3)
                act.activation(hidH[:, k % 4, :], hid[:, k % 2, :], ACT.Copy).then_inc(sg("hid_high"), 1)

            def rec_cast(w, s):
                if s == 0:
                    act.wait_ge(sg("rec_in"), w * 16 + 16)
                    act.activation(rec_raw, rec_raw, ACT.Copy, scale=W_SCALE).then_inc(sg("rec_scaled"), 1)
                    act.wait_ge(sg("rec_scaled"), w + 1)
                else:
                    act.wait_ge(sg("rec_rest"), w + 1)
                settle(act)
                act.activation(rec_w[:, bass.ds(w, 1), s, :].rearrange("p w n -> p (w n)"), rec_raw, ACT.Copy
                               ).then_inc(sg("rec_free" if s == 1 else "rec_part"), 1)

            def expert(e, u, half):
                first = isinstance(e, int) and e == 0
                last = isinstance(e, int) and e == E0 - 1
                for k in range(ITEMS0):
                    n = e * ITEMS0 + k
                    act.wait_ge(sg("gate_ps"), n + 1)
                    if not (first and k < 2):
                        act.wait_ge(sg("gated"), n - 1)
                    act.activation(silu[:, k % 2, :], bank[4 + k % 2][:, 0:BLK], ACT.Silu).then_inc(sg("silu"), 1)
                    if not (first and k == 0):
                        high(n - 1, (k - 1) % ITEMS0)
                    if k % C0 == 1 and not (last and k > 3 * C0):
                        xe_high(act, e * NBLK + k // C0 + 1, (k // C0 + 1) % 2)
                    if not isinstance(e, int):
                        if u == 1 and k == 8:
                            rec_cast(half, 0)
                        if u == 0 and k == 2:
                            rec_cast(half - 1, 1)
            experts(expert)(act, E0)
            high(E0 * ITEMS0 - 1, ITEMS0 - 1)

        def route(dve):
            steps = [0]

            def link(ins):
                steps[0] += 1
                ins.then_inc(sg("routing"), 1)
                dve.wait_ge(sg("routing"), steps[0])

            def spread(v):
                return v.rearrange("p (n z) -> p n z", z=1).broadcast_to([SEQ, n_soft, 4])

            dve.wait_ge(sg("route_in"), 32)
            dve.wait_ge(sg("logits"), 1)
            link(dve.tensor_tensor(prob.rearrange("p (t i) k -> p t (i k)", t=TILES),
                                   bank[0][0:SEQ, 0:TILES * 20].rearrange("p (t i) -> p t i", t=TILES),
                                   route_b.rearrange("p (z i) -> p z i", z=1).broadcast_to([SEQ, TILES, 20]),
                                   ALU.add))
            link(dve.tensor_reduce(top[:, 0, :], prob, AX, ALU.max))
            link(dve.tensor_tensor(prob, prob, spread(top[:, 0, :]), ALU.subtract))
            dve.wait_ge(sg("route_exp"), 1)
            link(dve.tensor_reduce(top[:, 0, :], prob, AX, ALU.add))
            link(dve.reciprocal(top[:, 1, :], top[:, 0, :]))
            link(dve.tensor_tensor(prob, prob, spread(top[:, 1, :]), ALU.mult))
            pair = {}
            for i in range(4):
                for j in range(i + 1, 4):
                    b = pair[i, j] = beat[:, len(pair), :]
                    ins = dve.tensor_tensor(b, prob[:, :, j], prob[:, :, i], ALU.is_gt)
            link(ins)
            r = [rank[:, :, i] for i in range(4)]
            dve.tensor_tensor(r[0], pair[0, 1], pair[0, 2], ALU.add)
            dve.scalar_tensor_tensor(out=r[1], in0=pair[0, 1], scalar=-1.0, in1=pair[1, 2], op0=ALU.mult, op1=ALU.add)
            dve.tensor_tensor(r[2], pair[0, 2], pair[1, 2], ALU.add)
            link(dve.tensor_tensor(r[3], pair[0, 3], pair[1, 3], ALU.add))
            dve.tensor_tensor(r[0], r[0], pair[0, 3], ALU.add)
            dve.scalar_tensor_tensor(out=r[1], in0=r[1], scalar=1.0, in1=pair[1, 3], op0=ALU.add, op1=ALU.add)
            dve.scalar_tensor_tensor(out=r[2], in0=r[2], scalar=-1.0, in1=pair[2, 3], op0=ALU.mult, op1=ALU.add)
            link(dve.scalar_tensor_tensor(out=r[3], in0=r[3], scalar=-1.0, in1=pair[2, 3], op0=ALU.mult,
                                          op1=ALU.subtract))
            dve.tensor_scalar(r[2], r[2], 2.0, None, ALU.add)
            link(dve.tensor_scalar(r[3], r[3], 3.0, None, ALU.add))
            second = beat[:, 0:4, :].rearrange("p a n -> p (a n)").rearrange("p (n k) -> p n k", k=4)
            dve.scalar_tensor_tensor(out=pick, in0=rank, scalar=0.0, in1=prob, op0=ALU.is_equal, op1=ALU.mult)
            link(dve.scalar_tensor_tensor(out=second, in0=rank, scalar=1.0, in1=prob, op0=ALU.is_equal,
                                          op1=ALU.mult))
            dve.tensor_reduce(top[:, 0, :], pick, AX, ALU.add)
            link(dve.tensor_reduce(top[:, 1, :], second, AX, ALU.add))
            link(dve.tensor_tensor(top[:, 2, :], top[:, 0, :], top[:, 1, :], ALU.add))
            link(dve.tensor_scalar(top[:, 2, :], top[:, 2, :], 0.9, None, ALU.is_le))
            dve.tensor_tensor(top[:, 1, :], top[:, 1, :], top[:, 2, :], ALU.mult)
            link(dve.tensor_tensor(second, second, spread(top[:, 2, :]), ALU.mult))
            dve.tensor_tensor(pick, pick, second, ALU.add)
            link(dve.scalar_tensor_tensor(out=top[:, 0, :], in0=top[:, 0, :], scalar=1e-9, in1=top[:, 1, :],
                                          op0=ALU.add, op1=ALU.add))
            link(dve.reciprocal(top[:, 1, :], top[:, 0, :]))
            link(dve.tensor_tensor(pick, pick, spread(top[:, 1, :]), ALU.mult))
            by_tile = pick.rearrange("p (t i) k -> p t i k", t=TILES)
            for g in range(GROUPS):
                dve.scalar_tensor_tensor(out=weight[:, :, g, :], in0=by_tile[:, :, 1 + g, :],
                                         scalar=1.0 / float(GROUPS) ** 0.5,
                                         in1=by_tile[:, :, 0, g:g + 1].broadcast_to([SEQ, TILES, 4]),
                                         op0=ALU.mult, op1=ALU.mult).then_inc(sg("weights"), 1)

        def ffn_dve(dve):
            norm_dve(dve, "ln2", st_blocks, xn_blocks, bank)
            ln2_low(dve)
            route(dve)

            def scale_x(g, b, j, u, loads):
                if isinstance(g, int) and g == 0:
                    dve.wait_ge(sg("share_first"), 16)
                else:
                    dve.wait_ge(sg(f"share_in{u}"), loads)
                if not isinstance(g, int) or g >= 2:
                    dve.wait_ge(sg("xe_low"), g - 1)
                dve.tensor_tensor(xe[:, b, :], xn_blocks[j], blk(share[:, u], j), ALU.mult).then_inc(sg("xe"), 1)

            def low(n, k):
                dve.wait_ge(sg("hid_high"), n + 1)
                dve.tensor_tensor(hidL[:, k % 4, :], hid[:, k % 2, :], hidH[:, k % 4, :].bitcast(F32), ALU.subtract
                                  ).then_inc(sg("hid_low"), 1)

            scale_x(0, 0, 0, 0, 16)

            def expert(e, u, half):
                first = isinstance(e, int) and e == 0
                last = isinstance(e, int) and e == E0 - 1
                for k in range(ITEMS0):
                    n = e * ITEMS0 + k
                    j = k // C0
                    if k % C0 == 0 and not (last and j == NBLK - 1):
                        if j < NBLK - 1:
                            scale_x(e * NBLK + j + 1, (j + 1) % 2, j + 1, u, half * 16 + 16)
                        else:
                            scale_x(e * NBLK + j + 1, 0, 0, 1 - u, (half + u) * 16 + 16)
                    dve.wait_ge(sg("silu"), n + 1)
                    dve.wait_ge(sg("up_ps"), n + 1)
                    if not (first and k < 2):
                        dve.wait_ge(sg("hid_low"), n - 1)
                    dve.tensor_tensor(hid[:, k % 2, :], silu[:, k % 2, :], bank[6 + k % 2][:, 0:BLK], ALU.mult
                                      ).then_inc(sg("gated"), 1)
                    if not (first and k == 0):
                        low(n - 1, (k - 1) % ITEMS0)
            experts(expert)(dve, E0)
            low(E0 * ITEMS0 - 1, ITEMS0 - 1)
            dve.wait_ge(sg("down"), E0 * ITEMS0)
            for j in range(NBLK):
                dve.tensor_tensor(st_blocks[j], st_blocks[j], bank[j][:, 0:BLK], ALU.add).then_inc(sg("routed"), 1)

        BEHIND = 2 * PAIR
        SIG, CAND, CELL, MEM = 0, 3 * SW, 4 * SW, 5 * SW
        HALF_SEQ = SEQ // 2
        xn_steps = xn[:, :].rearrange("p (t b) -> p t b", b=BATCH)
        hist_k = hist.rearrange("p t n -> p (t n)").rearrange("p (k t b) -> p k t b", k=KH, b=BATCH)

        def pair_banks(l, q):
            return bank[4 * l + 2 * q], bank[4 * l + 2 * q + 1]

        def wave(eng, both):
            for t in range(2 * BEHIND):
                both(t, t % 4)
            with eng.Fori(2, SEQ // 4) as i:
                for u in range(4):
                    both(i * 4 + u, u)
            for t in range(SEQ // 4 * 4, SEQ + BEHIND + 1):
                both(t, t % 4)

        def rec_sp(sp):
            sp.wait_ge(sg("routed"), NBLK)
            sp.dma_start(bias_raw[0:96], recb_in).then_inc(sg("recb_in"), 16)
            sp.dma_start(fc_w, fcw_in).then_inc(sg("fcw_in"), 16)
            sp.dma_start(fb2, fb2_in).then_inc(sg("fg_in"), 16)
            sp.dma_start(fg_w, fg_in).then_inc(sg("fg_in"), 16)
            sp.dma_start(fg_b, fgb_in.broadcast_to([SEQ, E1])).then_inc(sg("fg_in"), 16)
            for u in range(2):
                sp.dma_start(f_raw[:, u, :], f_in[u]).then_inc(sg(f"f_in{u}"), 16)

        def rec_pool(pool):
            pool.wait_ge(sg("xpair"), 2)

            def load(t, q):
                if here(t, 2 * PAIR, SEQ):
                    pool.wait_ge(sg("pre_y0"), t - 3)
                settle(pool)
                pool.tensor_copy(xcur[:, q], xpair[:, bass.ds(t, PAIR)].rearrange("p t g b -> p (t g b)")
                                 ).then_inc(sg("xcur"), PAIR)

            load(0, 0)

            def both(t, u):
                if u % PAIR == 0 and here(t, 0, SEQ - 4):
                    load(t + PAIR, 1 - u // PAIR)
                if here(t, BEHIND + 1, SEQ + BEHIND):
                    v = (u - 1) % 4
                    pool.wait_ge(sg("state1"), t - BEHIND)
                    settle(pool)
                    pool.tensor_copy(hist_k[:, :, bass.ds(t - BEHIND - 1, 1), :].rearrange("p k t b -> p k (t b)"),
                                     hfull[:, 1, v, :].rearrange("p (k b) -> p k b", k=KH)
                                     ).then_inc(sg("hist"), 1)
            wave(pool, both)

        def rec_pe(pe):
            norm_pe(pe, "ln3", st_blocks, bank, lambda e, j: e.wait_ge(sg("routed"), j + 1))
            normed(pe, "ln3")
            pe.wait_ge(sg("bias"), PAIR)
            pe.wait_ge(sg("rec_free"), 7 + 1)
            pe.wait_ge(sg("rec_part"), 7)

            def chunks(l, q, w, operand, out, which):
                x, y = pair_banks(l, q)
                for m in which:
                    at = (x, m * 64) if m < XCH else (y, (m - XCH) * 64)
                    for s in range(2):
                        mm = pe.matmul(at[0][:, at[1] + out.start:at[1] + out.stop], rec_w[:, w, s, m * P:(m + 1) * P],
                                       operand, start=False, stop=False, skip_group_check=True)
                return mm

            IFC, OM = range(XCH), range(XCH, GCH)
            BOTH = slice(0, PAIR * 2 * BATCH)

            def start_bias(l, q):
                x, y = pair_banks(l, q)
                for to, lo, n in ((x, 0, XCH), (y, XCH, GCH - XCH)):
                    pe.matmul(to[:, 0:n * 64].rearrange("p (a g b) -> p a g b", g=2, b=BATCH)[:, :, 0, :],
                              bias_part[0:96, l, :], bias_sel[0:96, lo * 32:(lo + n) * 32].rearrange(
                                  "p (a b) -> p a b", b=BATCH), start=True, stop=False, skip_group_check=True)

            def own(l, t, u, states):
                out = slice(u % PAIR * 32, u % PAIR * 32 + 32)
                for which, name in ((IFC, "pre_x"), (OM, "pre_y")):
                    for k in range(KH):
                        mm = chunks(l, u // PAIR, (WH0, WH1)[l] + k, states[k], out, which)
                    mm.then_inc(sg(f"{name}{l}"), 1)

            start_bias(0, 0)
            pe.wait_ge(sg("xcur"), PAIR)
            chunks(0, 0, WX0, xcur[:, 0], BOTH, IFC).then_inc(sg("pre_x0"), 1)
            chunks(0, 0, WX0, xcur[:, 0], BOTH, OM).then_inc(sg("pre_y0"), 1)

            def both(t, u):
                q, odd = u // PAIR, u % PAIR
                if here(t, 1, SEQ - 1):
                    pe.wait_ge(sg("state0"), t)
                    before = (u - 1) % 4
                    own(0, t, u, [hpair0[:, before // PAIR, k, before % PAIR] for k in range(KH)])
                if here(t, 0, SEQ - 3):
                    if odd == 0:
                        start_bias(0, 1 - q)
                        pe.wait_ge(sg("xcur"), t + 2 * PAIR)
                    chunks(0, 1 - q, WX0, xcur[:, 1 - q], BOTH, range(odd * GCH // 2, (odd + 1) * GCH // 2))
                if here(t, BEHIND + 1, SEQ + BEHIND - 1):
                    pe.wait_ge(sg("state1"), t - BEHIND)
                    own(1, t, u, [hpair1[:, 1 - odd, k] for k in range(KH)])
                if here(t, PAIR, SEQ + 1):
                    if odd == 0:
                        start_bias(1, 1 - q)
                        if isinstance(t, int) and t == SEQ:
                            pe.wait_ge(sg("state0"), t)
                    for which, name in ((IFC, "pre_x1"), (OM, "pre_y1")):
                        mm = chunks(1, 1 - q, WX1 + odd, hpair0[:, 1 - q, odd].rearrange("p s g b -> p (s g b)"),
                                    BOTH, which)
                        if isinstance(t, int) and t == PAIR + 1:
                            mm.then_inc(sg(name), 1)
            wave(pe, both)
            pe.wait_ge(sg("fcw_in"), 16)
            pe.wait_ge(sg("hist"), SEQ)
            for j in range(NBLK):
                for k in range(KH):
                    mm = pe.matmul(bank[4 + j][:, 0:BLK], fc_w[:, k, :],
                                   blk(hist_k[:, k].rearrange("p t b -> p (t b)"), j),
                                   start=(k == 0), stop=(k == KH - 1))
                mm.then_inc(sg("fc"), 1)

        UNSCALE = 1.0 / (H_SCALE * W_SCALE)

        def rec_act(act):
            norm_act(act, "ln3", xn_blocks, bank, 1)
            for q in range(2):
                normed(act, "ln3", (q + 1) * NBLK // 2)
                part = slice(q * HALF_SEQ, (q + 1) * HALF_SEQ)
                act.activation(xpair[:, part, 0, :], xn_steps[:, part], ACT.Copy, scale=H_SCALE
                               ).then_inc(sg("xpair_high"), 1)
            act.activation(warm[:, :], warm[:, :], ACT.Sigmoid)

            def gates_x(l, n):
                act.wait_ge(sg(f"sum_x{l}"), n)
                act.activation(gates[:, l, SIG:2 * SW], pre[:, l, 0:2 * SW], ACT.Sigmoid, scale=UNSCALE)
                act.activation(gates[:, l, CAND:CAND + SW], pre[:, l, 2 * SW:3 * SW], ACT.Tanh, scale=UNSCALE
                               ).then_inc(sg(f"gates{l}"), 1)

            def gates_y(l, n):
                act.wait_ge(sg(f"sum_y{l}"), n)
                act.activation(gates[:, l, 2 * SW:3 * SW], pre[:, l, 3 * SW:4 * SW], ACT.Sigmoid, scale=UNSCALE)
                act.activation(gates[:, l, MEM:MEM + SW], pre[:, l, 4 * SW:5 * SW], ACT.Tanh, scale=UNSCALE)

            def cell_of(l, n):
                act.wait_ge(sg(f"cell{l}"), n)
                act.activation(tanh_c[:, l], gates[:, l, CELL:CELL + SW], ACT.Tanh).then_inc(sg(f"tanh_c{l}"), 1)

            def both(t, u):
                for l, n, there in ((0, t + 1, here(t, 0, SEQ - 1)),
                                    (1, t - BEHIND + 1, here(t, BEHIND, SEQ + BEHIND - 1))):
                    if there:
                        gates_x(l, n)
                        gates_y(l, n)
                        cell_of(l, n)
            wave(act, both)
            for j in range(NBLK):
                act.wait_ge(sg("fc"), j + 1)
                if j >= 2:
                    act.wait_ge(sg("recurred"), j - 1)
                act.activation(fc_sb[:, j % 2], bank[4 + j][:, 0:BLK], ACT.Identity, bias=col(FC_B),
                               scale=1.0 / H_SCALE).then_inc(sg("fc_sb"), 1)

        def rec_dve(dve):
            steps = [0]

            def link(ins):
                steps[0] += 1
                ins.then_inc(sg("bias_step"), 1)
                dve.wait_ge(sg("bias_step"), steps[0])

            def biases():
                dve.wait_ge(sg("recb_in"), 16)
                for s in range(3):
                    link(dve.tensor_copy(bias_cast[0:96, :, s, :], bias_raw[0:96]))
                    if s < 2:
                        link(dve.tensor_tensor(bias_raw[0:96], bias_raw[0:96], bias_cast[0:96, :, s, :], ALU.subtract))
                for s in range(3):
                    dve.tensor_copy(bias_part[32 * s:32 * s + 32], bias_cast[32 * s:32 * s + 32, :, s, :])
                for step in range(PAIR):
                    dve.tensor_scalar(bias_sel[0:96, :].rearrange("p (m s b) -> p m s b", m=GCH, s=PAIR)[:, :, step, :],
                                      const[0:96, C_SEL:C_SEL + GW].rearrange("p (m b) -> p m b", m=GCH),
                                      H_SCALE * W_SCALE, None, ALU.mult).then_inc(sg("bias"), 1)

            norm_dve(dve, "ln3", st_blocks, xn_blocks, bank, biases)
            for q in range(2):
                part = slice(q * HALF_SEQ, (q + 1) * HALF_SEQ)
                dve.wait_ge(sg("xpair_high"), q + 1)
                dve.scalar_tensor_tensor(out=xpair[:, part, 1, :], in0=xn_steps[:, part], scalar=H_SCALE,
                                         in1=xpair[:, part, 0, :], op0=ALU.mult, op1=ALU.subtract
                                         ).then_inc(sg("xpair"), 1)
            for l in range(2):
                dve.memset(gates[:, l, CELL:CELL + SW], 0.0).then_inc(sg("cell_zero"), 1)
            dve.wait_ge(sg("cell_zero"), 2)

            def sum_part(l, n, u, name):
                x, y = pair_banks(l, u // PAIR)
                src, lo, count = (x, 0, XCH) if name == "x" else (y, XCH, GCH - XCH)
                dve.wait_ge(sg(f"pre_{name}{l}"), n)
                dve.tensor_reduce(pre[:, l, lo * BATCH:(lo + count) * BATCH].rearrange("p (m b) -> p m b", b=BATCH),
                                  src[:, 0:count * 64].rearrange("p (m s g b) -> p s m b g", m=count, s=PAIR, g=2
                                                                 )[:, u % PAIR], AX, ALU.add
                                  ).then_inc(sg(f"sum_{name}{l}"), 1)

            def products(l, n):
                dve.wait_ge(sg(f"gates{l}"), n)
                dve.tensor_tensor(prod[:, l], gates[:, l, SIG:2 * SW], gates[:, l, CAND:CAND + 2 * SW], ALU.mult
                                  ).then_inc(sg(f"prod{l}"), 1)

            def new_cell(l, n):
                dve.wait_ge(sg(f"prod{l}"), n)
                dve.tensor_tensor(gates[:, l, CELL:CELL + SW], prod[:, l, 0:SW], prod[:, l, SW:2 * SW], ALU.add
                                  ).then_inc(sg(f"cell{l}"), 1)

            def pair_of(l, u):
                return hpair1[:, u % 2] if l else hpair0[:, u // PAIR, :, u % PAIR]

            def new_state(l, n, u):
                if l == 1 and isinstance(n, int) and n > SEQ - 6:
                    dve.wait_ge(sg("hist"), n - 4)
                dve.wait_ge(sg(f"tanh_c{l}"), n)
                dve.scalar_tensor_tensor(out=out_h[:, l], in0=gates[:, l, 2 * SW:3 * SW], scalar=H_SCALE,
                                         in1=tanh_c[:, l], op0=ALU.mult, op1=ALU.mult).then_inc(sg(f"out{l}"), 1)

            def store_state(l, n, u):
                dve.wait_ge(sg(f"out{l}"), n)
                high = pair_of(l, u)[:, :, 0, :]
                full = hfull[:, l, u, :].rearrange("p (k b) -> p k b", k=KH)
                mem = gates[:, l, MEM:MEM + SW].rearrange("p (k b) -> p k b", k=KH)
                scaled = out_h[:, l].rearrange("p (k b) -> p k b", k=KH)
                dve.scalar_tensor_tensor(out=high, in0=mem, scalar=H_SCALE, in1=scaled, op0=ALU.mult, op1=ALU.add)
                dve.scalar_tensor_tensor(out=full, in0=mem, scalar=H_SCALE, in1=scaled, op0=ALU.mult, op1=ALU.add
                                         ).then_inc(sg(f"full{l}"), 1)

            def store_low(l, n, u):
                dve.wait_ge(sg(f"full{l}"), n)
                dve.tensor_tensor(pair_of(l, u)[:, :, 1, :], hfull[:, l, u, :].rearrange("p (k b) -> p k b", k=KH),
                                  pair_of(l, u)[:, :, 0, :], ALU.subtract).then_inc(sg(f"state{l}"), 1)

            def both(t, u):
                first_layer, second_layer = here(t, 0, SEQ - 1), here(t, BEHIND, SEQ + BEHIND - 1)
                n0, n1 = t + 1, t - BEHIND + 1
                ending = here(t, BEHIND + 1, SEQ + BEHIND)
                v = (u - 1) % 4
                if ending:
                    new_state(1, n1 - 1, v)
                if first_layer:
                    sum_part(0, n0, u, "x")
                if ending:
                    store_state(1, n1 - 1, v)
                if first_layer:
                    sum_part(0, n0, u, "y")
                if ending:
                    store_low(1, n1 - 1, v)
                if first_layer:
                    products(0, n0)
                    new_cell(0, n0)
                    new_state(0, n0, u)
                if second_layer:
                    sum_part(1, n1, u, "x")
                if first_layer:
                    store_state(0, n0, u)
                if second_layer:
                    sum_part(1, n1, u, "y")
                if first_layer:
                    store_low(0, n0, u)
                if second_layer:
                    products(1, n1)
                    new_cell(1, n1)
            wave(dve, both)
            for j in range(NBLK):
                dve.wait_ge(sg("fc_sb"), j + 1)
                dve.tensor_tensor(st_blocks[j], st_blocks[j], fc_sb[:, j % 2], ALU.add).then_inc(sg("recurred"), 1)

        ITEMS1 = NBLK * C1
        ln4_high, ln4_low = split_x("ln4", NBLK)

        def last_sp(sp):
            first, rest = slice(0, BLK), slice(BLK, TOKENS)
            sp.wait_ge(sg("mask_T"), 1)
            sp.dma_start(mask_dram[:, first], mask_T[:, first]).then_inc(sg("mask_out"), 16)
            sp.wait_ge(sg("mask_out"), 16)
            sp.dma_start(mask_b[:, 0, first], mask_dram[0:1, first].broadcast_to([P, BLK])
                         ).then_inc(sg("mask_first"), 16)
            sp.wait_ge(sg("mask_T"), NBLK)
            sp.dma_start(mask_dram[:, rest], mask_T[:, rest]).then_inc(sg("mask_out"), 16)
            sp.wait_ge(sg("mask_out"), 32)
            sp.dma_start(mask_b[:, 0, rest], mask_dram[0:1, rest].broadcast_to([P, TOKENS - BLK])
                         ).then_inc(sg("mask_in0"), 16)
            sp.dma_start(mask_b[:, 1, :], mask_dram[1:2, :].broadcast_to([P, TOKENS])).then_inc(sg("mask_in1"), 16)
            with sp.Fori(1, E1 // 2) as i:
                for u in range(2):
                    e = i * 2 + u
                    sp.wait_ge(sg("f_low"), e - 1)
                    sp.dma_start(f_raw[:, u, :], f_in[bass.ds(e, 1)].rearrange("e p n -> (e p) n")
                                 ).then_inc(sg(f"f_in{u}"), 16)
                    sp.wait_ge(sg("masked"), (e - 1) * ITEMS1)
                    sp.dma_start(mask_b[:, u, :], mask_dram[bass.ds(e, 1), :].broadcast_to([P, TOKENS])
                                 ).then_inc(sg(f"mask_in{u}"), 16)
            for j in range(NBLK):
                sp.wait_ge(sg("final"), j + 1)
                sp.dma_start(blk(out, j), st_blocks[j]).then_inc(sg("out"), 16)
            sp.wait_ge(sg("out"), NBLK * 16)

        def last_pool(pool):
            pool.wait_ge(sg("recurred"), NBLK)

            def f_split(e, u, half):
                pool.wait_ge(sg(f"f_in{u}"), half * 16 + 16)
                if not isinstance(e, int) or e >= 2:
                    pool.wait_ge(sg("f_down"), (e - 1) * ITEMS1)
                settle(pool)
                pool.tensor_tensor(wH[:, u, 0:F0], f_raw[:, u, :], one[:, :].broadcast_to([P, F0]), ALU.mult
                                   ).then_inc(sg("f_high"), 1)
                pool.wait_ge(sg("f_high"), e + 1)
                pool.tensor_tensor(wL[:, u, 0:F0], f_raw[:, u, :], wH[:, u, 0:F0].bitcast(F32), ALU.subtract
                                   ).then_inc(sg("f_low"), 1)
                at = slice(FB1 + e * C1, FB1 + (e + 1) * C1) if isinstance(e, int) else bass.ds(e * C1 + FB1, C1)
                pool.tensor_tensor(f_bias[:, u, :], cols[:, at], one[:, :].broadcast_to([P, C1]), ALU.mult
                                   ).then_inc(sg("f_bias"), 1)

            def expert(e, u, half):
                if isinstance(e, int) and e == 0:
                    f_split(0, 0, 0)
                if not (isinstance(e, int) and e == E1 - 1):
                    f_split(e + 1, 1 - u, half + u)
            experts(expert)(pool, E1)

        def last_pe(pe):
            norm_pe(pe, "ln4", st_blocks, bank, lambda e, j: e.wait_ge(sg("recurred"), j + 1))
            pe.wait_ge(sg("fg_in"), 48)
            for t in range(TILES):
                normed(pe, "ln4", t * NBLK // TILES + 1)
                mm = pe.matmul(bank[7][0:SEQ, t * E1:(t + 1) * E1], xn[:, t * SEQ:(t + 1) * SEQ], fg_w,
                               start=True, stop=True)
            mm.then_inc(sg("f_logits"), 1)
            pe.wait_ge(sg("mask"), 1)
            for t in range(TILES):
                mm = pe.transpose(bank[t // 4][0:E1, t % 4 * SEQ:(t % 4 + 1) * SEQ], chosen[:, t],
                                  ident[0:SEQ, 0:SEQ])
                if t % 4 == 3:
                    mm.then_inc(sg("mask_ps"), 1)
            for j in range(NBLK):
                pe.wait_ge(sg("mask_T"), j + 1)
                pe.matmul(bank[j][:, 0:BLK], fb2, blk(mask_T, j), start=True, stop=False, skip_group_check=True)

            def down(n, k, u):
                j, c = divmod(k, C1)
                w = H1 + c * P
                pe.wait_ge(sg("f_hid_low"), n + 1)
                split3(pe, bank[j][:, 0:BLK], wH[:, u, w:w + P], wL[:, u, w:w + P], hidH[:, k % 4, :],
                       hidL[:, k % 4, :], start=False, stop=False).then_inc(sg("f_down"), 1)

            def expert(e, u, half):
                first = isinstance(e, int) and e == 0
                for k in range(ITEMS1):
                    j, c = divmod(k, C1)
                    n = e * ITEMS1 + k
                    if k == 0:
                        pe.wait_ge(sg("f_low"), e + 1)
                    if first and c == 0:
                        pe.wait_ge(sg("x_low"), NBLK + j + 1)
                    if not (first and k < 4):
                        pe.wait_ge(sg("relu"), n - 3)
                    w = c * P
                    split3(pe, bank[4 + k % 4][:, 0:BLK], wH[:, u, w:w + P], wL[:, u, w:w + P], blk(xnH, j),
                           blk(xnL, j), start=True, stop=True).then_inc(sg("f_up"), 1)
                    if k >= LAG:
                        down(n - LAG, k - LAG, u)
                    elif not first:
                        down(n - LAG, k - LAG + ITEMS1, 1 - u)
            experts(expert)(pe, E1)
            for k in range(ITEMS1 - LAG, ITEMS1):
                down((E1 - 1) * ITEMS1 + k, k, 1)

        def last_act(act):
            norm_act(act, "ln4", xn_blocks, bank, 1)
            ln4_high(act)
            for j in range(NBLK):
                act.wait_ge(sg("mask_ps"), j + 1)
                act.activation(blk(mask_T, j), bank[j][0:E1, 0:BLK], ACT.Copy).then_inc(sg("mask_T"), 1)
            act.activation(warm[:, :], warm[:, :], ACT.Relu)

            def high(n, k):
                act.wait_ge(sg("masked"), n + 1)
                if not isinstance(n, int) or n >= 4:
                    act.wait_ge(sg("f_down"), n - 3)
                act.activation(hidH[:, k % 4, :], fhid[:, k % 2, :], ACT.Copy).then_inc(sg("f_hid_high"), 1)

            def expert(e, u, half):
                first = isinstance(e, int) and e == 0
                for k in range(ITEMS1):
                    n = e * ITEMS1 + k
                    c = k % C1
                    if c == 0 and k == 0:
                        act.wait_ge(sg("f_bias"), e + 1)
                    act.wait_ge(sg("f_up"), n + 1)
                    if not (first and k < 2):
                        act.wait_ge(sg("masked"), n - 1)
                    act.activation(relu[:, k % 2, :], bank[4 + k % 4][:, 0:BLK], ACT.Relu,
                                   bias=f_bias[:, u, c:c + 1]
                                   ).then_inc(sg("relu"), 1)
                    if not (first and k == 0):
                        high(n - 1, (k - 1) % ITEMS1)
            experts(expert)(act, E1)
            high(E1 * ITEMS1 - 1, ITEMS1 - 1)

        def last_dve(dve):
            norm_dve(dve, "ln4", st_blocks, xn_blocks, bank)
            ln4_low(dve)
            steps = [0]

            def link(ins):
                steps[0] += 1
                ins.then_inc(sg("mask_step"), 1)
                dve.wait_ge(sg("mask_step"), steps[0])

            def spread(v):
                return v.rearrange("p (t z) -> p t z", z=1).broadcast_to([SEQ, TILES, E1])

            dve.wait_ge(sg("f_logits"), 1)
            dve.wait_ge(sg("fg_in"), 48)
            link(dve.tensor_tensor(logit, bank[7][0:SEQ, 0:TILES * E1].rearrange("p (t e) -> p t e", t=TILES),
                                   fg_b.rearrange("p (z e) -> p z e", z=1).broadcast_to([SEQ, TILES, E1]), ALU.add))
            link(dve.tensor_reduce(best[:, 0], logit, AX, ALU.max))
            link(dve.tensor_tensor(chosen, logit, spread(best[:, 0]), ALU.is_equal))
            link(dve.tensor_tensor(chosen, chosen,
                                   const[0:SEQ, C_PRI:C_PRI + E1].rearrange("p (z e) -> p z e", z=1).broadcast_to(
                                       [SEQ, TILES, E1]), ALU.mult))
            link(dve.tensor_reduce(best[:, 1], chosen, AX, ALU.max))
            dve.tensor_tensor(chosen, chosen, spread(best[:, 1]), ALU.is_equal).then_inc(sg("mask"), 1)

            def low(n, k):
                dve.wait_ge(sg("f_hid_high"), n + 1)
                dve.tensor_tensor(hidL[:, k % 4, :], fhid[:, k % 2, :], hidH[:, k % 4, :].bitcast(F32), ALU.subtract
                                  ).then_inc(sg("f_hid_low"), 1)

            def expert(e, u, half):
                first = isinstance(e, int) and e == 0
                for k in range(ITEMS1):
                    n = e * ITEMS1 + k
                    if first and k == 0:
                        dve.wait_ge(sg("mask_first"), 16)
                    if k == (C1 if first else 0):
                        dve.wait_ge(sg(f"mask_in{u}"), half * 16 + 16)
                    dve.wait_ge(sg("relu"), n + 1)
                    if not (first and k < 2):
                        dve.wait_ge(sg("f_hid_low"), n - 1)
                    dve.tensor_tensor(fhid[:, k % 2, :], relu[:, k % 2, :], blk(mask_b[:, u], k // C1), ALU.mult
                                      ).then_inc(sg("masked"), 1)
                    if not (first and k == 0):
                        low(n - 1, (k - 1) % ITEMS1)
            experts(expert)(dve, E1)
            low(E1 * ITEMS1 - 1, ITEMS1 - 1)
            dve.wait_ge(sg("f_down"), E1 * ITEMS1)
            for j in range(NBLK):
                dve.tensor_tensor(st_blocks[j], st_blocks[j], bank[j][:, 0:BLK], ALU.add).then_inc(sg("final"), 1)


        block = ctx.enter_context(nc.Block())

        @block.sync
        def _(sp):
            tok_sp(sp)
            ffn_sp(sp)
            rec_sp(sp)
            last_sp(sp)

        @block.gpsimd
        def _(pool):
            tok_pool(pool)
            att_pool(pool)
            ffn_pool(pool)
            rec_pool(pool)
            last_pool(pool)

        @block.tensor
        def _(pe):
            tok_pe(pe)
            att_pe(pe)
            ffn_pe(pe)
            rec_pe(pe)
            last_pe(pe)

        @block.scalar
        def _(act):
            tok_act(act)
            att_act(act)
            ffn_act(act)
            rec_act(act)
            last_act(act)

        @block.vector
        def _(dve):
            tok_dve(dve)
            att_dve(dve)
            ffn_dve(dve)
            rec_dve(dve)
            last_dve(dve)


def kernel(**inputs):
    import numpy as np
    import concourse.bacc as bacc
    from concourse.bass_utils import run_bass_kernel_spmd

    a = {k: np.asarray(v) for k, v in inputs.items()}

    def padded_heads(v):
        v = v.reshape(v.shape[:-1] + (HEADS, HD))
        z = np.zeros(v.shape[:-1] + (PAD,), v.dtype)
        z[..., :HD] = v
        return z.reshape(v.shape[:-2] + (2, P))

    img = np.zeros((BATCH, SIDE + 2, SIDE + 2, COLORS), a["x"].dtype)
    img[:, 1:-1, 1:-1] = a["x"]
    grid = np.stack([img[:, PATCH * p:PATCH * p + WIDE, PATCH * q:PATCH * q + WIDE]
                     for p in range(GRID) for q in range(GRID)])
    patches = grid.reshape(PATCHES, BATCH, RCH, ROWS2).transpose(3, 2, 0, 1).reshape(ROWS2, RCH, EMB)
    taps = np.zeros((SHIFTS, WIDE, WIDE, COLORS, D), a["L0_tok_conv_w"].dtype)
    for s, (di, dj) in enumerate(((0, 0), (0, -1), (0, 1), (-1, 0), (1, 0))):
        taps[s, 1 + di:1 + di + PATCH, 1 + dj:1 + dj + PATCH] = a["L0_tok_conv_w"][:, :, 3 * s:3 * s + 3]
    taps = taps.reshape(SHIFTS, RCH, ROWS2, D).transpose(2, 0, 1, 3)

    wq, wk, wv = (padded_heads(a["L0_attn_in_proj_w"][i * D:(i + 1) * D].T) for i in range(3))
    qkvw = np.concatenate([wq, wk, wv], axis=1)
    bq, bk, bv = (padded_heads(a["L0_attn_in_proj_b"][i * D:(i + 1) * D]) for i in range(3))
    outw = padded_heads(a["L0_attn_out_proj_w"]).transpose(2, 1, 0)

    cols = np.zeros((P, NCOLS), np.float32)
    for i, v in ((CONV_B, a["L0_tok_conv_b"]), (GAMMA, a["L0_tok_gamma"]), (BETA, a["L0_tok_beta"]),
                 (DENSE_B, a["L0_tok_dense_b"]), (OUT_B, a["L0_attn_out_proj_b"]), (FC_B, a["L1_attn_bfc"])):
        cols[:, i] = v
    cols[:, QKV_B:QKV_B + 6] = np.concatenate([bq, bk, bv]).T
    cols[:, FB1:] = a["L1_ffn_b1"].reshape(E1 * C1, P).T

    const = np.zeros((P, NCONST), np.float32)
    const[:, C_ID:C_ID + P] = np.eye(P)
    i = np.arange(SEQ)
    const[:SEQ, C_DIST:C_DIST + SEQ] = -(i[None, :] - i[:, None]).astype(np.float32) ** 2
    for s in range(3):
        for m in range(GCH):
            const[32 * s + m, C_SEL + m * BATCH:C_SEL + (m + 1) * BATCH] = 1.0
    const[:, C_PRI:C_PRI + E1] = np.arange(E1, 0, -1)

    w2 = a["L0_ffn_W2"].reshape(E0, C0, P, D).transpose(0, 2, 1, 3).reshape(E0, P, H0)
    w0 = np.concatenate([a["L0_ffn_W1"], a["L0_ffn_W3"], w2], axis=2)
    route = np.concatenate([a["L0_ffn_Wr"], a["L0_ffn_Wgate"].transpose(1, 0, 2).reshape(D, E0)], axis=1)
    routeb = np.concatenate([a["L0_ffn_br"], a["L0_ffn_bgate"].reshape(E0)])[None]
    rec = np.concatenate([a["L1_attn_Wx0"], a["L1_attn_Wh0"], a["L1_attn_Wx1"], a["L1_attn_Wh1"]])
    recb = np.zeros((96, 2, P), np.float32)
    for s in range(3):
        for l in range(2):
            recb[32 * s:32 * s + GCH, l] = a[f"L1_attn_b{l}"].reshape(GCH, P)
    f2 = a["L1_ffn_W2"].reshape(E1, C1, P, D).transpose(0, 2, 1, 3).reshape(E1, P, H1)
    f = np.concatenate([a["L1_ffn_W1"], f2], axis=2)

    arrays = {
        "taps": taps, "patches": patches, "txt": a["txt"].transpose(2, 1, 0).reshape(D, WORDS * BATCH),
        "cols": cols, "const": const, "dense": a["L0_tok_dense_w"], "qkvw": qkvw, "outw": outw,
        "heads": a["L0_attn_t"][None], "w0": w0, "route": route, "routeb": routeb,
        "rec": rec.reshape(7, P, GP), "recb": recb,
        "fcw": a["L1_attn_Wfc"].reshape(KH, P, D).transpose(1, 0, 2), "f": f, "fb2": a["L1_ffn_b2"],
        "fg": a["L1_ffn_Wg"], "fgb": a["L1_ffn_bg"][None],
    }
    arrays = {f"in_{k}": np.ascontiguousarray(v) for k, v in arrays.items()}
    nc = bacc.Bacc("TRN2", target_bir_lowering=False, num_devices=1)
    args = [nc.dram_tensor(k, v.shape, mybir.dt.from_np(v.dtype), kind="ExternalInput").ap()
            for k, v in arrays.items()]
    args.append(nc.dram_tensor("out_stream", (D, TOKENS), F32, kind="ExternalOutput").ap())
    build(nc, *args)
    r = run_bass_kernel_spmd(nc, [arrays], core_ids=[0])
    got = r.results[0]["out_stream"].reshape(D, SEQ, BATCH)
    return np.ascontiguousarray(got.transpose(2, 1, 0))
```
